# Optimizing a Trainium2 kernel written in Bass

```python
import numpy as np
import jax
import jax.numpy as jnp

def _softmax(x, axis=-1):
    return jax.nn.softmax(x, axis=axis)

def _gelu(x):
    return jax.nn.gelu(x, approximate=True)

def _silu(x):
    return jax.nn.silu(x)

def _sigmoid(x):
    return jax.nn.sigmoid(x)

def _layernorm(x, axis=-1, eps=1e-05):
    m = jnp.mean(x, axis=axis, keepdims=True)
    v = jnp.var(x, axis=axis, keepdims=True)
    return (x - m) / jnp.sqrt(v + eps)

def _scatter_add(tgt, idx, src, axis=0):
    return tgt.at[idx].add(src)

def _segment_sum(src, seg, n):
    return jax.ops.segment_sum(src, seg, n)
kernel_name = 'mk_recurrent_d1_jaxref_r8_cde8a3'

def setup_inputs(seed: int=0):
    np.random.seed(seed)
    _w = jnp.asarray

    def _L0_attn_setup():
        import jax, jax.numpy as jnp
        import numpy as np
        H = 16
        HD = 64
        W = 128
        G = 32
        EPS = 1e-06
        NEG = -1e+30
        key = jax.random.key(seed)
        ks = jax.random.split(key, 7)
        B, S, D = (1, 1024, 128)
        inner = H * HD
        s = 0.02
        return {'x': jax.random.normal(ks[0], (B, S, D), jnp.float32), 'norm_w': jnp.ones((D,), jnp.float32), 'w_q': jax.random.normal(ks[1], (D, inner), jnp.float32) * s, 'w_k': jax.random.normal(ks[2], (D, inner), jnp.float32) * s, 'w_v': jax.random.normal(ks[3], (D, inner), jnp.float32) * s, 'w_out': jax.random.normal(ks[4], (inner, D), jnp.float32) * s, 'scorer_w': jax.random.normal(ks[5], (D, 1), jnp.float32) * s, 'scorer_b': jnp.zeros((1,), jnp.float32)}
    _L0_attn_in = _L0_attn_setup()

    def _L0_ffn_setup():
        import jax, jax.numpy as jnp
        import numpy as np
        B, S, H = (4, 256, 128)
        E, K = (8, 2)
        I_R, I_S = (4 * H, 8 * H)
        CAP_FACTOR = 1.25
        SCALE = 1.0
        key = jax.random.key(seed)
        ks = jax.random.split(key, 9)
        std = 0.02
        return {'x': jax.random.normal(ks[0], (B, S, H), jnp.float32), 'router_w': std * jax.random.normal(ks[1], (E, H), jnp.float32), 'rg': std * jax.random.normal(ks[2], (E, H, I_R), jnp.float32), 'ru': std * jax.random.normal(ks[3], (E, H, I_R), jnp.float32), 'rd': std * jax.random.normal(ks[4], (E, I_R, H), jnp.float32), 'sg': std * jax.random.normal(ks[5], (H, I_S), jnp.float32), 'su': std * jax.random.normal(ks[6], (H, I_S), jnp.float32), 'sd': std * jax.random.normal(ks[7], (I_S, H), jnp.float32)}
    _L0_ffn_in = _L0_ffn_setup()
    _d = {'L0_attn_x': _L0_attn_in['x'], 'L0_attn_norm_w': _L0_attn_in['norm_w'], 'L0_attn_w_q': _L0_attn_in['w_q'], 'L0_attn_w_k': _L0_attn_in['w_k'], 'L0_attn_w_v': _L0_attn_in['w_v'], 'L0_attn_w_out': _L0_attn_in['w_out'], 'L0_attn_scorer_w': _L0_attn_in['scorer_w'], 'L0_attn_scorer_b': _L0_attn_in['scorer_b'], 'L0_ffn_router_w': _L0_ffn_in['router_w'], 'L0_ffn_rg': _L0_ffn_in['rg'], 'L0_ffn_ru': _L0_ffn_in['ru'], 'L0_ffn_rd': _L0_ffn_in['rd'], 'L0_ffn_sg': _L0_ffn_in['sg'], 'L0_ffn_su': _L0_ffn_in['su'], 'L0_ffn_sd': _L0_ffn_in['sd']}
    _x0 = _d['L0_attn_x']
    _d['L0_attn_x'] = jax.random.normal(jax.random.fold_in(jax.random.key(seed), 1), (8, 512, 128), dtype=_x0.dtype)
    del _x0
    return _d

def reference(L0_attn_x, L0_attn_norm_w, L0_attn_w_q, L0_attn_w_k, L0_attn_w_v, L0_attn_w_out, L0_attn_scorer_w, L0_attn_scorer_b, L0_ffn_router_w, L0_ffn_rg, L0_ffn_ru, L0_ffn_rd, L0_ffn_sg, L0_ffn_su, L0_ffn_sd):

    def _L0_attn_ref(x, norm_w, w_q, w_k, w_v, w_out, scorer_w, scorer_b):
        import jax, jax.numpy as jnp
        import numpy as np
        H = 16
        HD = 64
        W = 128
        G = 32
        EPS = 1e-06
        NEG = -1e+30
        B, S, D = x.shape
        h = x * jax.lax.rsqrt(jnp.mean(x * x, axis=-1, keepdims=True) + EPS) * norm_w

        def proj(w):
            return jnp.einsum('bsd,de->bse', h, w).reshape(B, S, H, HD).transpose(0, 2, 1, 3)
        q, k, v = (proj(w_q), proj(w_k), proj(w_v))
        scale = HD ** (-0.5)
        nW = S // W
        qw = q.reshape(B, H, nW, W, HD)
        kw = k.reshape(B, H, nW, W, HD)
        vw = v.reshape(B, H, nW, W, HD)
        ll = jnp.einsum('bhnqd,bhnkd->bhnqk', qw, kw) * scale
        cm = jnp.tril(jnp.ones((W, W), bool))
        ll = jnp.where(cm, ll, NEG).reshape(B, H, S, W)
        scores = (jnp.einsum('bsd,do->bso', h, scorer_w) + scorer_b)[..., 0]
        _, idx = jax.lax.top_k(scores, G)
        kg = jnp.take_along_axis(k, idx[:, None, :, None], axis=2)
        vg = jnp.take_along_axis(v, idx[:, None, :, None], axis=2)
        lg = jnp.einsum('bhsd,bhgd->bhsg', q, kg) * scale
        pos = jnp.arange(S)
        gmask = idx[:, None, None, :] <= pos[None, None, :, None]
        lg = jnp.where(gmask, lg, NEG)
        attn = jax.nn.softmax(jnp.concatenate([ll, lg], axis=-1), axis=-1)
        a_loc = attn[..., :W].reshape(B, H, nW, W, W)
        o = jnp.einsum('bhnqk,bhnkd->bhnqd', a_loc, vw).reshape(B, H, S, HD)
        o = o + jnp.einsum('bhsg,bhgd->bhsd', attn[..., W:], vg)
        o = o.transpose(0, 2, 1, 3).reshape(B, S, H * HD)
        return x + jnp.einsum('bse,ed->bsd', o, w_out)

    def _L0_ffn_ref(x, router_w, rg, ru, rd, sg, su, sd):
        import jax, jax.numpy as jnp
        import numpy as np
        B, S, H = (4, 256, 128)
        E, K = (8, 2)
        I_R, I_S = (4 * H, 8 * H)
        CAP_FACTOR = 1.25
        SCALE = 1.0
        b, s, h = x.shape
        T = b * s
        capacity = max(int(CAP_FACTOR * T / E), 1)
        xf = x.reshape(T, h)
        eps = jnp.finfo(x.dtype).eps
        xn = xf * jax.lax.rsqrt(jnp.mean(xf * xf, axis=-1, keepdims=True) + eps)
        logits = xn @ router_w.T
        probs = jax.nn.softmax(logits, axis=-1)
        topk_p, topk_i = jax.lax.top_k(probs, K)
        rw = topk_p / jnp.sum(topk_p, axis=-1, keepdims=True)
        one_hot = jax.nn.one_hot(topk_i, E, dtype=x.dtype)
        mask = one_hot.sum(1)
        wdense = (one_hot * rw[..., None]).sum(1)
        sel = mask.T.astype(bool)
        order = jnp.argsort(~sel, axis=1, stable=True)
        dispatch = order[:, :capacity]
        count = sel.sum(axis=1)
        valid = (jnp.arange(capacity)[None, :] < count[:, None]).astype(x.dtype)
        xg = xf[dispatch]
        gate = jax.nn.silu(jnp.einsum('ech,ehi->eci', xg, rg))
        up = jnp.einsum('ech,ehi->eci', xg, ru)
        eout = jnp.einsum('eci,eih->ech', gate * up, rd)
        w = jnp.take_along_axis(wdense.T, dispatch, axis=1)
        contrib = eout * (w * valid)[..., None]
        routed = jnp.zeros_like(xf).at[dispatch.reshape(-1)].add(contrib.reshape(-1, h))
        shared = jax.nn.silu(x @ sg) * (x @ su) @ sd
        return shared + SCALE * routed.reshape(b, s, h)
    x = L0_attn_x
    xn = _layernorm(x, axis=-1)
    s = _L0_attn_ref(xn, L0_attn_norm_w, L0_attn_w_q, L0_attn_w_k, L0_attn_w_v, L0_attn_w_out, L0_attn_scorer_w, L0_attn_scorer_b)
    g = _silu(_L0_ffn_ref(xn, L0_ffn_router_w, L0_ffn_rg, L0_ffn_ru, L0_ffn_rd, L0_ffn_sg, L0_ffn_su, L0_ffn_sd))
    x = x + s * g
    return x

_drawn_inputs = setup_inputs


def setup_inputs(seed=0):
    import zlib

    import numpy as np

    out = dict(_drawn_inputs(seed))
    spreads = {'L0_attn_norm_w': (1.0, 0.6)}
    factors = {'L0_attn_w_q': 8.0,
     'L0_attn_w_k': 8.0,
     'L0_attn_w_v': 8.0,
     'L0_attn_w_out': 8.0,
     'L0_attn_scorer_w': 8.0,
     'L0_ffn_router_w': 8.0,
     'L0_ffn_rg': 8.0,
     'L0_ffn_ru': 8.0,
     'L0_ffn_rd': 8.0,
     'L0_ffn_sg': 6.82,
     'L0_ffn_su': 6.775,
     'L0_ffn_sd': 6.776}
    for name, (base, spread) in spreads.items():
        noise = np.random.default_rng([zlib.crc32(name.encode()), seed]).standard_normal(out[name].shape)
        drawn = base * np.exp(spread * noise) if base else spread * noise
        out[name] = jnp.asarray(drawn.astype(out[name].dtype))
    for name, factor in factors.items():
        out[name] = (out[name] * factor).astype(out[name].dtype)
    return out
```

```python
import concourse.bass as bass
from concourse import mybir
from contextlib import ExitStack



def recurrent_layer(nc, x, norm_w, w_q, w_k, w_v, w_out, scorer_w, scorer_b, router_wT,
                    rg, ru, rd, sg, su, sd, out):
    F32, BF16, U32 = mybir.dt.float32, mybir.dt.bfloat16, mybir.dt.uint32
    ALU, ACT, AX = mybir.AluOpType, mybir.ActivationFunctionType, mybir.AxisListType

    B, S, D = x.shape
    P = 128
    W = S // P
    T = B * S
    H, HD = w_q.shape[1] // 64, 64
    HG = 4
    G = H // HG
    NG = 32
    KEYS = P + NG
    E, _, FR = rg.shape
    FS = sg.shape[1]
    RB, SB = FR // P, FS // P
    CAP = max(int(1.25 * T / E), 1)
    CT = CAP // P
    HALF = CAP // 2
    SLOTS = E * CAP
    HOME = (0, 2, 1, 3)
    NEG = -1e30
    BIG = 3e38
    EPS_LN, EPS_ATT, EPS_FFN = 1e-5, 1e-6, 1.1920929e-07
    DMA = 16

    ctx = ExitStack()

    def sb(name, shape, dt=F32):
        return ctx.enter_context(nc.sbuf_tensor(name, shape, dt))

    def sem(name):
        return ctx.enter_context(nc.semaphore(name))

    def wait(eng, s, value):
        if not isinstance(value, int) or value > 0:
            eng.wait_ge(s, value)

    def settle(eng):
        eng.nop(nofuse=True)

    class Chain:

        def __init__(self, eng, s, per_round):
            self.eng, self.s, self.per = eng, s, per_round

        def round(self, r):
            self.base, self.n = r * self.per, 0

        def link(self, instruction):
            self.n += 1
            instruction.then_inc(self.s, 1)
            self.eng.wait_ge(self.s, self.base + self.n)

        def done(self):
            assert self.n == self.per, (self.n, self.per)

    x_rows = x.rearrange("b (w p) d -> b p w d", p=P)
    out_rows = out.rearrange("b (w p) d -> b p w d", p=P)

    with ctx:
        xg_dram = nc.dram_tensor("xg_dram", [SLOTS + 2 * W * P, D], F32, kind="Internal").ap()
        eo_dram = nc.dram_tensor("eo_dram", [SLOTS + 2 * W * P, D], F32, kind="Internal").ap()
        vg_dram = nc.dram_tensor("vg_dram", [B * NG, H * HD], F32, kind="Internal").ap()

        ident = sb("ident", [P, P])
        before = sb("before", [P, P], BF16)
        ones_bf = sb("ones_bf", [P, P], BF16)
        iota_e = sb("iota_e", [P, E])
        iota_g = sb("iota_g", [P, NG])
        trash = sb("trash", [P, 2, W])
        own = sb("own", [P, HG, 32])
        pow_m = sb("pow_m", [P, 2 * W])
        zeros = sb("zeros", [P, D])
        onesr = sb("onesr", [B, S])
        bias_s = sb("bias_s", [P, 1])
        normw = sb("normw", [P, 1])
        rs9 = sb("rs9", [D, E + 1])

        xn_all = sb("xn_all", [P, B, W, D])
        hT_all = sb("hT_all", [D, B, S])
        ffn_all = sb("ffn_all", [P, B, W, D])
        wq = sb("wq", [D, H * HD])
        wk = sb("wk", [D, H * HD])
        wv = sb("wv", [D, H * HD])
        wo = sb("wo", [P, G, 2, D])
        dest_all = sb("dest_all", [P, B, 2, W], U32)
        valid_all = sb("valid_all", [P, B, 2, W])
        dlog_all = sb("dlog_all", [P, B, W])
        score_all = sb("score_all", [P, B, W])
        r1_all = sb("r1_all", [P, B, W])
        maskb = sb("maskb", [P, W, KEYS])

        bank = [ctx.enter_context(nc.psum_tensor(f"bank{i}", [P, 512], F32)) for i in range(8)]

        wge = [sb(f"wge{i}", [D, FR]) for i in range(2)]
        wue = [sb(f"wue{i}", [D, FR]) for i in range(2)]
        wde = [sb(f"wde{i}", [P, RB, D]) for i in range(2)]
        we_loaded = sem("we_loaded")
        wattn_loaded = sem("wattn_loaded")
        wout_loaded = sem("wout_loaded")
        eo_stored = [sem(f"eo_stored{i}") for i in range(2)]
        scattered = sem("scattered")
        consts = sem("consts")

        def load_expert(sp, e, i):
            sp.dma_start(wge[i][:], rg[e]).then_inc(we_loaded, DMA)
            sp.dma_start(wue[i][:], ru[e]).then_inc(we_loaded, DMA)
            sp.dma_start(wde[i][:], rd[e].rearrange("(j p) d -> p j d", p=P)).then_inc(we_loaded, DMA)

        def stage1(s1):
            def sb(name, shape, dt=F32):
                return s1.enter_context(nc.sbuf_tensor(name, shape, dt))

            def sem(name):
                return s1.enter_context(nc.semaphore(name))

            x_st = sb("x_st", [P, W, D])
            xn_st = sb("xn_st", [P, W, D])
            h_st = sb("h_st", [P, W, D])
            xn_sc = sb("xn_sc", [P, W, D])
            xnT = sb("xnT", [D, S])
            wsg = sb("wsg", [D, FS])
            wsu = sb("wsu", [D, FS])
            wsd = sb("wsd", [P, SB, D])
            sil = sb("sil", [P, 2, S])
            acts = sb("acts", [P, 2, S])
            st6 = sb("st6", [P, W, 6])
            mv = sb("mv", [P, W, 2])
            var = sb("var", [P, 2, W])
            yv = sb("yv", [P, 2, W])
            t1 = sb("t1", [P, 2, W])
            rstd = sb("rstd", [P, W])
            r12 = sb("r12", [P, 2, W])
            lgs = sb("lgs", [P, W, E])
            sct = sb("sct", [P, W])
            mx8 = sb("mx8", [P, W, 8])
            ix8 = sb("ix8", [P, W, 8], U32)
            ixf = sb("ixf", [P, 2, W])
            oh = sb("oh", [P, 2, W, E])
            msk = sb("msk", [P, W, E], BF16)
            carry = sb("carry", [P, E])
            tsum = sb("tsum", [P, E])
            pos = sb("pos", [P, W, E])
            ohp = sb("ohp", [P, 2, W, E])
            posk = sb("posk", [P, 2, W])
            valid = sb("valid", [P, 2, W])
            dest = sb("dest", [P, 2, W])
            dest_st = sb("dest_st", [P, 2, W], U32)

            gate, up, down, tx, lg = bank[0:2], bank[2:4], bank[4], bank[5:7], bank[7]
            lgv = lg[:, 0:W * 16].rearrange("p (w e) -> p w e", e=16)
            pref = lg[:, 128:128 + W * E].rearrange("p (w e) -> p w e", e=E)
            tot = lg[:, 256:256 + W * E].rearrange("p (w e) -> p w e", e=E)

            x_loaded = sem("x_loaded")
            wffn_loaded, small_loaded = sem("wffn_loaded"), sem("small_loaded")
            var_ready, pow_ready = sem("var_ready"), sem("pow_ready")
            xn_ready, h_ready, xn_saved = sem("xn_ready"), sem("h_ready"), sem("xn_saved")
            tx_done, th_done, lg_done, pref_done = sem("tx_done"), sem("th_done"), sem("lg_done"), sem("pref_done")
            xnT_ready, hT_saved, lg_read = sem("xnT_ready"), sem("hT_saved"), sem("lg_read")
            mask_ready, pref_read, dest_ready = sem("mask_ready"), sem("pref_read"), sem("dest_ready")
            dest_saved, xsc_ready, xg_zeroed = sem("dest_saved"), sem("xsc_ready"), sem("xg_zeroed")
            gu_done, silu_done, act_ready = sem("gu_done"), sem("silu_done"), sem("act_ready")
            dn_done, ffn_saved = sem("dn_done"), sem("ffn_saved")
            lnc, rtc, pc = sem("lnc"), sem("rtc"), sem("pc")

            block = s1.enter_context(nc.Block())

            @block.sync
            def _(sp):
                sp.dma_start(x_st[:], x_rows[0]).then_inc(x_loaded, DMA)
                sp.dma_start(rs9[:, 0:E], router_wT).then_inc(small_loaded, DMA)
                sp.dma_start(rs9[:, E:E + 1], scorer_w).then_inc(small_loaded, DMA)
                sp.dma_start(normw[:], norm_w.rearrange("(d a) -> d a", a=1)).then_inc(small_loaded, DMA)
                sp.dma_start(bias_s[:], scorer_b.rearrange("(a b) -> a b", a=1).to_broadcast([P, 1]))\
                    .then_inc(small_loaded, DMA)
                sp.dma_start(wsg[:], sg).then_inc(wffn_loaded, DMA)
                sp.dma_start(wsu[:], su).then_inc(wffn_loaded, DMA)
                sp.dma_start(wsd[:], sd.rearrange("(j p) d -> p j d", p=P)).then_inc(wffn_loaded, DMA)
                sp.wait_ge(consts, 1)
                sp.dma_start(xg_dram[0:SLOTS, :].rearrange("(t p) d -> p t d", p=P),
                             zeros[:].unsqueeze(1).to_broadcast([P, SLOTS // P, D])).then_inc(xg_zeroed, DMA)
                with sp.Fori(1, B) as b:
                    sp.wait_ge(xn_ready, b * 1)
                    sp.dma_start(x_st[:], x_rows[b]).then_inc(x_loaded, DMA)
                load_expert(sp, 0, 0)
                load_expert(sp, 1, 1)
                for w_sb, w_dram in ((wq, w_q), (wk, w_k), (wv, w_v)):
                    sp.dma_start(w_sb[:], w_dram).then_inc(wattn_loaded, DMA)
                for c in range(HG):
                    for f in range(2):
                        src = w_out.rearrange("(g j f q) d -> j f q g d", j=HG, f=2, q=32)[HOME[c], f]
                        sp.dma_start(wo[32 * c:32 * c + 32, :, f, :], src).then_inc(wout_loaded, DMA)

            @block.gpsimd
            def _(pool):
                n = [0]

                def link(i):
                    n[0] += 1
                    i.then_inc(pc, 1)
                    pool.wait_ge(pc, n[0])

                link(pool.memset(zeros[:], 0.0))
                pool.memset(pow_m[:], -0.5).then_inc(consts, 1)
                for k in range(2):
                    pool.dma_start(eo_dram[SLOTS + k * W * P:SLOTS + (k + 1) * W * P, :]
                                   .rearrange("(t p) d -> p t d", p=P),
                                   zeros[:].unsqueeze(1).to_broadcast([P, W, D])).then_inc(eo_stored[k], DMA)
                link(pool.affine_select(out=ident[:], in_=zeros[:], compare_op=ALU.not_equal, fill=1.0,
                                        base=0, pattern=[[-1, P]], channel_multiplier=1))
                link(pool.memset(ones_bf[:], 1.0))
                link(pool.affine_select(out=before[:], in_=ones_bf[:], compare_op=ALU.is_gt, fill=0.0,
                                        base=0, pattern=[[1, P]], channel_multiplier=-1))
                link(pool.iota(iota_e[:], pattern=[[1, E]], base=0, channel_multiplier=0,
                               allow_small_or_imprecise_dtypes=True))
                link(pool.iota(iota_g[:], pattern=[[1, NG]], base=1, channel_multiplier=0,
                               allow_small_or_imprecise_dtypes=True))
                link(pool.iota(trash[:], pattern=[[W * P, 2], [P, W]], base=SLOTS, channel_multiplier=1,
                               allow_small_or_imprecise_dtypes=True))
                link(pool.memset(own[:], 1.0))
                link(pool.affine_select(out=own[:], in_=own[:], compare_op=ALU.is_ge, fill=0.0,
                                        base=0, pattern=[[-32, HG], [0, 32]], channel_multiplier=1))
                link(pool.affine_select(out=own[:], in_=own[:], compare_op=ALU.is_ge, fill=0.0,
                                        base=31, pattern=[[32, HG], [0, 32]], channel_multiplier=-1))
                link(pool.memset(onesr[:], 1.0))
                link(pool.memset(maskb[:], 0.0))
                pool.affine_select(out=maskb[:, :, 0:P], in_=maskb[:, :, 0:P], compare_op=ALU.is_ge,
                                   fill=NEG, base=0, pattern=[[0, W], [-1, P]], channel_multiplier=1)\
                    .then_inc(consts, 1)

                def norm_help(b):
                    pool.wait_ge(var_ready, b * 2 + 1)
                    pool.tensor_tensor(yv[:, 0, :], var[:, 0, :], pow_m[:, 0:W], ALU.pow).then_inc(pow_ready, 1)
                    pool.wait_ge(var_ready, b * 2 + 2)
                    pool.tensor_tensor(yv[:].rearrange("p a w -> p (a w)"), var[:].rearrange("p a w -> p (a w)"),
                                       pow_m[:], ALU.pow).then_inc(pow_ready, 1)
                    pool.wait_ge(xn_ready, b * 1 + 1)
                    wait(pool, th_done, b * 1)
                    pool.tensor_tensor(h_st[:], xn_st[:], r12[:, 0, :].unsqueeze(2).to_broadcast([P, W, D]),
                                       ALU.mult).then_inc(h_ready, 1)
                    pool.tensor_copy(r1_all[:, b, :], r12[:, 0, :])
                    pool.tensor_copy(xn_all[:, b, :, :], xn_st[:]).then_inc(xn_saved, 1)

                def scatter(b):
                    wait(pool, scattered, b * (2 * W * DMA))
                    pool.wait_ge(xn_saved, b * 1 + 1)
                    pool.tensor_copy(xn_sc[:], xn_all[:, b, :, :]).then_inc(xsc_ready, 1)
                    pool.wait_ge(dest_ready, b * 1 + 1)
                    pool.tensor_copy(dest_all[:, b, :, :], dest_st[:]).then_inc(dest_saved, 1)
                    pool.wait_ge(xsc_ready, b * 1 + 1)
                    settle(pool)
                    for w in range(W):
                        for k in range(2):
                            pool.indirect_dma_start(
                                out=xg_dram, out_offset=bass.IndirectOffsetOnAxis(ap=dest_st[:, k, w:w + 1], axis=0),
                                in_=xn_sc[:, w, :], in_offset=None).then_inc(scattered, DMA)

                def body(b, last=False):
                    if not last:
                        norm_help(b + 1)
                    scatter(b)

                norm_help(0)
                pool.wait_ge(xg_zeroed, DMA)
                body(0)
                with pool.Fori(1, B - 1) as b:
                    body(b)
                body(B - 1, last=True)

            @block.vector
            def _(dve):
                ln = Chain(dve, lnc, 13)
                rt = Chain(dve, rtc, 11)

                def root(v, y, t):
                    ln.link(dve.tensor_tensor(t, y, y, ALU.mult))
                    ln.link(dve.tensor_tensor(t, t, v, ALU.mult))
                    ln.link(dve.tensor_scalar(t, t, -0.5, 1.5, ALU.mult, ALU.add))

                def ln_a(b):
                    ln.round(b)
                    dve.wait_ge(x_loaded, b * DMA + DMA)
                    for w in range(W):
                        i = dve.bn_stats(st6[:, w, :], x_st[:, w, :])
                    ln.link(i)
                    settle(dve)
                    for w in range(W):
                        i = dve.bn_aggr(mv[:, w, :], st6[:, w, :])
                    ln.link(i)
                    dve.tensor_scalar(var[:, 0, :], mv[:, :, 1], EPS_LN, None, ALU.add).then_inc(var_ready, 1)

                def ln_b(b):
                    dve.wait_ge(pow_ready, b * 2 + 1)
                    dve.wait_ge(var_ready, b * 2 + 1)
                    root(var[:, 0, :], yv[:, 0, :], t1[:, 0, :])
                    ln.link(dve.tensor_tensor(rstd[:], yv[:, 0, :], t1[:, 0, :], ALU.mult))
                    ln.link(dve.tensor_tensor(t1[:, 1, :], rstd[:], rstd[:], ALU.mult))
                    ln.link(dve.tensor_tensor(t1[:, 1, :], t1[:, 1, :], mv[:, :, 1], ALU.mult))
                    ln.link(dve.tensor_scalar(var[:, 0, :], t1[:, 1, :], EPS_ATT, None, ALU.add))
                    dve.tensor_scalar(var[:, 1, :], t1[:, 1, :], EPS_FFN, None, ALU.add).then_inc(var_ready, 1)

                def ln_c(b):
                    dve.wait_ge(pow_ready, b * 2 + 2)
                    dve.wait_ge(var_ready, b * 2 + 2)
                    root(var[:], yv[:], t1[:])
                    wait(dve, xn_saved, b * 1)
                    ln.link(dve.tensor_tensor(r12[:], yv[:], t1[:], ALU.mult))
                    ln.done()

                def ln_d(b):
                    wait(dve, tx_done, b * 1)
                    for w in range(W):
                        i = dve.tensor_scalar(xn_st[:, w, :], x_st[:, w, :], mv[:, w, 0:1], rstd[:, w:w + 1],
                                              ALU.subtract, ALU.mult)
                    i.then_inc(xn_ready, 1)

                def route_a(b):
                    rt.round(b)
                    dve.wait_ge(lg_done, b * 1 + 1)
                    dve.tensor_tensor(lgs[:], lgv[:, :, 0:E], r12[:, 1, :].unsqueeze(2).to_broadcast([P, W, E]),
                                      ALU.mult)
                    rt.link(dve.tensor_tensor(sct[:], lgv[:, :, E], r12[:, 0, :], ALU.mult))
                    dve.tensor_scalar(score_all[:, b, :], sct[:], bias_s[:, 0:1], None, ALU.add)
                    for w in range(W):
                        i = dve.max(mx8[:, w, :], lgs[:, w, :])
                    rt.link(i)
                    settle(dve)
                    for w in range(W):
                        i = dve.max_index(ix8[:, w, :], mx8[:, w, :], lgs[:, w, :])
                    rt.link(i)
                    dve.tensor_tensor(dlog_all[:, b, :], mx8[:, :, 1], mx8[:, :, 0], ALU.subtract)
                    rt.link(dve.tensor_copy(ixf[:], ix8[:, :, 0:2].rearrange("p w k -> p k w")))
                    for k in range(2):
                        i = dve.tensor_tensor(oh[:, k, :, :], iota_e[:].unsqueeze(1).to_broadcast([P, W, E]),
                                              ixf[:, k, :].unsqueeze(2).to_broadcast([P, W, E]), ALU.is_equal)
                    rt.link(i)
                    dve.tensor_tensor(msk[:], oh[:, 0, :, :], oh[:, 1, :, :], ALU.add).then_inc(mask_ready, 1)

                def route_b(b):
                    dve.wait_ge(pref_done, b * 1 + 1)
                    dve.tensor_tensor(pos[:], pref, carry[:].unsqueeze(1).to_broadcast([P, W, E]), ALU.add)
                    rt.link(dve.tensor_reduce(tsum[:], tot.rearrange("p w e -> p e w"), AX.X, ALU.add))
                    dve.tensor_tensor(carry[:], carry[:], tsum[:], ALU.add).then_inc(pref_read, 1)
                    dve.wait_ge(pref_read, b * 1 + 1)
                    for k in range(2):
                        i = dve.tensor_tensor(ohp[:, k, :, :], oh[:, k, :, :], pos[:], ALU.mult)
                    rt.link(i)
                    rt.link(dve.tensor_reduce(posk[:], ohp[:], AX.X, ALU.add))
                    dve.tensor_scalar(valid[:], posk[:], float(CAP), None, ALU.is_lt)
                    rt.link(dve.scalar_tensor_tensor(dest[:], ixf[:], float(CAP), posk[:], ALU.mult, ALU.add))
                    dve.tensor_copy(valid_all[:, b, :, :], valid[:])
                    rt.link(dve.tensor_tensor(dest[:], dest[:], trash[:], ALU.subtract))
                    rt.link(dve.tensor_tensor(dest[:], dest[:], valid[:], ALU.mult))
                    wait(dve, scattered, b * (2 * W * DMA))
                    wait(dve, dest_saved, b * 1)
                    dve.tensor_tensor(dest_st[:], dest[:], trash[:], ALU.add).then_inc(dest_ready, 1)
                    rt.done()

                def product(b, j):
                    n = b * SB + j
                    dve.wait_ge(silu_done, n + 1)
                    wait(dve, dn_done, n - 1)
                    dve.tensor_tensor(acts[:, j % 2, :], sil[:, j % 2, :], up[j % 2][:], ALU.mult)\
                        .then_inc(act_ready, 1)

                def body(b, last=False):
                    dve.wait_ge(th_done, b * 1 + 1)
                    dve.tensor_scalar(hT_all[:, b, :], tx[1][:], normw[:, 0:1], None, ALU.mult).then_inc(hT_saved, 1)
                    route_a(b)
                    more = [] if last else [ln_a, ln_b, ln_c, ln_d]
                    for j in range(SB):
                        product(b, j)
                        if 1 <= j <= len(more):
                            more[j - 1](b + 1)
                        if j == 5:
                            route_b(b)

                dve.memset(carry[:], 0.0)
                for part in (ln_a, ln_b, ln_c):
                    part(0)
                ln_d(0)
                dve.wait_ge(small_loaded, 4 * DMA)
                dve.tensor_tensor(rs9[:, E:E + 1], rs9[:, E:E + 1], normw[:], ALU.mult).then_inc(consts, 1)
                dve.wait_ge(consts, 3)
                body(0)
                with dve.Fori(1, B - 1) as b:
                    body(b)
                body(B - 1, last=True)

            @block.scalar
            def _(act):
                def save_shared(b):
                    act.wait_ge(dn_done, b * SB + SB)
                    act.activation(ffn_all[:, b, :, :].rearrange("p w d -> p (w d)"), down[:], ACT.Copy)\
                        .then_inc(ffn_saved, 1)

                def body(b, first=False):
                    act.wait_ge(tx_done, b * 1 + 1)
                    wait(act, gu_done, b * SB)
                    act.activation(xnT[:], tx[0][:], ACT.Copy).then_inc(xnT_ready, 1)
                    if not first:
                        save_shared(b - 1)
                    for j in range(SB):
                        n = b * SB + j
                        act.wait_ge(gu_done, n + 1)
                        wait(act, act_ready, n - 1)
                        act.activation(sil[:, j % 2, :], gate[j % 2][:], ACT.Silu).then_inc(silu_done, 1)

                body(0, first=True)
                with act.Fori(1, B) as b:
                    body(b)
                save_shared(B - 1)

            @block.tensor
            def _(pe):
                def up_gate(b, j):
                    n = b * SB + j
                    wait(pe, silu_done, n - 1)
                    pe.matmul(gate[j % 2][:], wsg[:, j * P:(j + 1) * P], xnT[:], start=True, stop=True)
                    wait(pe, act_ready, n - 1)
                    pe.matmul(up[j % 2][:], wsu[:, j * P:(j + 1) * P], xnT[:], start=True, stop=True)\
                        .then_inc(gu_done, 1)

                def down_part(b, j):
                    pe.wait_ge(act_ready, b * SB + j + 1)
                    if j == 0:
                        wait(pe, ffn_saved, b * 1)
                    for w in range(W):
                        i = pe.matmul(down[:, w * D:(w + 1) * D], acts[:, j % 2, w * P:(w + 1) * P], wsd[:, j, :],
                                      start=(j == 0 and w == 0), stop=(j == SB - 1), skip_group_check=True)
                    i.then_inc(dn_done, 1)

                def body(b, first=False):
                    pe.wait_ge(xn_ready, b * 1 + 1)
                    wait(pe, xnT_ready, b * 1)
                    for w in range(W):
                        i = pe.transpose(tx[0][:, w * P:(w + 1) * P], xn_st[:, w, :], ident[:])
                    i.then_inc(tx_done, 1)
                    if not first:
                        down_part(b - 1, SB - 1)
                    pe.wait_ge(h_ready, b * 1 + 1)
                    wait(pe, hT_saved, b * 1)
                    for w in range(W):
                        i = pe.transpose(tx[1][:, w * P:(w + 1) * P], h_st[:, w, :], ident[:])
                    i.then_inc(th_done, 1)
                    pe.wait_ge(xnT_ready, b * 1 + 1)
                    wait(pe, pref_read, b * 1)
                    for w in range(W):
                        i = pe.matmul(lgv[:, w, 0:E + 1], xnT[:, w * P:(w + 1) * P], rs9[:], start=True, stop=True)
                    i.then_inc(lg_done, 1)
                    if first:
                        pe.wait_ge(wffn_loaded, 3 * DMA)
                    for j in range(SB):
                        up_gate(b, j)
                        if j >= 1:
                            down_part(b, j - 1)
                        if j == 3:
                            pe.wait_ge(mask_ready, b * 1 + 1)
                            pe.matmul(pref, before[:], msk[:], start=True, stop=False, skip_group_check=True)
                            for d in range(1, W):
                                pe.matmul(pref[:, d:W, :], ones_bf[:], msk[:, 0:W - d, :], start=False,
                                          stop=(d == W - 1), skip_group_check=True)
                            pe.matmul(tot, ones_bf[:], msk[:], start=True, stop=True).then_inc(pref_done, 1)

                pe.wait_ge(consts, 3)
                body(0, first=True)
                with pe.Fori(1, B) as b:
                    body(b)
                down_part(B - 1, SB - 1)

        def stage2(s2):
            def sb(name, shape, dt=F32):
                return s2.enter_context(nc.sbuf_tensor(name, shape, dt))

            def sem(name):
                return s2.enter_context(nc.semaphore(name))

            xgr = [sb(f"xgr{i}", [P, CT, D]) for i in range(2)]
            xgT = [sb(f"xgT{i}", [D, CAP]) for i in range(2)]
            acte = [sb(f"acte{i}", [P, RB, CAP]) for i in range(2)]
            sile = sb("sile", [P, 2, HALF])
            eo = [sb(f"eo{i}", [P, CT, D]) for i in range(2)]
            gate, up, tb, dn = bank[0:2], bank[2:4], bank[4:6], bank[6:8]
            STEPS = 2 * RB

            xgr_loaded = [sem(f"xgr_loaded{i}") for i in range(2)]
            w2_loaded = [sem(f"w2_loaded{i}") for i in range(2)]
            xt_done, xgT_ready, egu_done, esilu_done = sem("xt_done"), sem("xgT_ready"), sem("egu_done"), sem("esilu_done")
            eact_ready, edn_done, eo_saved = sem("eact_ready"), sem("edn_done"), sem("eo_saved")

            block = s2.enter_context(nc.Block())

            @block.sync
            def _(sp):
                def rows(e, i):
                    sp.dma_start(xgr[i][:], xg_dram[bass.ds(e * CAP, CAP), :].rearrange("(s p) d -> p s d", p=P))\
                        .then_inc(xgr_loaded[i], DMA)

                sp.wait_ge(scattered, B * 2 * W * DMA)
                rows(0, 0)
                rows(1, 1)
                with sp.Fori(1, E // 2) as r:
                    for i in range(2):
                        e = r * 2 + i
                        sp.wait_ge(xt_done, e - 1)
                        rows(e, i)
                        sp.wait_ge(edn_done, e - 1)
                        sp.dma_start(wge[i][:], rg[bass.ds(e, 1)].rearrange("a d f -> d (a f)")).then_inc(w2_loaded[i], DMA)
                        sp.dma_start(wue[i][:], ru[bass.ds(e, 1)].rearrange("a d f -> d (a f)")).then_inc(w2_loaded[i], DMA)
                        sp.dma_start(wde[i][:], rd[bass.ds(e, 1)].rearrange("a (j p) d -> p (a j) d", p=P))\
                            .then_inc(w2_loaded[i], DMA)

            @block.gpsimd
            def _(pool):
                with pool.Fori(0, E // 2) as r:
                    for i in range(2):
                        e = r * 2 + i
                        pool.wait_ge(eo_saved, e + 1)
                        pool.dma_start(eo_dram[bass.ds(e * CAP, CAP), :].rearrange("(s p) d -> p s d", p=P), eo[i][:])\
                            .then_inc(eo_stored[i], DMA)
                for i in range(2):
                    pool.wait_ge(eo_stored[i], (E // 2 + 1) * DMA)

            @block.scalar
            def _(act):
                def save(e, i, r):
                    act.wait_ge(edn_done, e + 1)
                    act.wait_ge(eo_stored[i], r * DMA + DMA)
                    act.activation(eo[i][:, 0:4, :].rearrange("p s d -> p (s d)"), dn[0][:], ACT.Copy)
                    act.activation(eo[i][:, 4, :], dn[1][:, 0:D], ACT.Copy).then_inc(eo_saved, 1)

                def body(r, first=False):
                    for i in range(2):
                        e = r * 2 + i
                        for s in range(STEPS):
                            n = e * STEPS + s
                            act.wait_ge(egu_done, n + 1)
                            wait(act, eact_ready, n - 1)
                            act.activation(sile[:, s % 2, :], gate[s % 2][:, 0:HALF], ACT.Silu).then_inc(esilu_done, 1)
                            if s == 1 and not (first and i == 0):
                                save(e - 1, 1 - i, r - 1 + i)

                body(0, first=True)
                with act.Fori(1, E // 2) as r:
                    body(r)
                save(E - 1, 1, E // 2 - 1)

            @block.vector
            def _(dve):
                def turned(e, i):
                    dve.wait_ge(xt_done, e + 1)
                    dve.tensor_copy(xgT[i][:, 0:512], tb[0][:])
                    dve.tensor_copy(xgT[i][:, 512:CAP], tb[1][:, 0:CAP - 512]).then_inc(xgT_ready, 1)

                def body(r, last=False):
                    for i in range(2):
                        e = r * 2 + i
                        for s in range(STEPS):
                            n = e * STEPS + s
                            j, h = s // 2, s % 2
                            dve.wait_ge(esilu_done, n + 1)
                            if s == 0:
                                wait(dve, edn_done, e - 1)
                            dve.tensor_tensor(acte[i][:, j, h * HALF:(h + 1) * HALF], sile[:, h, :], up[h][:, 0:HALF],
                                              ALU.mult).then_inc(eact_ready, 1)
                            if s == 0 and not (last and i == 1):
                                turned(e + 1, 1 - i)

                turned(0, 0)
                body(0)
                with dve.Fori(1, E // 2 - 1) as r:
                    body(r)
                body(E // 2 - 1, last=True)

            @block.tensor
            def _(pe):
                def turn(e, i, r):
                    pe.wait_ge(xgr_loaded[i], r * DMA + DMA)
                    wait(pe, xgT_ready, e)
                    for s in range(CT):
                        t = pe.transpose(tb[s // 4][:, (s % 4) * P:(s % 4 + 1) * P], xgr[i][:, s, :], ident[:])
                    t.then_inc(xt_done, 1)

                def up_gate(e, i, s):
                    n = e * STEPS + s
                    j, h = s // 2, s % 2
                    wait(pe, esilu_done, n - 1)
                    pe.matmul(gate[h][:, 0:HALF], wge[i][:, j * P:(j + 1) * P], xgT[i][:, h * HALF:(h + 1) * HALF],
                              start=True, stop=True)
                    wait(pe, eact_ready, n - 1)
                    pe.matmul(up[h][:, 0:HALF], wue[i][:, j * P:(j + 1) * P], xgT[i][:, h * HALF:(h + 1) * HALF],
                              start=True, stop=True).then_inc(egu_done, 1)

                def down(e, i):
                    pe.wait_ge(eact_ready, e * STEPS + STEPS)
                    wait(pe, eo_saved, e)
                    for s in range(CT):
                        for j in range(RB):
                            d = pe.matmul(dn[s // 4][:, (s % 4) * D:(s % 4 + 1) * D], acte[i][:, j, s * P:(s + 1) * P],
                                          wde[i][:, j, :], start=(j == 0), stop=(j == RB - 1))
                    d.then_inc(edn_done, 1)

                def body(r, first=False, last=False):
                    for i in range(2):
                        e = r * 2 + i
                        pe.wait_ge(xgT_ready, e + 1)
                        if not first:
                            pe.wait_ge(w2_loaded[i], r * 3 * DMA)
                        for s in range(STEPS):
                            up_gate(e, i, s)
                            if s == 0:
                                if not (first and i == 0):
                                    down(e - 1, 1 - i)
                                if not (last and i == 1):
                                    turn(e + 1, 1 - i, r + i)

                pe.wait_ge(we_loaded, 6 * DMA)
                turn(0, 0, 0)
                body(0, first=True)
                with pe.Fori(1, E // 2 - 1) as r:
                    body(r)
                body(E // 2 - 1, last=True)
                down(E - 1, 1)

        def choose(s3, kg_all, vg_all, gm_all, wts):
            with ExitStack() as own_mem:
                def sb(name, shape, dt=F32):
                    return own_mem.enter_context(nc.sbuf_tensor(name, shape, dt))

                def sem(name):
                    return s3.enter_context(nc.semaphore(name))

                sc8 = sb("sc8", [B, S])
                wk8 = [sb(f"wk8{i}", [B, S]) for i in range(2)]
                top = sb("top", [B, 8])
                sel8 = sb("sel8", [B, 2, S])
                selc = sb("selc", [P, 2, W, B])
                selr = sb("selr", [P, B, W])
                eqg = sb("eqg", [P, B, W, NG])
                seln = sb("seln", [P, B, W, NG])
                hgr = sb("hgr", [P, 2, D])
                hgT = sb("hgT", [D, B * NG])
                vgs = sb("vgs", [P, 2, H * HD])
                e2 = sb("e2", [P, B, W])
                den = sb("den", [P, B, W])

                sc_done, sel_ready, selc_done, seln_ready = sem("sc_done"), sem("sel_ready"), sem("selc_done"), sem("seln_ready")
                hgr_done, hgr_ready, hgT_done, hgT_ready = sem("hgr_done"), sem("hgr_ready"), sem("hgT_done"), sem("hgT_ready")
                kg_done, vg_done, vgs_ready = sem("kg_done"), sem("vg_done"), sem("vgs_ready")
                vg_stored, vg_loaded, e2_ready, cc = sem("vg_stored"), sem("vg_loaded"), sem("e2_ready"), sem("cc")
                block = own_mem.enter_context(nc.Block())

                @block.tensor
                def _(pe):
                    for w in range(W):
                        i = pe.transpose(bank[0][0:B, w * P:(w + 1) * P], score_all[:, :, w], ident[:])
                    i.then_inc(sc_done, 1)
                    pe.wait_ge(sel_ready, 1)
                    for a in range(2):
                        for w in range(W):
                            o = (a * W + w) * B
                            i = pe.transpose(bank[1][:, o:o + B], sel8[:, a, w * P:(w + 1) * P], ident[0:B, 0:B])
                    i.then_inc(selc_done, 1)
                    pe.wait_ge(seln_ready, 1)
                    for f in range(2):
                        for c in range(4):
                            for w in range(W):
                                i = pe.matmul(bank[2][32 * c:32 * c + 32, f * D:(f + 1) * D],
                                              seln[:, 4 * f + c, w, :], xn_all[:, 4 * f + c, w, :],
                                              start=(w == 0), stop=(w == W - 1))
                    i.then_inc(hgr_done, 1)
                    pe.wait_ge(hgr_ready, 1)
                    for f in range(2):
                        i = pe.transpose(bank[3][:, f * P:(f + 1) * P], hgr[:, f, :], ident[:])
                    i.then_inc(hgT_done, 1)
                    pe.wait_ge(hgT_ready, 1)
                    pe.wait_ge(wattn_loaded, 3 * DMA)
                    for f in range(2):
                        for n in range(2):
                            i = pe.matmul(bank[4 + 2 * f + n][:], hgT[:, f * P:(f + 1) * P], wv[:, n * 512:(n + 1) * 512],
                                          start=True, stop=True)
                    i.then_inc(vg_done, 1)
                    for m in range(2 * G):
                        i = pe.matmul(bank[m // 2][:, (m % 2) * B * NG:(m % 2 + 1) * B * NG], wk[:, m * P:(m + 1) * P],
                                      hgT[:], start=True, stop=True)
                    i.then_inc(kg_done, 1)

                @block.scalar
                def _(act):
                    act.activation(e2[:], dlog_all[:], ACT.Exp).then_inc(e2_ready, 1)
                    act.wait_ge(vg_done, 1)
                    for m in range(4):
                        i = act.activation(vgs[:, m // 2, (m % 2) * 512:(m % 2 + 1) * 512], bank[4 + m][:], ACT.Copy)
                    i.then_inc(vgs_ready, 1)

                @block.sync
                def _(sp):
                    sp.wait_ge(vgs_ready, 1)
                    sp.dma_start(vg_dram.rearrange("(f p) e -> p f e", p=P), vgs[:]).then_inc(vg_stored, DMA)
                    sp.wait_ge(vg_stored, DMA)
                    for c in range(HG):
                        src = vg_dram.rearrange("(b s) (g j d) -> j s b g d", s=NG, j=HG, d=HD)[HOME[c]]
                        for b in range(B):
                            sp.dma_start(vg_all[32 * c:32 * c + 32, b, :, :], src[:, b]).then_inc(vg_loaded, DMA)
                    sp.wait_ge(vg_loaded, HG * B * DMA)

                @block.vector
                def _(dve):
                    ch = Chain(dve, cc, 22)
                    ch.round(0)
                    dve.wait_ge(sc_done, 1)
                    ch.link(dve.tensor_copy(sc8[:], bank[0][0:B, :]))
                    now = sc8
                    for r in range(NG // 8):
                        ch.link(dve.max(top[:], now[:]))
                        ch.link(dve.match_replace(wk8[r % 2][:], top[:], now[:], -BIG))
                        now = wk8[r % 2]
                    ch.link(dve.tensor_tensor(sel8[:, 0, :], sc8[:], now[:], ALU.not_equal))
                    dve.tensor_tensor_scan(sel8[:, 1, :], onesr[:], sel8[:, 0, :], 0.0, ALU.mult, ALU.add)\
                        .then_inc(sel_ready, 1)
                    dve.wait_ge(selc_done, 1)
                    ch.link(dve.tensor_copy(selc[:].rearrange("p a w b -> p (a w b)"), bank[1][:, 0:2 * W * B]))
                    cum = selc[:, 1, :, :].rearrange("p w b -> p b w").unsqueeze(3).to_broadcast([P, B, W, NG])
                    place = iota_g[:].unsqueeze(1).unsqueeze(1).to_broadcast([P, B, W, NG])
                    dve.tensor_tensor(selr[:], selc[:, 0, :, :].rearrange("p w b -> p b w"), r1_all[:], ALU.mult)
                    ch.link(dve.tensor_tensor(eqg[:], place, cum, ALU.is_equal))
                    dve.tensor_tensor(seln[:], eqg[:], selr[:].unsqueeze(3).to_broadcast([P, B, W, NG]), ALU.mult)\
                        .then_inc(seln_ready, 1)
                    ch.link(dve.tensor_tensor(gm_all[:], place, cum, ALU.is_gt))
                    ch.link(dve.tensor_scalar(gm_all[:], gm_all[:], NEG, None, ALU.mult))
                    dve.tensor_copy(maskb[:, :, P:KEYS], gm_all[:, 0, :, :])
                    dve.wait_ge(hgr_done, 1)
                    dve.tensor_copy(hgr[:].rearrange("p f d -> p (f d)"), bank[2][:, 0:2 * D]).then_inc(hgr_ready, 1)
                    dve.wait_ge(hgT_done, 1)
                    dve.tensor_scalar(hgT[:], bank[3][:, 0:2 * P], normw[:, 0:1], None, ALU.mult).then_inc(hgT_ready, 1)
                    dve.wait_ge(e2_ready, 1)
                    ch.link(dve.tensor_scalar(den[:], e2[:], 1.0, None, ALU.add))
                    ch.link(dve.reciprocal(den[:], den[:]))
                    ch.link(dve.tensor_tensor(e2[:], e2[:], den[:], ALU.mult))
                    dve.tensor_tensor(wts[:, :, 0, :], den[:], valid_all[:, :, 0, :], ALU.mult)
                    ch.link(dve.tensor_tensor(wts[:, :, 1, :], e2[:], valid_all[:, :, 1, :], ALU.mult))
                    dve.wait_ge(kg_done, 1)
                    for m in range(G):
                        i = dve.tensor_copy(kg_all[:, 2 * m:2 * m + 2, :, :].rearrange("p m b s -> p (m b s)"), bank[m][:])
                    ch.link(i)

        def stage3(s3):
            def sb(name, shape, dt=F32):
                return s3.enter_context(nc.sbuf_tensor(name, shape, dt))

            def sem(name):
                return s3.enter_context(nc.semaphore(name))

            kg_all = sb("kg_all", [P, 2 * G, B, NG])
            vg_all = sb("vg_all", [P, B, G, HD])
            gm_all = sb("gm_all", [P, B, W, NG])
            wts = sb("wts", [P, B, 2, W])
            choose(s3, kg_all, vg_all, gm_all, wts)

            hTs = sb("hTs", [D, S])
            qT = [sb(f"qT{i}", [P, 2, S]) for i in range(2)]
            kT = [sb(f"kT{i}", [P, 2, W, KEYS]) for i in range(2)]
            vv = [sb(f"vv{i}", [P, W, HG * HD]) for i in range(2)]
            vgbd = [sb(f"vgbd{i}", [P, 2, HG, 32]) for i in range(2)]
            sm = [sb(f"sm{i}", [P, HG, KEYS]) for i in range(2)]
            nmx = [sb(f"nmx{i}", [P, HG]) for i in range(2)]
            ssum = [sb(f"ssum{i}", [P, HG]) for i in range(2)]
            rec = [sb(f"rec{i}", [P, HG]) for i in range(2)]
            ex = [sb(f"ex{i}", [P, HG, KEYS]) for i in range(2)]
            prob = sb("prob", [P, W, HG, P])
            probg = sb("probg", [P, W, HG, NG])
            pT = sb("pT", [P, W, HG, P])
            pTg = sb("pTg", [P, S])
            oT = sb("oT", [P, G, 2, S])
            gd = sb("gd", [P, 2, W], U32)
            g_st = sb("g_st", [P, 2, W, D])
            ff = sb("ff", [P, W, D])
            ef = sb("ef", [P, W, D])
            ss = sb("ss", [P, W, D])
            x_fin = sb("x_fin", [P, W, D])
            o_fin = sb("o_fin", [P, W, D])

            sx, sy, pa, tb, ob = bank[0], bank[1], bank[2:4], bank[4:6], bank[6:8]
            USES = 6
            TURNS = W + 1

            a_done, a_evac, hts_ready, kg_ready, vgbd_ready = (sem(n) for n in
                ("a_done", "a_evac", "hts_ready", "kg_ready", "vgbd_ready"))
            sx_done, sy_done, sx_read, sy_read = (sem(n) for n in ("sx_done", "sy_done", "sx_read", "sy_read"))
            exp_done, rec_ready, prob_ready = (sem(n) for n in ("exp_done", "rec_ready", "prob_ready"))
            turn_done, turn_evac, pv_done, o_evac = (sem(n) for n in ("turn_done", "turn_evac", "pv_done", "o_evac"))
            out_done, out_read, mask_set = sem("out_done"), sem("out_read"), sem("mask_set")
            gd_ready, gathered, gw_ready = sem("gd_ready"), sem("gathered"), sem("gw_ready")
            ff_ready, ef_ready, fin_ready, out_stored = sem("ff_ready"), sem("ef_ready"), sem("fin_ready"), sem("out_stored")
            xf_loaded, fc = sem("xf_loaded"), sem("fc")

            block = s3.enter_context(nc.Block())

            @block.sync
            def _(sp):
                def finish(b):
                    sp.wait_ge(fin_ready, b * 1 + 1)
                    sp.dma_start(out_rows[b], o_fin[:]).then_inc(out_stored, DMA)

                sp.dma_start(x_fin[:], x_rows[0]).then_inc(xf_loaded, DMA)
                with sp.Fori(0, B - 1) as b:
                    finish(b)
                    sp.wait_ge(out_stored, b * DMA + DMA)
                    sp.dma_start(x_fin[:], x_rows[b + 1]).then_inc(xf_loaded, DMA)
                finish(B - 1)
                sp.wait_ge(out_stored, B * DMA)

            @block.tensor
            def _(pe):
                def project(b, g, some):
                    i = b * G + g
                    if g == 0 and some[0] == 0:
                        pe.wait_ge(hts_ready, b * 1 + 1)
                    for m in some:
                        wait(pe, a_evac, i * USES + m - 1)
                        o = pa[m % 2]
                        if m < 4:
                            w_sb, blk = (wq, wk)[m // 2], 2 * g + m % 2
                            t = pe.matmul(o[:], w_sb[:, blk * P:(blk + 1) * P], hTs[:], start=True, stop=True)
                        else:
                            for w in range(2):
                                u = 2 * (m - 4) + w
                                t = pe.matmul(o[:, w * 256:(w + 1) * 256], hTs[:, u * P:(u + 1) * P],
                                              wv[:, g * 256:(g + 1) * 256], start=True, stop=True)
                        t.then_inc(a_done, 1)

                def scores(b, g, w):
                    i, par = b * G + g, g % 2
                    if w == 0:
                        pe.wait_ge(a_evac, i * USES + 4)
                        pe.wait_ge(kg_ready, i + 1)
                    n = i * W + w
                    for o, r0, s_done, s_read in ((sx, 0, sx_done, sx_read), (sy, 64, sy_done, sy_read)):
                        wait(pe, s_read, n)
                        for blk in range(2):
                            t = pe.matmul(o[:, blk * KEYS:(blk + 1) * KEYS],
                                          qT[par][r0:r0 + 64, blk, w * P:(w + 1) * P],
                                          kT[par][r0:r0 + 64, blk, w, :], start=True, stop=True)
                        t.then_inc(s_done, 1)

                def values_global(b, g):
                    i, par = b * G + g, g % 2
                    pe.wait_ge(turn_evac, i * TURNS + TURNS)
                    pe.wait_ge(vgbd_ready, i + 1)
                    if g == 0:
                        wait(pe, out_read, b * 1)
                    for f in range(2):
                        wait(pe, o_evac, i * 2 + f - 1)
                        pe.matmul(ob[f][:], vgbd[par][:, f, :, :].rearrange("p c d -> p (c d)"), pTg[:],
                                  start=True, stop=False, skip_group_check=True)

                def values_local(b, g):
                    i, par = b * G + g, g % 2
                    pe.wait_ge(a_evac, i * USES + USES)
                    for f in range(2):
                        for w in range(W):
                            for c in range(HG):
                                v0 = HOME[c] * HD + f * 32
                                t = pe.matmul(ob[f][32 * c:32 * c + 32, w * P:(w + 1) * P], vv[par][:, w, v0:v0 + 32],
                                              pT[:, w, c, :], start=False, stop=(w == W - 1), skip_group_check=True)
                        t.then_inc(pv_done, 1)

                def turn(b, g, some):
                    i = b * G + g
                    for u in some:
                        wait(pe, turn_evac, i * TURNS + u - 1)
                        o = tb[(g + u) % 2]
                        for c in range(4):
                            if u < W:
                                if c == 0:
                                    pe.wait_ge(prob_ready, i * W + u + 1)
                                src = prob[:, u, c, :]
                            else:
                                src = probg[:, c, :, :].rearrange("p c s -> p (c s)")
                            t = pe.transpose(o[:, c * P:(c + 1) * P], src, ident[:])
                        t.then_inc(turn_done, 1)

                def output(b, some):
                    pe.wait_ge(o_evac, b * (2 * G) + 2 * G)
                    for w in some:
                        for g in range(G):
                            for f in range(2):
                                t = pe.matmul(ob[0][:, w * D:(w + 1) * D], oT[:, g, f, w * P:(w + 1) * P],
                                              wo[:, g, f, :], start=(g + f == 0), stop=(g == G - 1 and f == 1))
                    if W - 1 in some:
                        t.then_inc(out_done, 1)

                def step(b, g, first=False, last=False):
                    before_it = None if first and g == 0 else (b if g else b - 1, (g - 1) % G)
                    after_it = None if last and g == G - 1 else (b if g < G - 1 else b + 1, (g + 1) % G)
                    scores(b, g, 0)
                    if before_it:
                        values_global(*before_it)
                    scores(b, g, 1)
                    if before_it:
                        values_local(*before_it)
                    scores(b, g, 2)
                    if after_it:
                        project(*after_it, (0, 1))
                    scores(b, g, 3)
                    if after_it:
                        project(*after_it, (2, 3))
                    if g == 0 and not first:
                        output(b - 1, (0, 1))
                    turn(b, g, (0, 1))
                    if after_it:
                        project(*after_it, (4, 5))
                    if g == 0 and not first:
                        output(b - 1, (2, 3))
                    turn(b, g, (2, 3, 4))

                project(0, 0, range(USES))
                for g in range(G):
                    step(0, g, first=True)
                pe.wait_ge(wout_loaded, 2 * HG * DMA)
                with pe.Fori(1, B - 1) as b:
                    for g in range(G):
                        step(b, g)
                for g in range(G):
                    step(B - 1, g, last=True)
                values_global(B - 1, G - 1)
                values_local(B - 1, G - 1)
                output(B - 1, range(W))

            @block.vector
            def _(dve):
                fin = Chain(dve, fc, 4)

                def mask_scores(b, g, w):
                    n = (b * G + g) * W + w
                    wait(dve, exp_done, n - 1)
                    for o, c0, s_done, s_read in ((sx, 0, sx_done, sx_read), (sy, 2, sy_done, sy_read)):
                        dve.wait_ge(s_done, n + 1)
                        settle(dve)
                        for c in range(2):
                            t = dve.tensor_tensor_reduce(out=sm[w % 2][:, c0 + c, :], in0=o[:, c * KEYS:(c + 1) * KEYS],
                                                         in1=maskb[:, w, :], scale=-1.0, scalar=BIG, op0=ALU.add,
                                                         op1=ALU.min, accum_out=nmx[w % 2][:, c0 + c:c0 + c + 1])
                        t.then_inc(s_read, 1)

                def invert(b, g, w):
                    n = (b * G + g) * W + w
                    dve.wait_ge(exp_done, n + 1)
                    wait(dve, prob_ready, n - 1)
                    dve.reciprocal(rec[w % 2][:], ssum[w % 2][:]).then_inc(rec_ready, 1)

                def take(b, g, some):
                    i, par = b * G + g, g % 2
                    for m in some:
                        dve.wait_ge(a_done, i * USES + m + 1)
                        o = pa[m % 2]
                        if m < 2:
                            t = dve.tensor_scalar(qT[par][:, m, :], o[:], float(HD) ** -0.5, None, ALU.mult)
                        elif m < 4:
                            t = dve.tensor_copy(kT[par][:, m - 2, :, 0:P], o[:].rearrange("p (w k) -> p w k", w=W))
                        else:
                            v = 2 * (m - 4)
                            t = dve.tensor_copy(vv[par][:, v:v + 2, :].rearrange("p w e -> p (w e)"), o[:])
                        t.then_inc(a_evac, 1)

                def join(b):
                    fin.round(b)
                    dve.wait_ge(gw_ready, b * 1 + 1)
                    fin.link(dve.tensor_tensor(ff[:], g_st[:, 0, :, :], g_st[:, 1, :, :], ALU.add))
                    dve.tensor_tensor(ff[:], ff[:], ffn_all[:, b, :, :], ALU.add).then_inc(ff_ready, 1)
                    dve.wait_ge(out_done, b * 1 + 1)
                    dve.tensor_tensor(ss[:], ob[0][:].rearrange("p (w d) -> p w d", w=W), xn_all[:, b, :, :], ALU.add)\
                        .then_inc(out_read, 1)

                def close(b):
                    dve.wait_ge(ef_ready, b * 1 + 1)
                    fin.link(dve.tensor_scalar(ef[:], ef[:], 1.0, None, ALU.add))
                    dve.wait_ge(out_read, b * 1 + 1)
                    dve.tensor_tensor(ss[:], ss[:], ff[:], ALU.mult)
                    fin.link(dve.reciprocal(ef[:], ef[:]))
                    fin.link(dve.tensor_tensor(ss[:], ss[:], ef[:], ALU.mult))
                    dve.wait_ge(xf_loaded, b * DMA + DMA)
                    dve.tensor_tensor(o_fin[:], ss[:], x_fin[:], ALU.add).then_inc(fin_ready, 1)
                    fin.done()

                def step(b, g, first=False, last=False):
                    after_it = None if last and g == G - 1 else (b if g < G - 1 else b + 1, (g + 1) % G)
                    if g == 0:
                        wait(dve, mask_set, b * 1)
                    mask_scores(b, g, 0)
                    mask_scores(b, g, 1)
                    invert(b, g, 0)
                    mask_scores(b, g, 2)
                    invert(b, g, 1)
                    if after_it:
                        take(*after_it, (0, 1))
                    mask_scores(b, g, 3)
                    if g == G - 1 and not last:
                        dve.wait_ge(sy_read, (b * G + g) * W + W)
                        dve.tensor_copy(maskb[:, :, P:KEYS], gm_all[:, b + 1, :, :]).then_inc(mask_set, 1)
                    invert(b, g, 2)
                    if after_it:
                        take(*after_it, (2, 3))
                    invert(b, g, 3)
                    if after_it:
                        take(*after_it, (4, 5))
                    if not first:
                        if g == 0:
                            join(b - 1)
                        if g == 1:
                            close(b - 1)

                take(0, 0, range(USES))
                for g in range(G):
                    step(0, g, first=True)
                with dve.Fori(1, B - 1) as b:
                    for g in range(G):
                        step(b, g)
                for g in range(G):
                    step(B - 1, g, last=True)
                join(B - 1)
                close(B - 1)

            @block.scalar
            def _(act):
                def exps(b, g, w):
                    i = b * G + g
                    n = i * W + w
                    act.wait_ge(sy_read, n + 1)
                    wait(act, rec_ready, n - 1)
                    wait(act, prob_ready, n - 1)
                    for c in range(HG):
                        t = act.activation(ex[w % 2][:, c, :], sm[w % 2][:, c, :], ACT.Exp, bias=nmx[w % 2][:, c:c + 1],
                                           scale=-1.0, accum_out=ssum[w % 2][:, c:c + 1])
                    t.then_inc(exp_done, 1)

                def save_values(b, g):
                    for f in range(2):
                        act.wait_ge(pv_done, (b * G + g) * 2 + f + 1)
                        act.activation(oT[:, g, f, :], ob[f][:], ACT.Copy).then_inc(o_evac, 1)

                def save_turned(b, g):
                    for u in range(TURNS):
                        act.wait_ge(turn_done, (b * G + g) * TURNS + u + 1)
                        o = tb[(g + u) % 2]
                        dst = pT[:, u, :, :].rearrange("p c q -> p (c q)") if u < W else pTg[:]
                        act.activation(dst, o[:], ACT.Copy).then_inc(turn_evac, 1)

                def sigmoid_part(b):
                    act.wait_ge(ff_ready, b * 1 + 1)
                    act.activation(ef[:], ff[:], ACT.Exp, scale=-1.0).then_inc(ef_ready, 1)

                def step(b, g, first=False):
                    exps(b, g, 0)
                    exps(b, g, 1)
                    if not (first and g == 0):
                        save_values(b if g else b - 1, (g - 1) % G)
                    exps(b, g, 2)
                    exps(b, g, 3)
                    save_turned(b, g)
                    if g == 0 and not first:
                        sigmoid_part(b - 1)

                for g in range(G):
                    step(0, g, first=True)
                with act.Fori(1, B) as b:
                    for g in range(G):
                        step(b, g)
                save_values(B - 1, G - 1)
                sigmoid_part(B - 1)

            @block.gpsimd
            def _(pool):
                def own_rows(b):
                    wait(pool, a_done, b * (G * USES))
                    pool.tensor_copy(hTs[:], hT_all[:, b, :]).then_inc(hts_ready, 1)

                def global_keys(b, g):
                    i, par = b * G + g, g % 2
                    wait(pool, sy_done, (i - 1) * W)
                    pool.tensor_copy(kT[par][:, :, :, P:KEYS],
                                     kg_all[:, 2 * g:2 * g + 2, b, :].unsqueeze(2).to_broadcast([P, 2, W, NG]))\
                        .then_inc(kg_ready, 1)

                def global_values(b, g):
                    i, par = b * G + g, g % 2
                    wait(pool, pv_done, (i - 1) * 2)
                    v = vg_all[:, b, g, :].rearrange("p (f d) -> p f d", f=2)
                    pool.tensor_tensor(vgbd[par][:], v.unsqueeze(2).to_broadcast([P, 2, HG, 32]),
                                       own[:].unsqueeze(1).to_broadcast([P, 2, HG, 32]), ALU.mult).then_inc(vgbd_ready, 1)

                def divide(b, g, w):
                    n = (b * G + g) * W + w
                    pool.wait_ge(rec_ready, n + 1)
                    if w == 0:
                        wait(pool, turn_done, (b * G + g) * TURNS)
                    for dst, k0, k1 in ((prob, 0, P), (probg, P, KEYS)):
                        t = pool.tensor_tensor(dst[:, w, :, :], ex[w % 2][:, :, k0:k1],
                                               rec[w % 2][:].unsqueeze(2).to_broadcast([P, HG, k1 - k0]), ALU.mult)
                    t.then_inc(prob_ready, 1)

                picks = [(k, w) for w in range(W) for k in range(2)]

                def gather(b, some):
                    for k, w in some:
                        pool.indirect_dma_start(out=g_st[:, k, w, :], out_offset=None, in_=eo_dram,
                                                in_offset=bass.IndirectOffsetOnAxis(ap=gd[:, k, w:w + 1], axis=0))\
                            .then_inc(gathered, DMA)

                def step(b, g, last=False):
                    if g == G - 1 and not last:
                        own_rows(b + 1)
                    if not (last and g == G - 1):
                        ahead = (b if g < G - 1 else b + 1, (g + 1) % G)
                        global_keys(*ahead)
                    for w in range(W):
                        divide(b, g, w)
                    if not (last and g == G - 1):
                        global_values(*ahead)
                    if g == 1:
                        wait(pool, ff_ready, b * 1)
                        pool.tensor_copy(gd[:], dest_all[:, b, :, :]).then_inc(gd_ready, 1)
                        pool.wait_ge(gd_ready, b * 1 + 1)
                        settle(pool)
                    if g >= 1:
                        gather(b, picks[3 * (g - 1):3 * g])
                    if g == G - 1:
                        pool.wait_ge(gathered, (b + 1) * (2 * W * DMA))
                        pool.tensor_tensor(g_st[:].rearrange("p k w d -> p (k w) d"),
                                           g_st[:].rearrange("p k w d -> p (k w) d"),
                                           wts[:, b, :, :].rearrange("p k w -> p (k w)").unsqueeze(2)
                                           .to_broadcast([P, 2 * W, D]), ALU.mult).then_inc(gw_ready, 1)

                own_rows(0)
                global_keys(0, 0)
                global_values(0, 0)
                for g in range(G):
                    step(0, g)
                with pool.Fori(1, B - 1) as b:
                    for g in range(G):
                        step(b, g)
                for g in range(G):
                    step(B - 1, g, last=True)

        for stage in (stage1, stage2, stage3):
            with ExitStack() as s:
                stage(s)


def kernel(**inputs):
    import numpy as _np
    import concourse.bacc as _bacc
    from concourse import mybir as _mybir
    from concourse.bass_utils import run_bass_kernel_spmd as _run

    nc = _bacc.Bacc("TRN2", target_bir_lowering=False, num_devices=1)
    arrays, args = {}, []
    for name in ["L0_attn_x", "L0_attn_norm_w", "L0_attn_w_q", "L0_attn_w_k", "L0_attn_w_v", "L0_attn_w_out",
                 "L0_attn_scorer_w", "L0_attn_scorer_b", "L0_ffn_router_w", "L0_ffn_rg", "L0_ffn_ru", "L0_ffn_rd",
                 "L0_ffn_sg", "L0_ffn_su", "L0_ffn_sd"]:
        a = _np.asarray(inputs[name])
        a = _np.ascontiguousarray(a.T if name == "L0_ffn_router_w" else a)
        arrays["in_" + name] = a
        args.append(nc.dram_tensor("in_" + name, a.shape, _mybir.dt.from_np(a.dtype), kind="ExternalInput").ap())
    shape = inputs["L0_attn_x"].shape
    out = nc.dram_tensor("out_0", shape, _mybir.dt.float32, kind="ExternalOutput").ap()
    recurrent_layer(nc, *args, out)
    r = _run(nc, [arrays], core_ids=[0])
    return r.results[0]["out_0"]
```

```python
import concourse.bass as bass
from concourse import mybir
from contextlib import ExitStack



def recurrent_layer(nc, x, norm_w, w_q, w_k, w_v, w_out, scorer_w, scorer_b, router_wT,
                    rg, ru, rd, sg, su, sd, out):
    F32, F32R, BF16, U32 = mybir.dt.float32, mybir.dt.float32r, mybir.dt.bfloat16, mybir.dt.uint32
    ALU, ACT, AX = mybir.AluOpType, mybir.ActivationFunctionType, mybir.AxisListType

    B, S, D = x.shape
    P = 128
    W = S // P
    T = B * S
    H, HD = w_q.shape[1] // 64, 64
    HG = 4
    G = H // HG
    NG = 32
    KEYS = P + NG
    E, _, FR = rg.shape
    FS = sg.shape[1]
    RB, SB = FR // P, FS // P
    CAP = max(int(1.25 * T / E), 1)
    CT = CAP // P
    HALF = CAP // 2
    SLOTS = E * CAP
    HOME = (0, 2, 1, 3)
    NEG = -1e30
    BIG = 3e38
    EPS_LN, EPS_ATT, EPS_FFN = 1e-5, 1e-6, 1.1920929e-07
    DMA = 16

    ctx = ExitStack()

    def sb(name, shape, dt=F32):
        return ctx.enter_context(nc.sbuf_tensor(name, shape, dt))

    def sem(name):
        return ctx.enter_context(nc.semaphore(name))

    def wait(eng, s, value):
        if not isinstance(value, int) or value > 0:
            eng.wait_ge(s, value)

    def settle(eng):
        eng.nop(nofuse=True)

    class Chain:

        def __init__(self, eng, s, per_round):
            self.eng, self.s, self.per = eng, s, per_round

        def round(self, r):
            self.base, self.n = r * self.per, 0

        def link(self, instruction):
            self.n += 1
            instruction.then_inc(self.s, 1)
            self.eng.wait_ge(self.s, self.base + self.n)

        def done(self):
            assert self.n == self.per, (self.n, self.per)

    x_rows = x.rearrange("b (w p) d -> b p w d", p=P)
    out_rows = out.rearrange("b (w p) d -> b p w d", p=P)

    with ctx:
        xg_dram = nc.dram_tensor("xg_dram", [SLOTS + 2 * W * P, D], F32, kind="Internal").ap()
        eo_dram = nc.dram_tensor("eo_dram", [SLOTS + 2 * W * P, D], F32, kind="Internal").ap()

        ident = sb("ident", [P, P])
        before = sb("before", [P, P], BF16)
        ones_bf = sb("ones_bf", [P, P], BF16)
        iota_e = sb("iota_e", [P, E])
        iota_g = sb("iota_g", [P, NG])
        trash = sb("trash", [P, 2, W])
        own = sb("own", [P, HG, 32])
        pow_m = sb("pow_m", [P, 2 * W])
        zeros = sb("zeros", [P, D])
        onesr = sb("onesr", [B, S])
        bias_s = sb("bias_s", [P, 1])
        normw = sb("normw", [P, 1])
        rs9 = sb("rs9", [D, E + 1])

        xn_all = sb("xn_all", [P, B, W, D])
        hT_all = sb("hT_all", [D, B, S])
        ffn_all = sb("ffn_all", [P, B, W, D])
        wv = sb("wv", [D, H * HD])
        wq2, wk2, wv2 = (sb(f"w{c}2", [D, 2, H * HD], F32R) for c in "qkv")
        wo = sb("wo", [P, G, 2, D])
        dest_all = sb("dest_all", [P, B, 2, W], U32)
        valid_all = sb("valid_all", [P, B, 2, W])
        dlog_all = sb("dlog_all", [P, B, W])
        score_all = sb("score_all", [P, B, W])
        r1_all = sb("r1_all", [P, B, W])
        maskb = sb("maskb", [P, W, KEYS])

        kg_all = sb("kg_all", [P, 2 * G, B, NG])
        gm_all = sb("gm_all", [P, B, W, NG])
        hgT = sb("hgT", [D, B * NG])

        bank = [ctx.enter_context(nc.psum_tensor(f"bank{i}", [P, 512], F32)) for i in range(8)]

        early = ExitStack()

        def sb(name, shape, dt=F32):
            return early.enter_context(nc.sbuf_tensor(name, shape, dt))

        wq = sb("wq", [D, H * HD])
        wk = sb("wk", [D, H * HD])
        wge = [sb(f"wge{i}", [D, FR]) for i in range(2)]
        wue = [sb(f"wue{i}", [D, FR]) for i in range(2)]
        wde = [sb(f"wde{i}", [P, RB, D]) for i in range(2)]
        wge2 = [sb(f"wge2{i}", [D, 2, FR], F32R) for i in range(2)]
        wue2 = [sb(f"wue2{i}", [D, 2, FR], F32R) for i in range(2)]
        wd_loaded = [sem(f"wd_loaded{i}") for i in range(2)]
        we_loaded, we_high, we_low = sem("we_loaded"), sem("we_high"), sem("we_low")
        wattn_loaded, wsplit = sem("wattn_loaded"), sem("wsplit")
        wout_loaded = sem("wout_loaded")
        eo_stored = [sem(f"eo_stored{i}") for i in range(2)]
        scattered = sem("scattered")
        consts = sem("consts")

        def product(pe, o, a, b):
            pe.matmul(o, a[0], b[0], start=True, stop=False)
            pe.matmul(o, a[0], b[1], start=False, stop=False)
            return pe.matmul(o, a[1], b[0], start=False, stop=True)

        def load_expert(sp, e, i):
            sp.dma_start(wge[i][:], rg[e]).then_inc(we_loaded, DMA)
            sp.dma_start(wue[i][:], ru[e]).then_inc(we_loaded, DMA)
            sp.dma_start(wde[i][:], rd[e].rearrange("(j p) d -> p j d", p=P)).then_inc(wd_loaded[i], DMA)

        def stage1(s1):
            def sb(name, shape, dt=F32):
                return s1.enter_context(nc.sbuf_tensor(name, shape, dt))

            def sem(name):
                return s1.enter_context(nc.semaphore(name))

            x_st = sb("x_st", [P, W, D])
            xn_st = sb("xn_st", [P, W, D])
            h_st = sb("h_st", [P, W, D])
            xn_sc = sb("xn_sc", [P, W, D])
            xnT = sb("xnT", [D, S])
            xnT2 = sb("xnT2", [D, 2, S], F32R)
            wsg = sb("wsg", [D, FS])
            wsu = sb("wsu", [D, FS])
            wsg2 = sb("wsg2", [D, 2, FS], F32R)
            wsu2 = sb("wsu2", [D, 2, FS], F32R)
            wsd = sb("wsd", [P, SB, D])
            sil = sb("sil", [P, 2, S])
            acts = sb("acts", [P, 2, S])
            st6 = sb("st6", [P, W, 6])
            mv = sb("mv", [P, W, 2])
            var = sb("var", [P, 2, W])
            yv = sb("yv", [P, 2, W])
            t1 = sb("t1", [P, 2, W])
            rstd = sb("rstd", [P, W])
            r12 = sb("r12", [P, 2, W])
            lgs = sb("lgs", [P, W, E])
            sct = sb("sct", [P, W])
            mx8 = sb("mx8", [P, W, 8])
            ix8 = sb("ix8", [P, W, 8], U32)
            ixf = sb("ixf", [P, 2, W])
            oh = sb("oh", [P, 2, W, E])
            msk = sb("msk", [P, W, E], BF16)
            carry = sb("carry", [P, E])
            tsum = sb("tsum", [P, E])
            pos = sb("pos", [P, W, E])
            ohp = sb("ohp", [P, 2, W, E])
            posk = sb("posk", [P, 2, W])
            valid = sb("valid", [P, 2, W])
            dest = sb("dest", [P, 2, W])
            dest_st = sb("dest_st", [P, 2, W], U32)

            gate, up, down, tx, lg = bank[0:2], bank[2:4], bank[4], bank[5:7], bank[7]
            lgv = lg[:, 0:W * 16].rearrange("p (w e) -> p w e", e=16)
            pref = lg[:, 128:128 + W * E].rearrange("p (w e) -> p w e", e=E)
            tot = lg[:, 256:256 + W * E].rearrange("p (w e) -> p w e", e=E)

            x_loaded = sem("x_loaded")
            wffn_loaded, small_loaded = sem("wffn_loaded"), sem("small_loaded")
            var_ready, pow_ready = sem("var_ready"), sem("pow_ready")
            xn_ready, h_ready, xn_saved = sem("xn_ready"), sem("h_ready"), sem("xn_saved")
            tx_done, th_done, lg_done, pref_done = sem("tx_done"), sem("th_done"), sem("lg_done"), sem("pref_done")
            ws_high, ws_low, xnT_high, xnT_low = sem("ws_high"), sem("ws_low"), sem("xnT_high"), sem("xnT_low")
            xnT_ready, hT_saved, lg_read = sem("xnT_ready"), sem("hT_saved"), sem("lg_read")
            mask_ready, pref_read, dest_ready = sem("mask_ready"), sem("pref_read"), sem("dest_ready")
            dest_saved, xsc_ready, xg_zeroed = sem("dest_saved"), sem("xsc_ready"), sem("xg_zeroed")
            gu_done, silu_done, act_ready = sem("gu_done"), sem("silu_done"), sem("act_ready")
            dn_done, ffn_saved = sem("dn_done"), sem("ffn_saved")
            lnc, rtc, pc = sem("lnc"), sem("rtc"), sem("pc")

            block = s1.enter_context(nc.Block())

            @block.sync
            def _(sp):
                sp.dma_start(x_st[:], x_rows[0]).then_inc(x_loaded, DMA)
                sp.dma_start(rs9[:, 0:E], router_wT).then_inc(small_loaded, DMA)
                sp.dma_start(rs9[:, E:E + 1], scorer_w).then_inc(small_loaded, DMA)
                sp.dma_start(normw[:], norm_w.rearrange("(d a) -> d a", a=1)).then_inc(small_loaded, DMA)
                sp.dma_start(bias_s[:], scorer_b.rearrange("(a b) -> a b", a=1).to_broadcast([P, 1]))\
                    .then_inc(small_loaded, DMA)
                sp.dma_start(wsg[:], sg).then_inc(wffn_loaded, DMA)
                sp.dma_start(wsu[:], su).then_inc(wffn_loaded, DMA)
                sp.dma_start(wsd[:], sd.rearrange("(j p) d -> p j d", p=P)).then_inc(wffn_loaded, DMA)
                sp.wait_ge(consts, 1)
                sp.dma_start(xg_dram[0:SLOTS, :].rearrange("(t p) d -> p t d", p=P),
                             zeros[:].unsqueeze(1).to_broadcast([P, SLOTS // P, D])).then_inc(xg_zeroed, DMA)
                with sp.Fori(1, B) as b:
                    sp.wait_ge(xn_ready, b * 1)
                    sp.dma_start(x_st[:], x_rows[b]).then_inc(x_loaded, DMA)
                load_expert(sp, 0, 0)
                load_expert(sp, 1, 1)
                for w_sb, w_dram in ((wq, w_q), (wk, w_k), (wv, w_v)):
                    sp.dma_start(w_sb[:], w_dram).then_inc(wattn_loaded, DMA)
                for c in range(HG):
                    for f in range(2):
                        src = w_out.rearrange("(g j f q) d -> j f q g d", j=HG, f=2, q=32)[HOME[c], f]
                        sp.dma_start(wo[32 * c:32 * c + 32, :, f, :], src).then_inc(wout_loaded, DMA)

            @block.gpsimd
            def _(pool):
                n = [0]

                def link(i):
                    n[0] += 1
                    i.then_inc(pc, 1)
                    pool.wait_ge(pc, n[0])

                link(pool.memset(zeros[:], 0.0))
                pool.memset(pow_m[:], -0.5).then_inc(consts, 1)
                for k in range(2):
                    pool.dma_start(eo_dram[SLOTS + k * W * P:SLOTS + (k + 1) * W * P, :]
                                   .rearrange("(t p) d -> p t d", p=P),
                                   zeros[:].unsqueeze(1).to_broadcast([P, W, D])).then_inc(eo_stored[k], DMA)
                link(pool.affine_select(out=ident[:], in_=zeros[:], compare_op=ALU.not_equal, fill=1.0,
                                        base=0, pattern=[[-1, P]], channel_multiplier=1))
                link(pool.memset(ones_bf[:], 1.0))
                link(pool.affine_select(out=before[:], in_=ones_bf[:], compare_op=ALU.is_gt, fill=0.0,
                                        base=0, pattern=[[1, P]], channel_multiplier=-1))
                link(pool.iota(iota_e[:], pattern=[[1, E]], base=0, channel_multiplier=0,
                               allow_small_or_imprecise_dtypes=True))
                link(pool.iota(iota_g[:], pattern=[[1, NG]], base=1, channel_multiplier=0,
                               allow_small_or_imprecise_dtypes=True))
                link(pool.iota(trash[:], pattern=[[W * P, 2], [P, W]], base=SLOTS, channel_multiplier=1,
                               allow_small_or_imprecise_dtypes=True))
                link(pool.memset(own[:], 1.0))
                link(pool.affine_select(out=own[:], in_=own[:], compare_op=ALU.is_ge, fill=0.0,
                                        base=0, pattern=[[-32, HG], [0, 32]], channel_multiplier=1))
                link(pool.affine_select(out=own[:], in_=own[:], compare_op=ALU.is_ge, fill=0.0,
                                        base=31, pattern=[[32, HG], [0, 32]], channel_multiplier=-1))
                link(pool.memset(onesr[:], 1.0))
                link(pool.memset(maskb[:], 0.0))
                pool.affine_select(out=maskb[:, :, 0:P], in_=maskb[:, :, 0:P], compare_op=ALU.is_ge,
                                   fill=NEG, base=0, pattern=[[0, W], [-1, P]], channel_multiplier=1)\
                    .then_inc(consts, 1)

                def norm_help(b):
                    pool.wait_ge(var_ready, b * 2 + 1)
                    pool.tensor_tensor(yv[:, 0, :], var[:, 0, :], pow_m[:, 0:W], ALU.pow).then_inc(pow_ready, 1)
                    pool.wait_ge(var_ready, b * 2 + 2)
                    pool.tensor_tensor(yv[:].rearrange("p a w -> p (a w)"), var[:].rearrange("p a w -> p (a w)"),
                                       pow_m[:], ALU.pow).then_inc(pow_ready, 1)
                    pool.wait_ge(xn_ready, b * 1 + 1)
                    wait(pool, th_done, b * 1)
                    pool.tensor_tensor(h_st[:], xn_st[:], r12[:, 0, :].unsqueeze(2).to_broadcast([P, W, D]),
                                       ALU.mult).then_inc(h_ready, 1)
                    pool.tensor_copy(r1_all[:, b, :], r12[:, 0, :])
                    pool.tensor_copy(xn_all[:, b, :, :], xn_st[:]).then_inc(xn_saved, 1)

                def scatter(b):
                    wait(pool, scattered, b * (2 * W * DMA))
                    pool.wait_ge(xn_saved, b * 1 + 1)
                    pool.tensor_copy(xn_sc[:], xn_all[:, b, :, :]).then_inc(xsc_ready, 1)
                    pool.wait_ge(dest_ready, b * 1 + 1)
                    pool.tensor_copy(dest_all[:, b, :, :], dest_st[:]).then_inc(dest_saved, 1)
                    pool.wait_ge(xsc_ready, b * 1 + 1)
                    settle(pool)
                    for w in range(W):
                        for k in range(2):
                            pool.indirect_dma_start(
                                out=xg_dram, out_offset=bass.IndirectOffsetOnAxis(ap=dest_st[:, k, w:w + 1], axis=0),
                                in_=xn_sc[:, w, :], in_offset=None).then_inc(scattered, DMA)

                def body(b, last=False):
                    if not last:
                        norm_help(b + 1)
                    scatter(b)

                norm_help(0)
                pool.wait_ge(xg_zeroed, DMA)
                body(0)
                with pool.Fori(1, B - 1) as b:
                    body(b)
                body(B - 1, last=True)

            @block.vector
            def _(dve):
                ln = Chain(dve, lnc, 13)
                rt = Chain(dve, rtc, 11)

                def root(v, y, t):
                    ln.link(dve.tensor_tensor(t, y, y, ALU.mult))
                    ln.link(dve.tensor_tensor(t, t, v, ALU.mult))
                    ln.link(dve.tensor_scalar(t, t, -0.5, 1.5, ALU.mult, ALU.add))

                def ln_a(b):
                    ln.round(b)
                    dve.wait_ge(x_loaded, b * DMA + DMA)
                    for w in range(W):
                        i = dve.bn_stats(st6[:, w, :], x_st[:, w, :])
                    ln.link(i)
                    settle(dve)
                    for w in range(W):
                        i = dve.bn_aggr(mv[:, w, :], st6[:, w, :])
                    ln.link(i)
                    dve.tensor_scalar(var[:, 0, :], mv[:, :, 1], EPS_LN, None, ALU.add).then_inc(var_ready, 1)

                def ln_b(b):
                    dve.wait_ge(pow_ready, b * 2 + 1)
                    dve.wait_ge(var_ready, b * 2 + 1)
                    root(var[:, 0, :], yv[:, 0, :], t1[:, 0, :])
                    ln.link(dve.tensor_tensor(rstd[:], yv[:, 0, :], t1[:, 0, :], ALU.mult))
                    ln.link(dve.tensor_tensor(t1[:, 1, :], rstd[:], rstd[:], ALU.mult))
                    ln.link(dve.tensor_tensor(t1[:, 1, :], t1[:, 1, :], mv[:, :, 1], ALU.mult))
                    ln.link(dve.tensor_scalar(var[:, 0, :], t1[:, 1, :], EPS_ATT, None, ALU.add))
                    dve.tensor_scalar(var[:, 1, :], t1[:, 1, :], EPS_FFN, None, ALU.add).then_inc(var_ready, 1)

                def ln_c(b):
                    dve.wait_ge(pow_ready, b * 2 + 2)
                    dve.wait_ge(var_ready, b * 2 + 2)
                    root(var[:], yv[:], t1[:])
                    wait(dve, xn_saved, b * 1)
                    ln.link(dve.tensor_tensor(r12[:], yv[:], t1[:], ALU.mult))
                    ln.done()

                def ln_d(b):
                    wait(dve, tx_done, b * 1)
                    for w in range(W):
                        i = dve.tensor_scalar(xn_st[:, w, :], x_st[:, w, :], mv[:, w, 0:1], rstd[:, w:w + 1],
                                              ALU.subtract, ALU.mult)
                    i.then_inc(xn_ready, 1)

                def route_a(b):
                    rt.round(b)
                    dve.wait_ge(lg_done, b * 1 + 1)
                    dve.tensor_tensor(lgs[:], lgv[:, :, 0:E], r12[:, 1, :].unsqueeze(2).to_broadcast([P, W, E]),
                                      ALU.mult)
                    rt.link(dve.tensor_tensor(sct[:], lgv[:, :, E], r12[:, 0, :], ALU.mult))
                    dve.tensor_scalar(score_all[:, b, :], sct[:], bias_s[:, 0:1], None, ALU.add)
                    for w in range(W):
                        i = dve.max(mx8[:, w, :], lgs[:, w, :])
                    rt.link(i)
                    settle(dve)
                    for w in range(W):
                        i = dve.max_index(ix8[:, w, :], mx8[:, w, :], lgs[:, w, :])
                    rt.link(i)
                    dve.tensor_tensor(dlog_all[:, b, :], mx8[:, :, 1], mx8[:, :, 0], ALU.subtract)
                    rt.link(dve.tensor_copy(ixf[:], ix8[:, :, 0:2].rearrange("p w k -> p k w")))
                    for k in range(2):
                        i = dve.tensor_tensor(oh[:, k, :, :], iota_e[:].unsqueeze(1).to_broadcast([P, W, E]),
                                              ixf[:, k, :].unsqueeze(2).to_broadcast([P, W, E]), ALU.is_equal)
                    rt.link(i)
                    dve.tensor_tensor(msk[:], oh[:, 0, :, :], oh[:, 1, :, :], ALU.add).then_inc(mask_ready, 1)

                def route_b(b):
                    dve.wait_ge(pref_done, b * 1 + 1)
                    dve.tensor_tensor(pos[:], pref, carry[:].unsqueeze(1).to_broadcast([P, W, E]), ALU.add)
                    rt.link(dve.tensor_reduce(tsum[:], tot.rearrange("p w e -> p e w"), AX.X, ALU.add))
                    dve.tensor_tensor(carry[:], carry[:], tsum[:], ALU.add).then_inc(pref_read, 1)
                    dve.wait_ge(pref_read, b * 1 + 1)
                    for k in range(2):
                        i = dve.tensor_tensor(ohp[:, k, :, :], oh[:, k, :, :], pos[:], ALU.mult)
                    rt.link(i)
                    rt.link(dve.tensor_reduce(posk[:], ohp[:], AX.X, ALU.add))
                    dve.tensor_scalar(valid[:], posk[:], float(CAP), None, ALU.is_lt)
                    rt.link(dve.scalar_tensor_tensor(dest[:], ixf[:], float(CAP), posk[:], ALU.mult, ALU.add))
                    dve.tensor_copy(valid_all[:, b, :, :], valid[:])
                    rt.link(dve.tensor_tensor(dest[:], dest[:], trash[:], ALU.subtract))
                    rt.link(dve.tensor_tensor(dest[:], dest[:], valid[:], ALU.mult))
                    wait(dve, scattered, b * (2 * W * DMA))
                    wait(dve, dest_saved, b * 1)
                    dve.tensor_tensor(dest_st[:], dest[:], trash[:], ALU.add).then_inc(dest_ready, 1)
                    rt.done()

                def silu_up(b, j):
                    n = b * SB + j
                    dve.wait_ge(silu_done, n + 1)
                    wait(dve, dn_done, n - 1)
                    dve.tensor_tensor(acts[:, j % 2, :], sil[:, j % 2, :], up[j % 2][:], ALU.mult)\
                        .then_inc(act_ready, 1)

                def low_parts(f):
                    dve.wait_ge(ws_high, 2)
                    cols = slice(f * FS // 2, (f + 1) * FS // 2)
                    dve.tensor_tensor(wsg2[:, 1, cols], wsg[:, cols], wsg2[:, 0, cols], ALU.subtract)
                    dve.tensor_tensor(wsu2[:, 1, cols], wsu[:, cols], wsu2[:, 0, cols], ALU.subtract).then_inc(ws_low, 1)

                def body(b, first=False, last=False):
                    dve.wait_ge(xnT_ready, b * 1 + 1)
                    dve.wait_ge(xnT_high, b * 1 + 1)
                    dve.tensor_tensor(xnT2[:, 1, :], xnT[:], xnT2[:, 0, :], ALU.subtract).then_inc(xnT_low, 1)
                    dve.wait_ge(th_done, b * 1 + 1)
                    dve.tensor_scalar(hT_all[:, b, :], tx[1][:], normw[:, 0:1], None, ALU.mult).then_inc(hT_saved, 1)
                    route_a(b)
                    more = [] if last else [ln_a, ln_b, ln_c, ln_d]
                    for j in range(SB):
                        silu_up(b, j)
                        if first and j == 0:
                            low_parts(1)
                        if 1 <= j <= len(more):
                            more[j - 1](b + 1)
                        if j == (3 if last else 5):
                            route_b(b)

                dve.memset(carry[:], 0.0)
                for part in (ln_a, ln_b, ln_c):
                    part(0)
                ln_d(0)
                dve.wait_ge(small_loaded, 4 * DMA)
                dve.tensor_tensor(rs9[:, E:E + 1], rs9[:, E:E + 1], normw[:], ALU.mult).then_inc(consts, 1)
                dve.wait_ge(consts, 3)
                low_parts(0)
                body(0, first=True)
                with dve.Fori(1, B - 1) as b:
                    body(b)
                body(B - 1, last=True)
                for i in range(2):
                    dve.wait_ge(we_high, i + 1)
                    dve.tensor_tensor(wge2[i][:, 1, :], wge[i][:], wge2[i][:, 0, :], ALU.subtract)
                    dve.tensor_tensor(wue2[i][:, 1, :], wue[i][:], wue2[i][:, 0, :], ALU.subtract).then_inc(we_low, 1)

            @block.scalar
            def _(act):
                def save_shared(b):
                    act.wait_ge(dn_done, b * SB + SB)
                    act.activation(ffn_all[:, b, :, :].rearrange("p w d -> p (w d)"), down[:], ACT.Copy)\
                        .then_inc(ffn_saved, 1)

                def body(b, first=False):
                    act.wait_ge(tx_done, b * 1 + 1)
                    wait(act, gu_done, b * SB)
                    act.activation(xnT[:], tx[0][:], ACT.Copy).then_inc(xnT_ready, 1)
                    act.activation(xnT2[:, 0, :], tx[0][:], ACT.Copy).then_inc(xnT_high, 1)
                    if not first:
                        save_shared(b - 1)
                    for j in range(SB):
                        n = b * SB + j
                        act.wait_ge(gu_done, n + 1)
                        wait(act, act_ready, n - 1)
                        act.activation(sil[:, j % 2, :], gate[j % 2][:], ACT.Silu).then_inc(silu_done, 1)

                act.wait_ge(wffn_loaded, 3 * DMA)
                for w2, w_sb in ((wsg2, wsg), (wsu2, wsu)):
                    act.activation(w2[:, 0, :], w_sb[:], ACT.Copy).then_inc(ws_high, 1)
                body(0, first=True)
                with act.Fori(1, B) as b:
                    body(b)
                act.wait_ge(we_loaded, 4 * DMA)
                for i in range(2):
                    act.activation(wge2[i][:, 0, :], wge[i][:], ACT.Copy)
                    act.activation(wue2[i][:, 0, :], wue[i][:], ACT.Copy).then_inc(we_high, 1)
                save_shared(B - 1)

            @block.tensor
            def _(pe):
                def up_gate(b, j):
                    n = b * SB + j
                    wait(pe, silu_done, n - 1)
                    x2 = [xnT2[:, k, :] for k in range(2)]
                    product(pe, gate[j % 2][:], [wsg2[:, k, j * P:(j + 1) * P] for k in range(2)], x2)
                    wait(pe, act_ready, n - 1)
                    product(pe, up[j % 2][:], [wsu2[:, k, j * P:(j + 1) * P] for k in range(2)], x2).then_inc(gu_done, 1)

                def down_part(b, j):
                    pe.wait_ge(act_ready, b * SB + j + 1)
                    if j == 0:
                        wait(pe, ffn_saved, b * 1)
                    for w in range(W):
                        i = pe.matmul(down[:, w * D:(w + 1) * D], acts[:, j % 2, w * P:(w + 1) * P], wsd[:, j, :],
                                      start=(j == 0 and w == 0), stop=(j == SB - 1), skip_group_check=True)
                    i.then_inc(dn_done, 1)

                def body(b, first=False, last=False):
                    pe.wait_ge(xn_ready, b * 1 + 1)
                    wait(pe, xnT_ready, b * 1)
                    for w in range(W):
                        i = pe.transpose(tx[0][:, w * P:(w + 1) * P], xn_st[:, w, :], ident[:])
                    i.then_inc(tx_done, 1)
                    if not first:
                        down_part(b - 1, SB - 1)
                    pe.wait_ge(h_ready, b * 1 + 1)
                    wait(pe, hT_saved, b * 1)
                    for w in range(W):
                        i = pe.transpose(tx[1][:, w * P:(w + 1) * P], h_st[:, w, :], ident[:])
                    i.then_inc(th_done, 1)
                    pe.wait_ge(xnT_ready, b * 1 + 1)
                    wait(pe, pref_read, b * 1)
                    for w in range(W):
                        i = pe.matmul(lgv[:, w, 0:E + 1], xnT[:, w * P:(w + 1) * P], rs9[:], start=True, stop=True)
                    i.then_inc(lg_done, 1)
                    pe.wait_ge(xnT_low, b * 1 + 1)
                    for j in range(SB):
                        if first and j % (SB // 2) == 0:
                            pe.wait_ge(ws_low, 2 * j // SB + 1)
                        up_gate(b, j)
                        if j >= 1:
                            down_part(b, j - 1)
                        if j == (2 if last else 3):
                            pe.wait_ge(mask_ready, b * 1 + 1)
                            pe.matmul(pref, before[:], msk[:], start=True, stop=False, skip_group_check=True)
                            for d in range(1, W):
                                pe.matmul(pref[:, d:W, :], ones_bf[:], msk[:, 0:W - d, :], start=False,
                                          stop=(d == W - 1), skip_group_check=True)
                            pe.matmul(tot, ones_bf[:], msk[:], start=True, stop=True).then_inc(pref_done, 1)

                pe.wait_ge(consts, 3)
                body(0, first=True)
                with pe.Fori(1, B - 1) as b:
                    body(b)
                body(B - 1, last=True)
                down_part(B - 1, SB - 1)

        def stage2(s2):
            def sb(name, shape, dt=F32):
                return s2.enter_context(nc.sbuf_tensor(name, shape, dt))

            def sem(name):
                return s2.enter_context(nc.semaphore(name))

            xgr = [sb(f"xgr{i}", [P, CT, D]) for i in range(2)]
            xgT2 = [sb(f"xgT2{i}", [D, 2, CAP], F32R) for i in range(2)]
            acte = [sb(f"acte{i}", [P, RB, CAP]) for i in range(2)]
            sile = sb("sile", [P, 2, HALF])
            eo = [sb(f"eo{i}", [P, CT, D]) for i in range(2)]
            sc8 = sb("sc8", [B, S])
            wk8 = [sb(f"wk8{i}", [B, S]) for i in range(2)]
            top = sb("top", [B, 8])
            sel8 = sb("sel8", [B, 2, S])
            selc = sb("selc", [P, 2, W, B])
            selr = sb("selr", [P, B, W])
            eqg = gm_all
            seln = sb("seln", [P, B, W, NG])
            hgr = sb("hgr", [P, 2, D])
            gate, up, tb, dn = bank[0:2], bank[2:4], bank[4:6], bank[6:8]
            STEPS = 2 * RB
            assert E - 4 == NG // 8

            wgu_loaded = [sem(f"wgu_loaded{i}") for i in range(2)]
            xgT_high = sem("xgT_high")
            xgr_loaded = [sem(f"xgr_loaded{i}") for i in range(2)]
            xt_done, xgT_ready, egu_done, esilu_done = sem("xt_done"), sem("xgT_ready"), sem("egu_done"), sem("esilu_done")
            eact_ready, edn_done, eo_saved = sem("eact_ready"), sem("edn_done"), sem("eo_saved")
            sc_done, sc_read, sel_ready, selc_done = sem("sc_done"), sem("sc_read"), sem("sel_ready"), sem("selc_done")
            top_ready, rest_ready, selc_ready, eqg_ready = (sem(n) for n in
                ("top_ready", "rest_ready", "selc_ready", "eqg_ready"))
            seln_ready, hgr_done, hgr_ready, hgT_done = (sem(n) for n in ("seln_ready", "hgr_done", "hgr_ready", "hgT_done"))
            hgT_ready, kg_done, kg_saved, gm_ready = (sem(n) for n in ("hgT_ready", "kg_done", "kg_saved", "gm_ready"))

            block = s2.enter_context(nc.Block())

            @block.sync
            def _(sp):
                def rows(e, i):
                    sp.dma_start(xgr[i][:], xg_dram[bass.ds(e * CAP, CAP), :].rearrange("(s p) d -> p s d", p=P))\
                        .then_inc(xgr_loaded[i], DMA)

                sp.wait_ge(scattered, B * 2 * W * DMA)
                rows(0, 0)
                rows(1, 1)
                with sp.Fori(1, E // 2) as r:
                    for i in range(2):
                        e = r * 2 + i
                        sp.wait_ge(xt_done, e - 1)
                        rows(e, i)
                        sp.wait_ge(we_low, e)
                        sp.dma_start(wge[i][:], rg[bass.ds(e, 1)].rearrange("a d f -> d (a f)")).then_inc(wgu_loaded[i], DMA)
                        sp.dma_start(wue[i][:], ru[bass.ds(e, 1)].rearrange("a d f -> d (a f)")).then_inc(wgu_loaded[i], DMA)
                        sp.wait_ge(edn_done, e - 1)
                        sp.dma_start(wde[i][:], rd[bass.ds(e, 1)].rearrange("a (j p) d -> p (a j) d", p=P))\
                            .then_inc(wd_loaded[i], DMA)

            @block.gpsimd
            def _(pool):
                def split_attention(k):
                    w_sb, w2 = ((wq, wq2), (wk, wk2), (wv, wv2))[k]
                    pool.tensor_copy(w2[:, 0, :], w_sb[:]).then_inc(wsplit, 1)
                    pool.wait_ge(wsplit, 2 * k + 1)
                    pool.tensor_tensor(w2[:, 1, :], w_sb[:], w2[:, 0, :], ALU.subtract).then_inc(wsplit, 1)

                def split_expert(r, i):
                    e = r * 2 + i
                    pool.wait_ge(wgu_loaded[i], r * 2 * DMA)
                    pool.wait_ge(egu_done, (e - 1) * STEPS)
                    settle(pool)
                    pool.tensor_copy(wge2[i][:, 0, :], wge[i][:])
                    pool.tensor_copy(wue2[i][:, 0, :], wue[i][:]).then_inc(we_high, 1)
                    pool.wait_ge(we_high, e + 1)
                    pool.tensor_tensor(wge2[i][:, 1, :], wge[i][:], wge2[i][:, 0, :], ALU.subtract)
                    pool.tensor_tensor(wue2[i][:, 1, :], wue[i][:], wue2[i][:, 0, :], ALU.subtract).then_inc(we_low, 1)

                def store(r, i):
                    e = r * 2 + i
                    pool.wait_ge(eo_saved, e + 1)
                    pool.dma_start(eo_dram[bass.ds(e * CAP, CAP), :].rearrange("(s p) d -> p s d", p=P), eo[i][:])\
                        .then_inc(eo_stored[i], DMA)

                pool.wait_ge(wattn_loaded, 3 * DMA)
                split_attention(0)
                split_attention(1)
                with pool.Fori(0, E // 2 - 1) as r:
                    for i in range(2):
                        split_expert(r + 1, i)
                        store(r, i)
                split_attention(2)
                for i in range(2):
                    store(E // 2 - 1, i)
                for i in range(2):
                    pool.wait_ge(eo_stored[i], (E // 2 + 1) * DMA)

            @block.scalar
            def _(act):
                def save(e, i, r):
                    act.wait_ge(edn_done, e + 1)
                    act.wait_ge(eo_stored[i], r * DMA + DMA)
                    act.activation(eo[i][:, 0:4, :].rearrange("p s d -> p (s d)"), dn[0][:], ACT.Copy)
                    act.activation(eo[i][:, 4, :], dn[1][:, 0:D], ACT.Copy).then_inc(eo_saved, 1)

                def save_keys(m):
                    act.wait_ge(kg_done, m + 1)
                    act.activation(kg_all[:, 2 * m:2 * m + 2, :, :].rearrange("p m b s -> p (m b s)"), tb[m % 2][:],
                                   ACT.Copy).then_inc(kg_saved, 1)

                def body(r, first=False, last=False):
                    for i in range(2):
                        e = r * 2 + i
                        for s in range(STEPS):
                            n = e * STEPS + s
                            act.wait_ge(egu_done, n + 1)
                            wait(act, eact_ready, n - 1)
                            act.activation(sile[:, s % 2, :], gate[s % 2][:, 0:HALF], ACT.Silu).then_inc(esilu_done, 1)
                            if s == 1 and not (first and i == 0):
                                save(e - 1, 1 - i, r - 1 + i)
                            if last and i == 1 and s == 6:
                                save_keys(0)
                                save_keys(1)

                body(0, first=True)
                with act.Fori(1, E // 2 - 1) as r:
                    body(r)
                body(E // 2 - 1, last=True)
                save_keys(2)
                save_keys(3)
                save(E - 1, 1, E // 2 - 1)

            @block.vector
            def _(dve):
                def turned_high(e, i):
                    dve.wait_ge(xt_done, e + 1)
                    dve.tensor_copy(xgT2[i][:, 0, 0:512], tb[0][:])
                    dve.tensor_copy(xgT2[i][:, 0, 512:CAP], tb[1][:, 0:CAP - 512]).then_inc(xgT_high, 1)

                def turned_low(e, i):
                    dve.wait_ge(xgT_high, e + 1)
                    dve.tensor_tensor(xgT2[i][:, 1, 0:512], tb[0][:], xgT2[i][:, 0, 0:512], ALU.subtract)
                    dve.tensor_tensor(xgT2[i][:, 1, 512:CAP], tb[1][:, 0:CAP - 512], xgT2[i][:, 0, 512:CAP],
                                      ALU.subtract).then_inc(xgT_ready, 1)

                BH = B // 2
                cum = selc[:, 1, :, :].rearrange("p w b -> p b w").unsqueeze(3).to_broadcast([P, B, W, NG])
                place = iota_g[:].unsqueeze(1).unsqueeze(1).to_broadcast([P, BH, W, NG])

                def half(a, f):
                    return a[:, f * BH:(f + 1) * BH]

                def take_scores():
                    dve.wait_ge(sc_done, 1)
                    dve.tensor_copy(wk8[0][:], tb[0][0:B, :]).then_inc(rest_ready, 1)
                    dve.tensor_copy(sc8[:], tb[0][0:B, :]).then_inc(sc_read, 1)

                def greatest(r, i):
                    n = r * 2 + i - 2
                    dve.wait_ge(rest_ready, n + 1)
                    settle(dve)
                    dve.max(top[:], wk8[i][:]).then_inc(top_ready, 1)

                def strike(r, i):
                    n = r * 2 + i - 2
                    dve.wait_ge(top_ready, n + 1)
                    settle(dve)
                    dve.match_replace(wk8[1 - i][:], top[:], wk8[i][:], -BIG).then_inc(rest_ready, 1)

                def chosen():
                    dve.wait_ge(sc_read, 1)
                    dve.wait_ge(rest_ready, NG // 8 + 1)
                    dve.tensor_tensor(sel8[:, 0, :], sc8[:], wk8[0][:], ALU.not_equal).then_inc(sel_ready, 1)

                def counted():
                    dve.wait_ge(sel_ready, 1)
                    dve.tensor_tensor_scan(sel8[:, 1, :], onesr[:], sel8[:, 0, :], 0.0, ALU.mult, ALU.add)\
                        .then_inc(sel_ready, 1)

                def as_columns():
                    dve.wait_ge(selc_done, 1)
                    dve.tensor_copy(selc[:].rearrange("p a w b -> p (a w b)"), tb[0][:, 0:2 * W * B])\
                        .then_inc(selc_ready, 1)
                    dve.wait_ge(selc_ready, 1)
                    dve.tensor_tensor(selr[:], selc[:, 0, :, :].rearrange("p w b -> p b w"), r1_all[:], ALU.mult)

                def one_hot(f):
                    dve.tensor_tensor(half(eqg, f), place, half(cum, f), ALU.is_equal).then_inc(eqg_ready, 1)

                def one_hot_scaled(f):
                    dve.wait_ge(eqg_ready, 2)
                    dve.tensor_tensor(half(seln, f), half(eqg, f),
                                      half(selr, f).unsqueeze(3).to_broadcast([P, BH, W, NG]), ALU.mult)\
                        .then_inc(seln_ready, 1)

                def take_rows():
                    dve.wait_ge(hgr_done, 1)
                    dve.tensor_copy(hgr[:].rearrange("p f d -> p (f d)"), tb[1][:, 0:2 * D]).then_inc(hgr_ready, 1)

                def take_columns():
                    dve.wait_ge(hgT_done, 1)
                    dve.tensor_scalar(hgT[:], tb[0][:, 0:2 * P], normw[:, 0:1], None, ALU.mult).then_inc(hgT_ready, 1)

                def global_mask(f):
                    dve.tensor_tensor(half(gm_all, f), place, half(cum, f), ALU.is_gt).then_inc(gm_ready, 1)
                    dve.wait_ge(gm_ready, f * 2 + 1)
                    dve.tensor_scalar(half(gm_all, f), half(gm_all, f), NEG, None, ALU.mult).then_inc(gm_ready, 1)

                beside = {(0, 0, 3): [take_scores],
                          (E // 2 - 1, 0, 1): [chosen], (E // 2 - 1, 0, 2): [counted],
                          (E // 2 - 1, 0, 4): [as_columns],
                          (E // 2 - 1, 0, 5): [lambda: one_hot(0)], (E // 2 - 1, 0, 6): [lambda: one_hot(1)],
                          (E // 2 - 1, 0, 7): [lambda: one_hot_scaled(0)], (E // 2 - 1, 1, 0): [lambda: one_hot_scaled(1)],
                          (E // 2 - 1, 1, 2): [take_rows], (E // 2 - 1, 1, 4): [take_columns]}

                def body(r, last=False):
                    for i in range(2):
                        e = r * 2 + i
                        for s in range(STEPS):
                            n = e * STEPS + s
                            j, h = s // 2, s % 2
                            dve.wait_ge(esilu_done, n + 1)
                            if s == 0:
                                wait(dve, edn_done, e - 1)
                            dve.tensor_tensor(acte[i][:, j, h * HALF:(h + 1) * HALF], sile[:, h, :], up[h][:, 0:HALF],
                                              ALU.mult).then_inc(eact_ready, 1)
                            if s == 0 and not (last and i == 1):
                                turned_high(e + 1, 1 - i)
                            if s == 1 and not (last and i == 1):
                                turned_low(e + 1, 1 - i)
                            if isinstance(r, int):
                                for work in beside.get((r, i, s), []):
                                    work()
                            elif s == 3:
                                greatest(r, i)
                            elif s == 5:
                                strike(r, i)

                turned_high(0, 0)
                turned_low(0, 0)
                body(0)
                with dve.Fori(1, E // 2 - 1) as r:
                    body(r)
                body(E // 2 - 1, last=True)
                for f in range(2):
                    global_mask(f)
                dve.wait_ge(gm_ready, 2)
                dve.tensor_copy(maskb[:, :, P:KEYS], gm_all[:, 0, :, :])

            @block.tensor
            def _(pe):
                def turn_scores():
                    pe.wait_ge(xgT_ready, 2)
                    for w in range(W):
                        t = pe.transpose(tb[0][0:B, w * P:(w + 1) * P], score_all[:, :, w], ident[:])
                    t.then_inc(sc_done, 1)

                def turn_chosen():
                    pe.wait_ge(xgT_ready, E)
                    pe.wait_ge(sel_ready, 2)
                    for a in range(2):
                        for w in range(W):
                            o = (a * W + w) * B
                            t = pe.transpose(tb[0][:, o:o + B], sel8[:, a, w * P:(w + 1) * P], ident[0:B, 0:B])
                    t.then_inc(selc_done, 1)

                def pick_rows():
                    pe.wait_ge(seln_ready, 2)
                    for f in range(2):
                        for w in range(W):
                            for c in range(4):
                                t = pe.matmul(tb[1][32 * c:32 * c + 32, f * D:(f + 1) * D],
                                              seln[:, 4 * f + c, w, :], xn_all[:, 4 * f + c, w, :],
                                              start=(w == 0), stop=(w == W - 1), skip_group_check=True)
                    t.then_inc(hgr_done, 1)

                def turn_rows():
                    pe.wait_ge(hgr_ready, 1)
                    for f in range(2):
                        t = pe.transpose(tb[0][:, f * P:(f + 1) * P], hgr[:, f, :], ident[:])
                    t.then_inc(hgT_done, 1)

                def global_keys(m):
                    if m == 0:
                        pe.wait_ge(hgT_ready, 1)
                        pe.wait_ge(wattn_loaded, 3 * DMA)
                    wait(pe, kg_saved, m - 1)
                    for k in range(2):
                        blk = 2 * m + k
                        t = pe.matmul(tb[m % 2][:, k * B * NG:(k + 1) * B * NG], wk[:, blk * P:(blk + 1) * P], hgT[:],
                                      start=True, stop=True)
                    t.then_inc(kg_done, 1)

                beside = {(0, 0, 2): turn_scores, (E // 2 - 1, 0, 4): turn_chosen,
                          (E // 2 - 1, 1, 1): pick_rows, (E // 2 - 1, 1, 3): turn_rows,
                          (E // 2 - 1, 1, 5): lambda: global_keys(0), (E // 2 - 1, 1, 6): lambda: global_keys(1)}

                def turn(e, i, r):
                    if isinstance(e, int) and e == 2:
                        pe.wait_ge(sc_read, 1)
                    pe.wait_ge(xgr_loaded[i], r * DMA + DMA)
                    wait(pe, xgT_ready, e)
                    for s in range(CT):
                        t = pe.transpose(tb[s // 4][:, (s % 4) * P:(s % 4 + 1) * P], xgr[i][:, s, :], ident[:])
                    t.then_inc(xt_done, 1)

                def up_gate(e, i, s):
                    n = e * STEPS + s
                    j, h = s // 2, s % 2
                    wait(pe, esilu_done, n - 1)
                    x2 = [xgT2[i][:, k, h * HALF:(h + 1) * HALF] for k in range(2)]
                    product(pe, gate[h][:, 0:HALF], [wge2[i][:, k, j * P:(j + 1) * P] for k in range(2)], x2)
                    wait(pe, eact_ready, n - 1)
                    product(pe, up[h][:, 0:HALF], [wue2[i][:, k, j * P:(j + 1) * P] for k in range(2)], x2)\
                        .then_inc(egu_done, 1)

                def down(e, i, r):
                    pe.wait_ge(wd_loaded[i], r * DMA + DMA)
                    pe.wait_ge(eact_ready, e * STEPS + STEPS)
                    wait(pe, eo_saved, e)
                    for s in range(CT):
                        for j in range(RB):
                            d = pe.matmul(dn[s // 4][:, (s % 4) * D:(s % 4 + 1) * D], acte[i][:, j, s * P:(s + 1) * P],
                                          wde[i][:, j, :], start=(j == 0), stop=(j == RB - 1))
                    d.then_inc(edn_done, 1)

                def body(r, first=False, last=False):
                    for i in range(2):
                        e = r * 2 + i
                        pe.wait_ge(xgT_ready, e + 1)
                        pe.wait_ge(we_low, e + 1)
                        for s in range(STEPS):
                            up_gate(e, i, s)
                            if s == 0:
                                if not (first and i == 0):
                                    down(e - 1, 1 - i, r - 1 + i)
                                if not (last and i == 1):
                                    turn(e + 1, 1 - i, r + i)
                            if isinstance(r, int) and (r, i, s) in beside:
                                beside[r, i, s]()

                turn(0, 0, 0)
                body(0, first=True)
                with pe.Fori(1, E // 2 - 1) as r:
                    body(r)
                body(E // 2 - 1, last=True)
                global_keys(2)
                global_keys(3)
                down(E - 1, 1, E // 2 - 1)

        def stage3(s3):
            def sb(name, shape, dt=F32):
                return s3.enter_context(nc.sbuf_tensor(name, shape, dt))

            def sem(name):
                return s3.enter_context(nc.semaphore(name))

            vg_all = sb("vg_all", [P, B, G * HD])
            wts = sb("wts", [P, B, 2, W])
            e2 = sb("e2", [P, B, W])
            den = sb("den", [P, B, W])
            hTs = sb("hTs", [D, 2, S], F32R)
            qT = [sb(f"qT{i}", [P, 2, S]) for i in range(2)]
            kT = [sb(f"kT{i}", [P, 2, W, KEYS]) for i in range(2)]
            vv = [sb(f"vv{i}", [P, W, HG * HD]) for i in range(2)]
            vgbd = [sb(f"vgbd{i}", [P, 2, HG, 32]) for i in range(2)]
            sm = [sb(f"sm{i}", [P, HG, KEYS]) for i in range(2)]
            nmx = [sb(f"nmx{i}", [P, HG]) for i in range(2)]
            ssum = [sb(f"ssum{i}", [P, HG]) for i in range(2)]
            rec = [sb(f"rec{i}", [P, HG]) for i in range(2)]
            ex = [sb(f"ex{i}", [P, HG, KEYS]) for i in range(2)]
            prob = sb("prob", [P, W, HG, P])
            probg = sb("probg", [P, W, HG, NG])
            pT = sb("pT", [P, W, HG, P])
            pTg = sb("pTg", [P, S])
            oT = sb("oT", [P, G, 2, S])
            gd = sb("gd", [P, 2, W], U32)
            g_st = sb("g_st", [P, 2, W, D])
            ff = sb("ff", [P, W, D])
            ef = sb("ef", [P, W, D])
            ss = sb("ss", [P, W, D])
            x_fin = sb("x_fin", [P, W, D])
            o_fin = sb("o_fin", [P, W, D])

            sx, sy, pa, tb, ob = bank[0], bank[1], bank[2:4], bank[4:6], bank[6:8]
            USES = 6
            TURNS = W + 1

            a_done, a_evac, hts_high, kg_ready, vgbd_ready = (sem(n) for n in
                ("a_done", "a_evac", "hts_high", "kg_ready", "vgbd_ready"))
            hts_low = sem("hts_low")
            sx_done, sy_done, sx_read, sy_read = (sem(n) for n in ("sx_done", "sy_done", "sx_read", "sy_read"))
            exp_done, rec_ready, prob_ready = (sem(n) for n in ("exp_done", "rec_ready", "prob_ready"))
            turn_done, turn_evac, pv_done, o_evac = (sem(n) for n in ("turn_done", "turn_evac", "pv_done", "o_evac"))
            out_done, out_read, mask_set = sem("out_done"), sem("out_read"), sem("mask_set")
            gd_ready, gathered, gw_ready = sem("gd_ready"), sem("gathered"), sem("gw_ready")
            vg_done, vg_saved, e2_ready, wc = sem("vg_done"), sem("vg_saved"), sem("e2_ready"), sem("wc")
            g_added, sf_ready, inv_ready, quot_ready = sem("g_added"), sem("sf_ready"), sem("inv_ready"), sem("quot_ready")
            ff_ready, ef_ready, fin_ready, out_stored = sem("ff_ready"), sem("ef_ready"), sem("fin_ready"), sem("out_stored")
            xf_loaded = sem("xf_loaded")

            block = s3.enter_context(nc.Block())

            @block.sync
            def _(sp):
                def finish(b):
                    sp.wait_ge(fin_ready, b * 1 + 1)
                    sp.dma_start(out_rows[b], o_fin[:]).then_inc(out_stored, DMA)

                sp.dma_start(x_fin[:], x_rows[0]).then_inc(xf_loaded, DMA)
                with sp.Fori(0, B - 1) as b:
                    finish(b)
                    sp.wait_ge(out_stored, b * DMA + DMA)
                    sp.dma_start(x_fin[:], x_rows[b + 1]).then_inc(xf_loaded, DMA)
                finish(B - 1)
                sp.wait_ge(out_stored, B * DMA)

            @block.tensor
            def _(pe):
                def project(b, g, some):
                    i = b * G + g
                    if g == 0 and some[0] == 0:
                        pe.wait_ge(hts_low, b * 1 + 1)
                    for m in some:
                        wait(pe, a_evac, i * USES + m - 1)
                        o = pa[m % 2]
                        if m < 4:
                            w2, blk = (wq2, wk2)[m // 2], 2 * g + m % 2
                            t = product(pe, o[:], [w2[:, k, blk * P:(blk + 1) * P] for k in range(2)],
                                        [hTs[:, k, :] for k in range(2)])
                        else:
                            for w in range(2):
                                u = 2 * (m - 4) + w
                                t = product(pe, o[:, w * HG * HD:(w + 1) * HG * HD],
                                            [hTs[:, k, u * P:(u + 1) * P] for k in range(2)],
                                            [wv2[:, k, g * HG * HD:(g + 1) * HG * HD] for k in range(2)])
                        t.then_inc(a_done, 1)

                def scores(b, g, w):
                    i, par = b * G + g, g % 2
                    if w == 0:
                        pe.wait_ge(a_evac, i * USES + 4)
                        pe.wait_ge(kg_ready, i + 1)
                    n = i * W + w
                    for o, r0, s_done, s_read in ((sx, 0, sx_done, sx_read), (sy, 64, sy_done, sy_read)):
                        wait(pe, s_read, n)
                        for blk in range(2):
                            t = pe.matmul(o[:, blk * KEYS:(blk + 1) * KEYS],
                                          qT[par][r0:r0 + 64, blk, w * P:(w + 1) * P],
                                          kT[par][r0:r0 + 64, blk, w, :], start=True, stop=True)
                        t.then_inc(s_done, 1)

                def values_global(b, g):
                    i, par = b * G + g, g % 2
                    pe.wait_ge(turn_evac, i * TURNS + TURNS)
                    pe.wait_ge(vgbd_ready, i + 1)
                    if g == 0:
                        wait(pe, out_read, b * 1)
                    for f in range(2):
                        wait(pe, o_evac, i * 2 + f - 1)
                        pe.matmul(ob[f][:], vgbd[par][:, f, :, :].rearrange("p c d -> p (c d)"), pTg[:],
                                  start=True, stop=False, skip_group_check=True)

                def values_local(b, g, f):
                    i, par = b * G + g, g % 2
                    pe.wait_ge(a_evac, i * USES + USES)
                    for w in range(W):
                        for c in range(HG):
                            v0 = HOME[c] * HD + f * 32
                            t = pe.matmul(ob[f][32 * c:32 * c + 32, w * P:(w + 1) * P], vv[par][:, w, v0:v0 + 32],
                                          pT[:, w, c, :], start=False, stop=(w == W - 1), skip_group_check=True)
                    t.then_inc(pv_done, 1)

                def turn(b, g, some):
                    i = b * G + g
                    if isinstance(b, int) and b == 0 and g == 0:
                        pe.wait_ge(vg_saved, 4)
                    for u in some:
                        wait(pe, turn_evac, i * TURNS + u - 1)
                        o = tb[(g + u) % 2]
                        for c in range(4):
                            if u < W:
                                if c == 0:
                                    pe.wait_ge(prob_ready, i * W + u + 1)
                                src = prob[:, u, c, :]
                            else:
                                src = probg[:, c, :, :].rearrange("p c s -> p (c s)")
                            t = pe.transpose(o[:, c * P:(c + 1) * P], src, ident[:])
                        t.then_inc(turn_done, 1)

                def output(b, some):
                    pe.wait_ge(o_evac, b * (2 * G) + 2 * G)
                    for w in some:
                        for g in range(G):
                            for f in range(2):
                                t = pe.matmul(ob[0][:, w * D:(w + 1) * D], oT[:, g, f, w * P:(w + 1) * P],
                                              wo[:, g, f, :], start=(g + f == 0), stop=(g == G - 1 and f == 1))
                    if W - 1 in some:
                        t.then_inc(out_done, 1)

                def step(b, g, first=False, last=False):
                    before_it = None if first and g == 0 else (b if g else b - 1, (g - 1) % G)
                    after_it = None if last and g == G - 1 else (b if g < G - 1 else b + 1, (g + 1) % G)
                    scores(b, g, 0)
                    if before_it:
                        values_global(*before_it)
                    scores(b, g, 1)
                    if before_it:
                        values_local(*before_it, 0)
                    scores(b, g, 2)
                    if before_it:
                        values_local(*before_it, 1)
                    scores(b, g, 3)
                    if after_it:
                        project(*after_it, (0, 1, 2, 3))
                    if g == 0 and not first:
                        output(b - 1, (0, 1))
                    turn(b, g, (0, 1))
                    if after_it:
                        project(*after_it, (4,))
                    if g == 0 and not first:
                        output(b - 1, (2, 3))
                    turn(b, g, (2,))
                    if after_it:
                        project(*after_it, (5,))
                    turn(b, g, (3, 4))

                def all_global_values():
                    for k, o in enumerate((tb[0], tb[1], ob[0], ob[1])):
                        for f in range(2):
                            for c in range(HG):
                                cols = wv[:].rearrange("p (g j d) -> p j g d", g=G, j=HG)[:, HOME[c]]
                                t = pe.matmul(o[32 * c:32 * c + 32, f * G * HD:(f + 1) * G * HD],
                                              hgT[:, (2 * k + f) * NG:(2 * k + f + 1) * NG], cols, start=True, stop=True)
                        t.then_inc(vg_done, 1)

                project(0, 0, range(USES))
                all_global_values()
                for g in range(G):
                    step(0, g, first=True)
                pe.wait_ge(wout_loaded, 2 * HG * DMA)
                with pe.Fori(1, B - 1) as b:
                    for g in range(G):
                        step(b, g)
                for g in range(G):
                    step(B - 1, g, last=True)
                values_global(B - 1, G - 1)
                for f in range(2):
                    values_local(B - 1, G - 1, f)
                output(B - 1, range(W))

            @block.vector
            def _(dve):
                def low_part(b):
                    dve.wait_ge(hts_high, b * 1 + 1)
                    dve.tensor_tensor(hTs[:, 1, :], hT_all[:, b, :], hTs[:, 0, :], ALU.subtract).then_inc(hts_low, 1)

                def mask_scores(b, g, w):
                    n = (b * G + g) * W + w
                    wait(dve, exp_done, n - 1)
                    for o, c0, s_done, s_read in ((sx, 0, sx_done, sx_read), (sy, 2, sy_done, sy_read)):
                        dve.wait_ge(s_done, n + 1)
                        settle(dve)
                        for c in range(2):
                            t = dve.tensor_tensor_reduce(out=sm[w % 2][:, c0 + c, :], in0=o[:, c * KEYS:(c + 1) * KEYS],
                                                         in1=maskb[:, w, :], scale=-1.0, scalar=BIG, op0=ALU.add,
                                                         op1=ALU.min, accum_out=nmx[w % 2][:, c0 + c:c0 + c + 1])
                        t.then_inc(s_read, 1)

                def invert(b, g, w):
                    n = (b * G + g) * W + w
                    dve.wait_ge(exp_done, n + 1)
                    wait(dve, prob_ready, n - 1)
                    dve.reciprocal(rec[w % 2][:], ssum[w % 2][:]).then_inc(rec_ready, 1)

                def take(b, g, some):
                    i, par = b * G + g, g % 2
                    for m in some:
                        dve.wait_ge(a_done, i * USES + m + 1)
                        o = pa[m % 2]
                        if m < 2:
                            t = dve.tensor_scalar(qT[par][:, m, :], o[:], float(HD) ** -0.5, None, ALU.mult)
                        elif m < 4:
                            t = dve.tensor_copy(kT[par][:, m - 2, :, 0:P], o[:].rearrange("p (w k) -> p w k", w=W))
                        else:
                            v = 2 * (m - 4)
                            t = dve.tensor_copy(vv[par][:, v:v + 2, :].rearrange("p w e -> p (w e)"), o[:])
                        t.then_inc(a_evac, 1)

                def finish(b, part):
                    if part == "ff":
                        dve.wait_ge(gw_ready, b * 1 + 1)
                        dve.tensor_tensor(ff[:], g_st[:, 0, :, :], g_st[:, 1, :, :], ALU.add).then_inc(g_added, 1)
                    if part == "ff+":
                        dve.wait_ge(g_added, b * 1 + 1)
                        dve.tensor_tensor(ff[:], ff[:], ffn_all[:, b, :, :], ALU.add).then_inc(ff_ready, 1)
                    if part == "s":
                        dve.wait_ge(out_done, b * 1 + 1)
                        dve.tensor_tensor(ss[:], ob[0][:].rearrange("p (w d) -> p w d", w=W), xn_all[:, b, :, :],
                                          ALU.add).then_inc(out_read, 1)
                    if part == "s*ff":
                        dve.wait_ge(ff_ready, b * 1 + 1)
                        dve.wait_ge(out_read, b * 1 + 1)
                        dve.tensor_tensor(ss[:], ss[:], ff[:], ALU.mult)
                    if part == "1+e":
                        dve.wait_ge(ef_ready, b * 1 + 1)
                        dve.tensor_scalar(ef[:], ef[:], 1.0, None, ALU.add).then_inc(sf_ready, 1)
                    if part in range(W):
                        if part == 0:
                            dve.wait_ge(sf_ready, b * 1 + 1)
                        dve.reciprocal(ef[:, part, :], ef[:, part, :]).then_inc(inv_ready, 1)
                    if part == "/":
                        dve.wait_ge(inv_ready, b * W + W)
                        dve.tensor_tensor(ss[:], ss[:], ef[:], ALU.mult).then_inc(quot_ready, 1)
                    if part == "x+":
                        dve.wait_ge(quot_ready, b * 1 + 1)
                        dve.wait_ge(xf_loaded, b * DMA + DMA)
                        dve.tensor_tensor(o_fin[:], ss[:], x_fin[:], ALU.add).then_inc(fin_ready, 1)

                def step(b, g, first=False, last=False):
                    after_it = None if last and g == G - 1 else (b if g < G - 1 else b + 1, (g + 1) % G)
                    parts = ((), (), ()) if first else ((("ff",), ("ff+",), ("s",)), (("s*ff",), ("1+e",), (0,)),
                                                        ((1,), (2,), (3,)), (("/",), ("x+",), ()))[g]
                    if g == 0:
                        wait(dve, mask_set, b * 1)
                    mask_scores(b, g, 0)
                    for part in parts[0]:
                        finish(b - 1, part)
                    mask_scores(b, g, 1)
                    if g == G - 1 and not last:
                        low_part(b + 1)
                    for part in parts[1]:
                        finish(b - 1, part)
                    invert(b, g, 0)
                    mask_scores(b, g, 2)
                    invert(b, g, 1)
                    mask_scores(b, g, 3)
                    if g == G - 1 and not last:
                        dve.wait_ge(sy_read, (b * G + g) * W + W)
                        dve.tensor_copy(maskb[:, :, P:KEYS], gm_all[:, b + 1, :, :]).then_inc(mask_set, 1)
                    if after_it:
                        take(*after_it, (0,))
                    invert(b, g, 2)
                    if after_it:
                        take(*after_it, (1, 2))
                    invert(b, g, 3)
                    if after_it:
                        take(*after_it, (3, 4, 5))
                    for part in parts[2]:
                        finish(b - 1, part)

                def weights():
                    ch = Chain(dve, wc, 4)
                    ch.round(0)
                    dve.wait_ge(e2_ready, 1)
                    ch.link(dve.tensor_scalar(den[:], e2[:], 1.0, None, ALU.add))
                    ch.link(dve.reciprocal(den[:], den[:]))
                    ch.link(dve.tensor_tensor(e2[:], e2[:], den[:], ALU.mult))
                    dve.tensor_tensor(wts[:, :, 0, :], den[:], valid_all[:, :, 0, :], ALU.mult)
                    ch.link(dve.tensor_tensor(wts[:, :, 1, :], e2[:], valid_all[:, :, 1, :], ALU.mult))
                    ch.done()

                low_part(0)
                take(0, 0, range(USES))
                weights()
                for g in range(G):
                    step(0, g, first=True)
                with dve.Fori(1, B - 1) as b:
                    for g in range(G):
                        step(b, g)
                for g in range(G):
                    step(B - 1, g, last=True)
                for part in ("ff", "ff+", "s", "s*ff", "1+e", *range(W), "/", "x+"):
                    finish(B - 1, part)

            @block.scalar
            def _(act):
                def exps(b, g, w):
                    i = b * G + g
                    n = i * W + w
                    act.wait_ge(sy_read, n + 1)
                    wait(act, rec_ready, n - 1)
                    wait(act, prob_ready, n - 1)
                    for c in range(HG):
                        t = act.activation(ex[w % 2][:, c, :], sm[w % 2][:, c, :], ACT.Exp, bias=nmx[w % 2][:, c:c + 1],
                                           scale=-1.0, accum_out=ssum[w % 2][:, c:c + 1])
                    t.then_inc(exp_done, 1)

                def high_part(b):
                    wait(act, a_done, b * (G * USES))
                    act.activation(hTs[:, 0, :], hT_all[:, b, :], ACT.Copy).then_inc(hts_high, 1)

                def save_values(b, g, f):
                    act.wait_ge(pv_done, (b * G + g) * 2 + f + 1)
                    act.activation(oT[:, g, f, :], ob[f][:], ACT.Copy).then_inc(o_evac, 1)

                def save_turned(b, g):
                    for u in range(TURNS):
                        act.wait_ge(turn_done, (b * G + g) * TURNS + u + 1)
                        o = tb[(g + u) % 2]
                        dst = pT[:, u, :, :].rearrange("p c q -> p (c q)") if u < W else pTg[:]
                        act.activation(dst, o[:], ACT.Copy).then_inc(turn_evac, 1)

                def sigmoid_part(b):
                    act.wait_ge(ff_ready, b * 1 + 1)
                    act.activation(ef[:], ff[:], ACT.Exp, scale=-1.0).then_inc(ef_ready, 1)

                def step(b, g, first=False, last=False):
                    if g == G - 1 and not last:
                        high_part(b + 1)
                    exps(b, g, 0)
                    exps(b, g, 1)
                    if not (first and g == 0):
                        save_values(b if g else b - 1, (g - 1) % G, 0)
                    exps(b, g, 2)
                    if not (first and g == 0):
                        save_values(b if g else b - 1, (g - 1) % G, 1)
                    exps(b, g, 3)
                    save_turned(b, g)
                    if g == 0 and not first:
                        sigmoid_part(b - 1)

                high_part(0)
                act.activation(e2[:], dlog_all[:], ACT.Exp).then_inc(e2_ready, 1)
                for k, o in enumerate((tb[0], tb[1], ob[0], ob[1])):
                    act.wait_ge(vg_done, k + 1)
                    act.activation(vg_all[:, 2 * k:2 * k + 2, :].rearrange("p b e -> p (b e)"), o[:], ACT.Copy)\
                        .then_inc(vg_saved, 1)
                for g in range(G):
                    step(0, g, first=True)
                with act.Fori(1, B - 1) as b:
                    for g in range(G):
                        step(b, g)
                for g in range(G):
                    step(B - 1, g, last=True)
                for f in range(2):
                    save_values(B - 1, G - 1, f)
                sigmoid_part(B - 1)

            @block.gpsimd
            def _(pool):
                def global_keys(b, g):
                    i, par = b * G + g, g % 2
                    wait(pool, sy_done, (i - 1) * W)
                    pool.tensor_copy(kT[par][:, :, :, P:KEYS],
                                     kg_all[:, 2 * g:2 * g + 2, b, :].unsqueeze(2).to_broadcast([P, 2, W, NG]))\
                        .then_inc(kg_ready, 1)

                def global_values(b, g):
                    i, par = b * G + g, g % 2
                    wait(pool, pv_done, (i - 1) * 2)
                    v = vg_all[:, b, g * HD:(g + 1) * HD].rearrange("p (f d) -> p f d", f=2)
                    pool.tensor_tensor(vgbd[par][:], v.unsqueeze(2).to_broadcast([P, 2, HG, 32]),
                                       own[:].unsqueeze(1).to_broadcast([P, 2, HG, 32]), ALU.mult).then_inc(vgbd_ready, 1)

                def divide(b, g, w):
                    n = (b * G + g) * W + w
                    pool.wait_ge(rec_ready, n + 1)
                    if w == 0:
                        wait(pool, turn_done, (b * G + g) * TURNS)
                    for dst, k0, k1 in ((prob, 0, P), (probg, P, KEYS)):
                        t = pool.tensor_tensor(dst[:, w, :, :], ex[w % 2][:, :, k0:k1],
                                               rec[w % 2][:].unsqueeze(2).to_broadcast([P, HG, k1 - k0]), ALU.mult)
                    t.then_inc(prob_ready, 1)

                picks = [(k, w) for w in range(W) for k in range(2)]

                def gather(b, some):
                    for k, w in some:
                        pool.indirect_dma_start(out=g_st[:, k, w, :], out_offset=None, in_=eo_dram,
                                                in_offset=bass.IndirectOffsetOnAxis(ap=gd[:, k, w:w + 1], axis=0))\
                            .then_inc(gathered, DMA)

                def step(b, g, last=False):
                    if not (last and g == G - 1):
                        ahead = (b if g < G - 1 else b + 1, (g + 1) % G)
                        global_keys(*ahead)
                    for w in range(W):
                        divide(b, g, w)
                    if not (last and g == G - 1):
                        global_values(*ahead)
                    if g == 0:
                        wait(pool, g_added, b * 1)
                        pool.tensor_copy(gd[:], dest_all[:, b, :, :]).then_inc(gd_ready, 1)
                        pool.wait_ge(gd_ready, b * 1 + 1)
                        settle(pool)
                    gather(b, picks[3 * g:3 * g + 3])
                    if g == G - 1:
                        pool.wait_ge(gathered, (b + 1) * (2 * W * DMA))
                        pool.wait_ge(wc, 4)
                        pool.tensor_tensor(g_st[:].rearrange("p k w d -> p (k w) d"),
                                           g_st[:].rearrange("p k w d -> p (k w) d"),
                                           wts[:, b, :, :].rearrange("p k w -> p (k w)").unsqueeze(2)
                                           .to_broadcast([P, 2 * W, D]), ALU.mult).then_inc(gw_ready, 1)

                global_keys(0, 0)
                pool.wait_ge(vg_saved, 4)
                global_values(0, 0)
                for g in range(G):
                    step(0, g)
                with pool.Fori(1, B - 1) as b:
                    for g in range(G):
                        step(b, g)
                for g in range(G):
                    step(B - 1, g, last=True)
        with early:
            for stage in (stage1, stage2):
                with ExitStack() as s:
                    stage(s)
        with ExitStack() as s:
            stage3(s)


def kernel(**inputs):
    import numpy as _np
    import concourse.bacc as _bacc
    from concourse import mybir as _mybir
    from concourse.bass_utils import run_bass_kernel_spmd as _run

    nc = _bacc.Bacc("TRN2", target_bir_lowering=False, num_devices=1)
    arrays, args = {}, []
    for name in ["L0_attn_x", "L0_attn_norm_w", "L0_attn_w_q", "L0_attn_w_k", "L0_attn_w_v", "L0_attn_w_out",
                 "L0_attn_scorer_w", "L0_attn_scorer_b", "L0_ffn_router_w", "L0_ffn_rg", "L0_ffn_ru", "L0_ffn_rd",
                 "L0_ffn_sg", "L0_ffn_su", "L0_ffn_sd"]:
        a = _np.asarray(inputs[name])
        a = _np.ascontiguousarray(a.T if name == "L0_ffn_router_w" else a)
        arrays["in_" + name] = a
        args.append(nc.dram_tensor("in_" + name, a.shape, _mybir.dt.from_np(a.dtype), kind="ExternalInput").ap())
    shape = inputs["L0_attn_x"].shape
    out = nc.dram_tensor("out_0", shape, _mybir.dt.float32, kind="ExternalOutput").ap()
    recurrent_layer(nc, *args, out)
    r = _run(nc, [arrays], core_ids=[0])
    return r.results[0]["out_0"]
```

```python
import concourse.bass as bass
from concourse import mybir
from contextlib import ExitStack



def recurrent_layer(nc, x, norm_w, w_q, w_k, w_v, w_out, scorer_w, scorer_b, router_wT,
                    rg, ru, rd, sg, su, sd, out):
    F32, F32R, BF16, U32 = mybir.dt.float32, mybir.dt.float32r, mybir.dt.bfloat16, mybir.dt.uint32
    ALU, ACT, AX = mybir.AluOpType, mybir.ActivationFunctionType, mybir.AxisListType

    B, S, D = x.shape
    P = 128
    W = S // P
    T = B * S
    H, HD = w_q.shape[1] // 64, 64
    HG = 4
    G = H // HG
    NG = 32
    KEYS = P + NG
    E, _, FR = rg.shape
    FS = sg.shape[1]
    RB, SB = FR // P, FS // P
    CAP = max(int(1.25 * T / E), 1)
    CT = CAP // P
    HALF = CAP // 2
    SLOTS = E * CAP
    HOME = (0, 2, 1, 3)
    NEG = -1e30
    BIG = 3e38
    EPS_LN, EPS_ATT, EPS_FFN = 1e-5, 1e-6, 1.1920929e-07
    DMA = 16

    ctx = ExitStack()

    def sb(name, shape, dt=F32):
        return ctx.enter_context(nc.sbuf_tensor(name, shape, dt))

    def sem(name):
        return ctx.enter_context(nc.semaphore(name))

    def wait(eng, s, value):
        if not isinstance(value, int) or value > 0:
            eng.wait_ge(s, value)

    def settle(eng):
        eng.nop(nofuse=True)

    class Chain:

        def __init__(self, eng, s, per_round):
            self.eng, self.s, self.per = eng, s, per_round

        def round(self, r, n=0):
            self.base, self.n = r * self.per, n

        def link(self, instruction):
            self.n += 1
            instruction.then_inc(self.s, 1)
            self.eng.wait_ge(self.s, self.base + self.n)

        def done(self):
            assert self.n == self.per, (self.n, self.per)

    x_rows = x.rearrange("b (w p) d -> b p w d", p=P)
    out_rows = out.rearrange("b (w p) d -> b p w d", p=P)

    with ctx:
        xg_dram = nc.dram_tensor("xg_dram", [SLOTS + 2 * W * P, D], F32, kind="Internal").ap()
        eo_dram = nc.dram_tensor("eo_dram", [SLOTS + 2 * W * P, D], F32, kind="Internal").ap()

        ident = sb("ident", [P, P])
        before = sb("before", [P, P], BF16)
        ones_bf = sb("ones_bf", [P, P], BF16)
        iota_e = sb("iota_e", [P, E])
        iota_g = sb("iota_g", [P, NG])
        trash = sb("trash", [P, 2, W])
        own = sb("own", [P, HG, 32])
        pow_m = sb("pow_m", [P, 2 * W])
        zeros = sb("zeros", [P, D])
        onesr = sb("onesr", [B, S])
        bias_s = sb("bias_s", [P, 1])
        normw = sb("normw", [P, 1])
        rs9 = sb("rs9", [D, E + 1])

        xn_all = sb("xn_all", [P, B, W, D])
        hT_all = sb("hT_all", [D, B, S])
        ffn_all = sb("ffn_all", [P, B, W, D])
        wv = sb("wv", [D, H * HD])
        wq2, wk2, wv2 = (sb(f"w{c}2", [D, 2, H * HD], F32R) for c in "qkv")
        wo = sb("wo", [P, G, 2, D])
        dest_all = sb("dest_all", [P, B, 2, W], U32)
        valid_all = sb("valid_all", [P, B, 2, W])
        dlog_all = sb("dlog_all", [P, B, W])
        score_all = sb("score_all", [P, B, W])
        r1_all = sb("r1_all", [P, B, W])
        maskb = sb("maskb", [P, W, KEYS])

        kg_all = sb("kg_all", [P, 2 * G, B, NG])
        gm_all = sb("gm_all", [P, B, W, NG])
        hgT = sb("hgT", [D, B * NG])
        hTs = sb("hTs", [D, 2, S], F32R)
        late = sb("late", [P, 2, CT * D])

        bank = [ctx.enter_context(nc.psum_tensor(f"bank{i}", [P, 512], F32)) for i in range(8)]

        early = ExitStack()

        def sb(name, shape, dt=F32):
            return early.enter_context(nc.sbuf_tensor(name, shape, dt))

        wq = sb("wq", [D, H * HD])
        wk = sb("wk", [D, H * HD])
        wge = [sb(f"wge{i}", [D, FR]) for i in range(2)]
        wue = [sb(f"wue{i}", [D, FR]) for i in range(2)]
        wde = [sb(f"wde{i}", [P, RB, D]) for i in range(2)]
        xgr = [sb(f"xgr{i}", [P, CT, D]) for i in range(2)]
        xgr_loaded = [sem(f"xgr_loaded{i}") for i in range(2)]
        wge2 = [sb(f"wge2{i}", [D, 2, FR], F32R) for i in range(2)]
        wue2 = [sb(f"wue2{i}", [D, 2, FR], F32R) for i in range(2)]
        wd_loaded = [sem(f"wd_loaded{i}") for i in range(2)]
        we_loaded, we_high, we_low = sem("we_loaded"), sem("we_high"), sem("we_low")
        wattn_loaded, wsplit = sem("wattn_loaded"), sem("wsplit")
        wout_loaded = sem("wout_loaded")
        eo_stored = [sem(f"eo_stored{i}") for i in range(2)]
        scattered = sem("scattered")
        hts_high, hts_low = sem("hts_high"), sem("hts_low")
        consts = sem("consts")

        def product(pe, o, a, b, more=False):
            pe.matmul(o, a[0], b[0], start=not more, stop=False, skip_group_check=more)
            pe.matmul(o, a[0], b[1], start=False, stop=False, skip_group_check=more)
            return pe.matmul(o, a[1], b[0], start=False, stop=True, skip_group_check=more)

        def load_rows(sp, e, i):
            sp.dma_start(xgr[i][:], xg_dram[bass.ds(e * CAP, CAP), :].rearrange("(s p) d -> p s d", p=P))\
                .then_inc(xgr_loaded[i], DMA)

        def load_expert(sp, e, i):
            sp.dma_start(wge[i][:], rg[e]).then_inc(we_loaded, DMA)
            sp.dma_start(wue[i][:], ru[e]).then_inc(we_loaded, DMA)
            sp.dma_start(wde[i][:], rd[e].rearrange("(j p) d -> p j d", p=P)).then_inc(wd_loaded[i], DMA)

        def stage1(s1):
            def sb(name, shape, dt=F32):
                return s1.enter_context(nc.sbuf_tensor(name, shape, dt))

            def sem(name):
                return s1.enter_context(nc.semaphore(name))

            x_st = sb("x_st", [P, W, D])
            xn_st = sb("xn_st", [P, W, D])
            h_st = sb("h_st", [P, W, D])
            xn_sc = sb("xn_sc", [P, W, D])
            xnT = sb("xnT", [D, S])
            xnT2 = sb("xnT2", [D, 2, S], F32R)
            wsg = sb("wsg", [D, FS])
            wsu = sb("wsu", [D, FS])
            wsg2 = sb("wsg2", [D, 2, FS], F32R)
            wsu2 = sb("wsu2", [D, 2, FS], F32R)
            wsd = sb("wsd", [P, SB, D])
            sil = sb("sil", [P, 2, S])
            acts = sb("acts", [P, 2, S])
            st6 = sb("st6", [P, W, 6])
            mv = sb("mv", [P, W, 2])
            var = sb("var", [P, 2, W])
            yv = sb("yv", [P, 2, W])
            t1 = sb("t1", [P, 2, W])
            rstd = sb("rstd", [P, W])
            r12 = sb("r12", [P, 2, W])
            lgs = sb("lgs", [P, W, E])
            sct = sb("sct", [P, W])
            mx8 = sb("mx8", [P, W, 8])
            ix8 = sb("ix8", [P, W, 8], U32)
            ixf = sb("ixf", [P, 2, W])
            oh = sb("oh", [P, 2, W, E])
            msk = sb("msk", [P, W, E], BF16)
            carry = sb("carry", [P, E])
            tsum = sb("tsum", [P, E])
            pos = sb("pos", [P, W, E])
            ohp = sb("ohp", [P, 2, W, E])
            posk = sb("posk", [P, 2, W])
            valid = sb("valid", [P, 2, W])
            dest = sb("dest", [P, 2, W])
            dest_st = sb("dest_st", [P, 2, W], U32)

            gate, up, down, tx, lg = bank[0:2], bank[2:4], bank[4], bank[5:7], bank[7]
            lgv = lg[:, 0:W * 16].rearrange("p (w e) -> p w e", e=16)
            pref = lg[:, 128:128 + W * E].rearrange("p (w e) -> p w e", e=E)
            tot = lg[:, 256:256 + W * E].rearrange("p (w e) -> p w e", e=E)

            x_loaded = sem("x_loaded")
            wffn_loaded, small_loaded = sem("wffn_loaded"), sem("small_loaded")
            var_ready, pow_ready = sem("var_ready"), sem("pow_ready")
            xn_ready, h_ready, xn_saved = sem("xn_ready"), sem("h_ready"), sem("xn_saved")
            tx_done, th_done, lg_done, pref_done = sem("tx_done"), sem("th_done"), sem("lg_done"), sem("pref_done")
            ws_high, ws_low, xnT_high, xnT_low = sem("ws_high"), sem("ws_low"), sem("xnT_high"), sem("xnT_low")
            xnT_ready, hT_saved = sem("xnT_ready"), sem("hT_saved")
            mask_ready, pref_read, dest_ready = sem("mask_ready"), sem("pref_read"), sem("dest_ready")
            xsc_ready, xg_zeroed = sem("xsc_ready"), sem("xg_zeroed")
            gu_done, silu_done, act_ready = sem("gu_done"), sem("silu_done"), sem("act_ready")
            dn_done, ffn_saved = sem("dn_done"), sem("ffn_saved")
            r12_ready, rs9_ready, wsd_loaded = sem("r12_ready"), sem("rs9_ready"), sem("wsd_loaded")
            lnc, rtc, pc = sem("lnc"), sem("rtc"), sem("pc")

            block = s1.enter_context(nc.Block())

            @block.sync
            def _(sp):
                sp.dma_start(x_st[:], x_rows[0]).then_inc(x_loaded, DMA)
                sp.dma_start(rs9[:, 0:E], router_wT).then_inc(small_loaded, DMA)
                sp.dma_start(rs9[:, E:E + 1], scorer_w).then_inc(small_loaded, DMA)
                sp.dma_start(normw[:], norm_w.rearrange("(d a) -> d a", a=1)).then_inc(small_loaded, DMA)
                sp.dma_start(bias_s[:], scorer_b.rearrange("(a b) -> a b", a=1).to_broadcast([P, 1]))\
                    .then_inc(small_loaded, DMA)
                sp.dma_start(wsg[:], sg).then_inc(wffn_loaded, DMA)
                sp.dma_start(wsu[:], su).then_inc(wffn_loaded, DMA)
                sp.dma_start(wsd[:], sd.rearrange("(j p) d -> p j d", p=P)).then_inc(wsd_loaded, DMA)
                sp.wait_ge(consts, 1)
                sp.dma_start(xg_dram[0:SLOTS, :].rearrange("(t p) d -> p t d", p=P),
                             zeros[:].unsqueeze(1).to_broadcast([P, SLOTS // P, D])).then_inc(xg_zeroed, DMA)
                with sp.Fori(1, B) as b:
                    sp.wait_ge(xn_ready, b * 1)
                    sp.dma_start(x_st[:], x_rows[b]).then_inc(x_loaded, DMA)
                load_expert(sp, 0, 0)
                load_expert(sp, 1, 1)
                for w_sb, w_dram in ((wq, w_q), (wk, w_k), (wv, w_v)):
                    sp.dma_start(w_sb[:], w_dram).then_inc(wattn_loaded, DMA)
                for c in range(HG):
                    for f in range(2):
                        src = w_out.rearrange("(g j f q) d -> j f q g d", j=HG, f=2, q=32)[HOME[c], f]
                        sp.dma_start(wo[32 * c:32 * c + 32, :, f, :], src).then_inc(wout_loaded, DMA)
                sp.wait_ge(scattered, B * 2 * W * DMA)
                load_rows(sp, 0, 0)
                load_rows(sp, 1, 1)

            @block.gpsimd
            def _(pool):
                n = [0]

                def link(i):
                    n[0] += 1
                    i.then_inc(pc, 1)
                    pool.wait_ge(pc, n[0])

                link(pool.memset(zeros[:], 0.0))
                pool.memset(pow_m[:], -0.5).then_inc(consts, 1)
                link(pool.affine_select(out=ident[:], in_=zeros[:], compare_op=ALU.not_equal, fill=1.0,
                                        base=0, pattern=[[-1, P]], channel_multiplier=1))
                link(pool.memset(ones_bf[:], 1.0))
                link(pool.affine_select(out=before[:], in_=ones_bf[:], compare_op=ALU.is_gt, fill=0.0,
                                        base=0, pattern=[[1, P]], channel_multiplier=-1))
                link(pool.iota(iota_e[:], pattern=[[1, E]], base=0, channel_multiplier=0,
                               allow_small_or_imprecise_dtypes=True))
                pool.iota(trash[:], pattern=[[W * P, 2], [P, W]], base=SLOTS, channel_multiplier=1,
                          allow_small_or_imprecise_dtypes=True).then_inc(consts, 1)

                def norm_help(b):
                    pool.wait_ge(var_ready, b * 2 + 1)
                    pool.tensor_tensor(yv[:, 0, :], var[:, 0, :], pow_m[:, 0:W], ALU.pow).then_inc(pow_ready, 1)
                    pool.wait_ge(var_ready, b * 2 + 2)
                    pool.tensor_tensor(yv[:].rearrange("p a w -> p (a w)"), var[:].rearrange("p a w -> p (a w)"),
                                       pow_m[:], ALU.pow).then_inc(pow_ready, 1)
                    pool.wait_ge(xn_ready, b * 1 + 1)
                    pool.wait_ge(r12_ready, b * 1 + 1)
                    wait(pool, th_done, b * 1)
                    pool.tensor_tensor(h_st[:], xn_st[:], r12[:, 0, :].unsqueeze(2).to_broadcast([P, W, D]),
                                       ALU.mult).then_inc(h_ready, 1)
                    pool.tensor_copy(r1_all[:, b, :], r12[:, 0, :])
                    pool.tensor_copy(xn_all[:, b, :, :], xn_st[:]).then_inc(xn_saved, 1)

                def scatter(b):
                    pool.wait_ge(xn_saved, b * 1 + 1)
                    if isinstance(b, int) and b == B - 1:
                        rows, to = xn_all[:, b, :, :], dest_all[:, b, :, :]
                        pool.wait_ge(dest_ready, b * 1 + 1)
                        pool.wait_ge(scattered, b * (2 * W * DMA))
                    else:
                        rows, to = xn_sc, dest_st
                        wait(pool, scattered, b * (2 * W * DMA))
                        pool.tensor_copy(xn_sc[:], xn_all[:, b, :, :]).then_inc(xsc_ready, 1)
                        pool.wait_ge(dest_ready, b * 1 + 1)
                        pool.tensor_copy(dest_all[:, b, :, :], dest_st[:])
                        pool.wait_ge(xsc_ready, b * 1 + 1)
                    settle(pool)
                    for w in range(W):
                        for k in range(2):
                            pool.indirect_dma_start(
                                out=xg_dram, out_offset=bass.IndirectOffsetOnAxis(ap=to[:, k, w:w + 1], axis=0),
                                in_=rows[:, w, :], in_offset=None).then_inc(scattered, DMA)

                def body(b, last=False):
                    if not last:
                        norm_help(b + 1)
                    scatter(b)

                norm_help(0)
                link(pool.iota(iota_g[:], pattern=[[1, NG]], base=1, channel_multiplier=0,
                               allow_small_or_imprecise_dtypes=True))
                link(pool.memset(own[:], 1.0))
                link(pool.affine_select(out=own[:], in_=own[:], compare_op=ALU.is_ge, fill=0.0,
                                        base=0, pattern=[[-32, HG], [0, 32]], channel_multiplier=1))
                link(pool.affine_select(out=own[:], in_=own[:], compare_op=ALU.is_ge, fill=0.0,
                                        base=31, pattern=[[32, HG], [0, 32]], channel_multiplier=-1))
                link(pool.memset(onesr[:], 1.0))
                link(pool.memset(maskb[:], 0.0))
                pool.affine_select(out=maskb[:, :, 0:P], in_=maskb[:, :, 0:P], compare_op=ALU.is_ge,
                                   fill=NEG, base=0, pattern=[[0, W], [-1, P]], channel_multiplier=1)
                pool.wait_ge(xg_zeroed, DMA)
                body(0)
                with pool.Fori(1, B - 1) as b:
                    body(b)
                body(B - 1, last=True)

            @block.vector
            def _(dve):
                ln = Chain(dve, lnc, 12)
                rt = Chain(dve, rtc, 11)

                def root(v, y, t):
                    ln.link(dve.tensor_tensor(t, y, y, ALU.mult))
                    ln.link(dve.tensor_tensor(t, t, v, ALU.mult))
                    ln.link(dve.tensor_scalar(t, t, -0.5, 1.5, ALU.mult, ALU.add))

                def ln_a(b):
                    ln.round(b)
                    dve.wait_ge(x_loaded, b * DMA + DMA)
                    for w in range(W):
                        i = dve.bn_stats(st6[:, w, :], x_st[:, w, :])
                    ln.link(i)
                    settle(dve)
                    for w in range(W):
                        i = dve.bn_aggr(mv[:, w, :], st6[:, w, :])
                    ln.link(i)
                    dve.tensor_scalar(var[:, 0, :], mv[:, :, 1], EPS_LN, None, ALU.add).then_inc(var_ready, 1)

                def ln_b(b):
                    dve.wait_ge(pow_ready, b * 2 + 1)
                    dve.wait_ge(var_ready, b * 2 + 1)
                    root(var[:, 0, :], yv[:, 0, :], t1[:, 0, :])
                    ln.link(dve.tensor_tensor(rstd[:], yv[:, 0, :], t1[:, 0, :], ALU.mult))
                    ln.link(dve.tensor_tensor(t1[:, 1, :], rstd[:], rstd[:], ALU.mult))
                    ln.link(dve.tensor_tensor(t1[:, 1, :], t1[:, 1, :], mv[:, :, 1], ALU.mult))
                    ln.link(dve.tensor_scalar(var[:, 0, :], t1[:, 1, :], EPS_ATT, None, ALU.add))
                    dve.tensor_scalar(var[:, 1, :], t1[:, 1, :], EPS_FFN, None, ALU.add).then_inc(var_ready, 1)

                def ln_c(b):
                    dve.wait_ge(pow_ready, b * 2 + 2)
                    dve.wait_ge(var_ready, b * 2 + 2)
                    root(var[:], yv[:], t1[:])
                    wait(dve, xn_saved, b * 1)
                    dve.tensor_tensor(r12[:], yv[:], t1[:], ALU.mult).then_inc(r12_ready, 1)
                    ln.done()

                def ln_d(b):
                    wait(dve, tx_done, b * 1)
                    for w in range(W):
                        i = dve.tensor_scalar(xn_st[:, w, :], x_st[:, w, :], mv[:, w, 0:1], rstd[:, w:w + 1],
                                              ALU.subtract, ALU.mult)
                    i.then_inc(xn_ready, 1)

                def save_scaled(b):
                    dve.wait_ge(th_done, b * 1 + 1)
                    dve.tensor_scalar(hT_all[:, b, :], tx[1][:], normw[:, 0:1], None, ALU.mult).then_inc(hT_saved, 1)

                def route_a(b):
                    rt.round(b)
                    dve.wait_ge(lg_done, b * 1 + 1)
                    dve.wait_ge(r12_ready, b * 1 + 1)
                    dve.tensor_tensor(lgs[:], lgv[:, :, 0:E], r12[:, 1, :].unsqueeze(2).to_broadcast([P, W, E]),
                                      ALU.mult)
                    rt.link(dve.tensor_tensor(sct[:], lgv[:, :, E], r12[:, 0, :], ALU.mult))
                    dve.tensor_scalar(score_all[:, b, :], sct[:], bias_s[:, 0:1], None, ALU.add)
                    for w in range(W):
                        i = dve.max(mx8[:, w, :], lgs[:, w, :])
                    rt.link(i)

                def route_b(b):
                    settle(dve)
                    for w in range(W):
                        i = dve.max_index(ix8[:, w, :], mx8[:, w, :], lgs[:, w, :])
                    rt.link(i)
                    dve.tensor_tensor(dlog_all[:, b, :], mx8[:, :, 1], mx8[:, :, 0], ALU.subtract)
                    rt.link(dve.tensor_copy(ixf[:], ix8[:, :, 0:2].rearrange("p w k -> p k w")))
                    for k in range(2):
                        i = dve.tensor_tensor(oh[:, k, :, :], iota_e[:].unsqueeze(1).to_broadcast([P, W, E]),
                                              ixf[:, k, :].unsqueeze(2).to_broadcast([P, W, E]), ALU.is_equal)
                    rt.link(i)
                    dve.tensor_tensor(msk[:], oh[:, 0, :, :], oh[:, 1, :, :], ALU.add).then_inc(mask_ready, 1)

                def route_c(b):
                    dve.wait_ge(pref_done, b * 1 + 1)
                    dve.tensor_tensor(pos[:], pref, carry[:].unsqueeze(1).to_broadcast([P, W, E]), ALU.add)
                    rt.link(dve.tensor_reduce(tsum[:], tot.rearrange("p w e -> p e w"), AX.X, ALU.add))
                    dve.tensor_tensor(carry[:], carry[:], tsum[:], ALU.add).then_inc(pref_read, 1)
                    dve.wait_ge(pref_read, b * 1 + 1)
                    for k in range(2):
                        i = dve.tensor_tensor(ohp[:, k, :, :], oh[:, k, :, :], pos[:], ALU.mult)
                    rt.link(i)
                    rt.link(dve.tensor_reduce(posk[:], ohp[:], AX.X, ALU.add))

                def route_d(b):
                    rt.round(b, 8)
                    dve.tensor_scalar(valid[:], posk[:], float(CAP), None, ALU.is_lt)
                    rt.link(dve.scalar_tensor_tensor(dest[:], ixf[:], float(CAP), posk[:], ALU.mult, ALU.add))
                    dve.tensor_copy(valid_all[:, b, :, :], valid[:])
                    rt.link(dve.tensor_tensor(dest[:], dest[:], trash[:], ALU.subtract))
                    rt.link(dve.tensor_tensor(dest[:], dest[:], valid[:], ALU.mult))
                    if isinstance(b, int) and b == B - 1:
                        to = dest_all[:, b, :, :]
                    else:
                        to = dest_st[:]
                        dve.wait_ge(xsc_ready, b * 1 + 1)
                    dve.tensor_tensor(to, dest[:], trash[:], ALU.add).then_inc(dest_ready, 1)
                    rt.done()

                def silu_up(b, j):
                    n = b * SB + j
                    dve.wait_ge(silu_done, n + 1)
                    wait(dve, dn_done, n - 1)
                    dve.tensor_tensor(acts[:, j % 2, :], sil[:, j % 2, :], up[j % 2][:], ALU.mult)\
                        .then_inc(act_ready, 1)

                def low_parts(f):
                    dve.wait_ge(ws_high, 2)
                    cols = slice(f * FS // 2, (f + 1) * FS // 2)
                    dve.tensor_tensor(wsg2[:, 1, cols], wsg[:, cols], wsg2[:, 0, cols], ALU.subtract)
                    dve.tensor_tensor(wsu2[:, 1, cols], wsu[:, cols], wsu2[:, 0, cols], ALU.subtract).then_inc(ws_low, 1)

                def body(b, first=False, last=False):
                    dve.wait_ge(xnT_ready, b * 1 + 1)
                    dve.wait_ge(xnT_high, b * 1 + 1)
                    dve.tensor_tensor(xnT2[:, 1, :], xnT[:], xnT2[:, 0, :], ALU.subtract).then_inc(xnT_low, 1)
                    if last:
                        plan = {-1: [route_a], 0: [save_scaled, route_b], 2: [route_c, route_d]}
                    else:
                        plan = {0: [save_scaled, route_a], 1: [route_b], 2: [ln_a], 3: [ln_b], 4: [ln_c], 5: [ln_d],
                                6: [route_c]}
                    if not first:
                        route_d(b - 1)
                    for j in range(-1, SB):
                        if j >= 0:
                            silu_up(b, j)
                        if first and j == 0:
                            low_parts(1)
                        for part in plan.get(j, []):
                            part(b + 1 if part in (ln_a, ln_b, ln_c, ln_d) else b)

                dve.memset(carry[:], 0.0)
                for part in (ln_a, ln_b, ln_d, ln_c):
                    part(0)
                dve.wait_ge(small_loaded, 4 * DMA)
                dve.tensor_tensor(rs9[:, E:E + 1], rs9[:, E:E + 1], normw[:], ALU.mult).then_inc(rs9_ready, 1)
                dve.wait_ge(consts, 2)
                low_parts(0)
                body(0, first=True)
                with dve.Fori(1, B - 1) as b:
                    body(b)
                body(B - 1, last=True)
                for i in range(2):
                    dve.wait_ge(we_high, i + 1)
                    dve.tensor_tensor(wge2[i][:, 1, :], wge[i][:], wge2[i][:, 0, :], ALU.subtract)
                    dve.tensor_tensor(wue2[i][:, 1, :], wue[i][:], wue2[i][:, 0, :], ALU.subtract).then_inc(we_low, 1)

            @block.scalar
            def _(act):
                def save_shared(b):
                    act.wait_ge(dn_done, b * SB + SB)
                    act.activation(ffn_all[:, b, :, :].rearrange("p w d -> p (w d)"), down[:], ACT.Copy)\
                        .then_inc(ffn_saved, 1)

                def body(b, first=False):
                    act.wait_ge(tx_done, b * 1 + 1)
                    wait(act, gu_done, b * SB)
                    act.activation(xnT[:], tx[0][:], ACT.Copy).then_inc(xnT_ready, 1)
                    act.activation(xnT2[:, 0, :], tx[0][:], ACT.Copy).then_inc(xnT_high, 1)
                    if not first:
                        save_shared(b - 1)
                    for j in range(SB):
                        n = b * SB + j
                        act.wait_ge(gu_done, n + 1)
                        wait(act, act_ready, n - 1)
                        act.activation(sil[:, j % 2, :], gate[j % 2][:], ACT.Silu).then_inc(silu_done, 1)

                act.wait_ge(consts, 1)
                for k in range(2):
                    act.dma_start(eo_dram[SLOTS + k * W * P:SLOTS + (k + 1) * W * P, :]
                                   .rearrange("(t p) d -> p t d", p=P),
                                   zeros[:].unsqueeze(1).to_broadcast([P, W, D])).then_inc(eo_stored[k], DMA)
                act.wait_ge(wffn_loaded, 2 * DMA)
                for w2, w_sb in ((wsg2, wsg), (wsu2, wsu)):
                    act.activation(w2[:, 0, :], w_sb[:], ACT.Copy).then_inc(ws_high, 1)
                body(0, first=True)
                with act.Fori(1, B) as b:
                    body(b)
                act.wait_ge(we_loaded, 4 * DMA)
                for i in range(2):
                    act.activation(wge2[i][:, 0, :], wge[i][:], ACT.Copy)
                    act.activation(wue2[i][:, 0, :], wue[i][:], ACT.Copy).then_inc(we_high, 1)
                save_shared(B - 1)

            @block.tensor
            def _(pe):
                def up_gate(b, j):
                    n = b * SB + j
                    wait(pe, silu_done, n - 1)
                    x2 = [xnT2[:, k, :] for k in range(2)]
                    product(pe, gate[j % 2][:], [wsg2[:, k, j * P:(j + 1) * P] for k in range(2)], x2)
                    wait(pe, act_ready, n - 1)
                    product(pe, up[j % 2][:], [wsu2[:, k, j * P:(j + 1) * P] for k in range(2)], x2).then_inc(gu_done, 1)

                def down_part(b, j):
                    pe.wait_ge(act_ready, b * SB + j + 1)
                    if j == 0:
                        pe.wait_ge(wsd_loaded, DMA)
                        wait(pe, ffn_saved, b * 1)
                    for w in range(W):
                        i = pe.matmul(down[:, w * D:(w + 1) * D], acts[:, j % 2, w * P:(w + 1) * P], wsd[:, j, :],
                                      start=(j == 0 and w == 0), stop=(j == SB - 1), skip_group_check=True)
                    i.then_inc(dn_done, 1)

                def turn_rows(b):
                    pe.wait_ge(xn_ready, b * 1 + 1)
                    wait(pe, xnT_high, b * 1)
                    for w in range(W):
                        i = pe.transpose(tx[0][:, w * P:(w + 1) * P], xn_st[:, w, :], ident[:])
                    i.then_inc(tx_done, 1)

                def turn_scaled_rows(b):
                    pe.wait_ge(h_ready, b * 1 + 1)
                    wait(pe, hT_saved, b * 1)
                    for w in range(W):
                        i = pe.transpose(tx[1][:, w * P:(w + 1) * P], h_st[:, w, :], ident[:])
                    i.then_inc(th_done, 1)

                def body(b, first=False, last=False):
                    if not first:
                        down_part(b - 1, SB - 1)
                    pe.wait_ge(xnT_ready, b * 1 + 1)
                    wait(pe, pref_read, b * 1)
                    if first:
                        pe.wait_ge(rs9_ready, 1)
                    for w in range(W):
                        i = pe.matmul(lgv[:, w, 0:E + 1], xnT[:, w * P:(w + 1) * P], rs9[:], start=True, stop=True)
                    i.then_inc(lg_done, 1)
                    pe.wait_ge(xnT_low, b * 1 + 1)
                    for j in range(SB):
                        if first and j % (SB // 2) == 0:
                            pe.wait_ge(ws_low, 2 * j // SB + 1)
                        up_gate(b, j)
                        if j == (1 if first else 0):
                            turn_scaled_rows(b)
                        if j == SB - 1 and not last:
                            turn_rows(b + 1)
                        if j >= 1:
                            down_part(b, j - 1)
                        if j == (1 if last else 3):
                            pe.wait_ge(mask_ready, b * 1 + 1)
                            pe.matmul(pref, before[:], msk[:], start=True, stop=False, skip_group_check=True)
                            for d in range(1, W):
                                pe.matmul(pref[:, d:W, :], ones_bf[:], msk[:, 0:W - d, :], start=False,
                                          stop=(d == W - 1), skip_group_check=True)
                            pe.matmul(tot, ones_bf[:], msk[:], start=True, stop=True).then_inc(pref_done, 1)

                pe.wait_ge(consts, 2)
                turn_rows(0)
                body(0, first=True)
                with pe.Fori(1, B - 1) as b:
                    body(b)
                body(B - 1, last=True)
                down_part(B - 1, SB - 1)

        def stage2(s2):
            def sb(name, shape, dt=F32):
                return s2.enter_context(nc.sbuf_tensor(name, shape, dt))

            def sem(name):
                return s2.enter_context(nc.semaphore(name))

            xgT2 = [sb(f"xgT2{i}", [D, 2, CAP], F32R) for i in range(2)]
            acte = [sb(f"acte{i}", [P, RB, CAP]) for i in range(2)]
            sile = sb("sile", [P, 2, HALF])
            eo = [late[:, i, :].rearrange("p (s d) -> p s d", d=D) for i in range(2)]
            sc8 = sb("sc8", [B, S])
            wk8 = [sb(f"wk8{i}", [B, S]) for i in range(2)]
            top = sb("top", [B, 8])
            sel8 = sb("sel8", [B, 2, S])
            selc = sb("selc", [P, 2, W, B])
            selr = sb("selr", [P, B, W])
            eqg = gm_all
            seln = sb("seln", [P, B, W, NG])
            hgr = sb("hgr", [P, 2, D])
            gate, up, tb, dn = bank[0:2], bank[2:4], bank[4:6], bank[6:8]
            STEPS = 2 * RB
            assert E - 4 == NG // 8

            wgu_loaded = [sem(f"wgu_loaded{i}") for i in range(2)]
            xgT_high = sem("xgT_high")
            xt_done, xgT_ready, egu_done, esilu_done = sem("xt_done"), sem("xgT_ready"), sem("egu_done"), sem("esilu_done")
            eact_ready, edn_done, eo_saved = sem("eact_ready"), sem("edn_done"), sem("eo_saved")
            sc_done, sc_read, sel_ready, selc_done = sem("sc_done"), sem("sc_read"), sem("sel_ready"), sem("selc_done")
            top_ready, rest_ready, selc_ready, eqg_ready = (sem(n) for n in
                ("top_ready", "rest_ready", "selc_ready", "eqg_ready"))
            seln_ready, hgr_done, hgr_ready, hgT_done = (sem(n) for n in ("seln_ready", "hgr_done", "hgr_ready", "hgT_done"))
            hgT_ready, kg_done, kg_saved, gm_ready = (sem(n) for n in ("hgT_ready", "kg_done", "kg_saved", "gm_ready"))

            block = s2.enter_context(nc.Block())

            @block.sync
            def _(sp):
                def store(e, i):
                    sp.wait_ge(eo_saved, e + 1)
                    sp.dma_start(eo_dram[bass.ds(e * CAP, CAP), :].rearrange("(s p) d -> p s d", p=P), eo[i])\
                        .then_inc(eo_stored[i], DMA)

                with sp.Fori(1, E // 2) as r:
                    for i in range(2):
                        e = r * 2 + i
                        sp.wait_ge(xt_done, e - 1)
                        load_rows(sp, e, i)
                        sp.wait_ge(we_low, e)
                        sp.dma_start(wge[i][:], rg[bass.ds(e, 1)].rearrange("a d f -> d (a f)")).then_inc(wgu_loaded[i], DMA)
                        sp.dma_start(wue[i][:], ru[bass.ds(e, 1)].rearrange("a d f -> d (a f)")).then_inc(wgu_loaded[i], DMA)
                        sp.wait_ge(edn_done, e - 1)
                        sp.dma_start(wde[i][:], rd[bass.ds(e, 1)].rearrange("a (j p) d -> p (a j) d", p=P))\
                            .then_inc(wd_loaded[i], DMA)
                        store(e - 2, i)
                store(E - 2, 0)
                store(E - 1, 1)

            @block.gpsimd
            def _(pool):
                def split_attention(k):
                    w_sb, w2 = ((wq, wq2), (wk, wk2), (wv, wv2))[k]
                    pool.tensor_copy(w2[:, 0, :], w_sb[:]).then_inc(wsplit, 1)
                    pool.wait_ge(wsplit, 2 * k + 1)
                    pool.tensor_tensor(w2[:, 1, :], w_sb[:], w2[:, 0, :], ALU.subtract).then_inc(wsplit, 1)

                def split_expert(r, i):
                    e = r * 2 + i
                    pool.wait_ge(wgu_loaded[i], r * 2 * DMA)
                    pool.wait_ge(egu_done, (e - 1) * STEPS)
                    settle(pool)
                    pool.tensor_copy(wge2[i][:, 0, :], wge[i][:])
                    pool.tensor_copy(wue2[i][:, 0, :], wue[i][:]).then_inc(we_high, 1)
                    pool.wait_ge(we_high, e + 1)
                    pool.tensor_tensor(wge2[i][:, 1, :], wge[i][:], wge2[i][:, 0, :], ALU.subtract)
                    pool.tensor_tensor(wue2[i][:, 1, :], wue[i][:], wue2[i][:, 0, :], ALU.subtract).then_inc(we_low, 1)

                pool.wait_ge(wattn_loaded, 3 * DMA)
                split_attention(0)
                split_attention(1)
                with pool.Fori(0, E // 2 - 1) as r:
                    for i in range(2):
                        split_expert(r + 1, i)
                split_attention(2)
                pool.tensor_copy(hTs[:, 0, :], hT_all[:, 0, :]).then_inc(hts_high, 1)
                pool.wait_ge(hts_high, 1)
                pool.tensor_tensor(hTs[:, 1, :], hT_all[:, 0, :], hTs[:, 0, :], ALU.subtract).then_inc(hts_low, 1)

            @block.scalar
            def _(act):
                def save(e, i, r):
                    act.wait_ge(edn_done, e + 1)
                    act.wait_ge(eo_stored[i], r * DMA + DMA)
                    act.activation(eo[i][:, 0:4, :].rearrange("p s d -> p (s d)"), dn[0][:], ACT.Copy)
                    act.activation(eo[i][:, 4, :], dn[1][:, 0:D], ACT.Copy).then_inc(eo_saved, 1)

                def turned_high(e, i):
                    act.wait_ge(xt_done, e + 1)
                    act.activation(xgT2[i][:, 0, 0:512], tb[0][:], ACT.Copy).then_inc(xgT_high, 1)
                    act.activation(xgT2[i][:, 0, 512:CAP], tb[1][:, 0:CAP - 512], ACT.Copy).then_inc(xgT_high, 1)

                def save_keys(m):
                    act.wait_ge(kg_done, m + 1)
                    act.activation(kg_all[:, 2 * m:2 * m + 2, :, :].rearrange("p m b s -> p (m b s)"), tb[m % 2][:],
                                   ACT.Copy).then_inc(kg_saved, 1)

                def body(r, first=False, last=False):
                    for i in range(2):
                        e = r * 2 + i
                        for s in range(STEPS):
                            n = e * STEPS + s
                            act.wait_ge(egu_done, n + 1)
                            wait(act, eact_ready, n - 1)
                            act.activation(sile[:, s % 2, :], gate[s % 2][:, 0:HALF], ACT.Silu).then_inc(esilu_done, 1)
                            if s == 1 and not (last and i == 1):
                                turned_high(e + 1, 1 - i)
                            if s == 3 and not (first and i == 0):
                                save(e - 1, 1 - i, r - 1 + i)
                            if last and i == 1 and s == 7:
                                save_keys(0)
                                save_keys(1)

                turned_high(0, 0)
                body(0, first=True)
                with act.Fori(1, E // 2 - 1) as r:
                    body(r)
                body(E // 2 - 1, last=True)
                save_keys(2)
                save_keys(3)
                save(E - 1, 1, E // 2 - 1)

            @block.vector
            def _(dve):
                def turned_low(e, i, k):
                    dve.wait_ge(xgT_high, e * 2 + k + 1)
                    c0, c1 = 512 * k, min(512 * k + 512, CAP)
                    dve.tensor_tensor(xgT2[i][:, 1, c0:c1], tb[k][:, 0:c1 - c0], xgT2[i][:, 0, c0:c1],
                                      ALU.subtract).then_inc(xgT_ready, 1)

                BH = B // 2
                cum = selc[:, 1, :, :].rearrange("p w b -> p b w").unsqueeze(3).to_broadcast([P, B, W, NG])
                place = iota_g[:].unsqueeze(1).unsqueeze(1).to_broadcast([P, BH, W, NG])

                def half(a, f):
                    return a[:, f * BH:(f + 1) * BH]

                def take_scores():
                    dve.wait_ge(sc_done, 1)
                    dve.tensor_copy(wk8[0][:], tb[0][0:B, :]).then_inc(rest_ready, 1)

                def keep_scores():
                    dve.tensor_copy(sc8[:], tb[0][0:B, :]).then_inc(sc_read, 1)

                def greatest(r, i):
                    n = r * 2 + i - 2
                    dve.wait_ge(rest_ready, n + 1)
                    settle(dve)
                    dve.max(top[:], wk8[i][:]).then_inc(top_ready, 1)

                def strike(r, i):
                    n = r * 2 + i - 2
                    dve.wait_ge(top_ready, n + 1)
                    settle(dve)
                    dve.match_replace(wk8[1 - i][:], top[:], wk8[i][:], -BIG).then_inc(rest_ready, 1)

                def chosen():
                    dve.wait_ge(sc_read, 1)
                    dve.wait_ge(rest_ready, NG // 8 + 1)
                    dve.tensor_tensor(sel8[:, 0, :], sc8[:], wk8[0][:], ALU.not_equal).then_inc(sel_ready, 1)

                def counted():
                    dve.wait_ge(sel_ready, 1)
                    dve.tensor_tensor_scan(sel8[:, 1, :], onesr[:], sel8[:, 0, :], 0.0, ALU.mult, ALU.add)\
                        .then_inc(sel_ready, 1)

                def as_columns():
                    dve.wait_ge(selc_done, 1)
                    dve.tensor_copy(selc[:].rearrange("p a w b -> p (a w b)"), tb[0][:, 0:2 * W * B])\
                        .then_inc(selc_ready, 1)
                    dve.wait_ge(selc_ready, 1)
                    dve.tensor_tensor(selr[:], selc[:, 0, :, :].rearrange("p w b -> p b w"), r1_all[:], ALU.mult)

                def one_hot(f):
                    dve.tensor_tensor(half(eqg, f), place, half(cum, f), ALU.is_equal).then_inc(eqg_ready, 1)

                def one_hot_scaled(f):
                    dve.wait_ge(eqg_ready, 2)
                    dve.tensor_tensor(half(seln, f), half(eqg, f),
                                      half(selr, f).unsqueeze(3).to_broadcast([P, BH, W, NG]), ALU.mult)\
                        .then_inc(seln_ready, 1)

                def take_rows():
                    dve.wait_ge(hgr_done, 1)
                    dve.tensor_copy(hgr[:].rearrange("p f d -> p (f d)"), tb[1][:, 0:2 * D]).then_inc(hgr_ready, 1)

                def take_columns():
                    dve.wait_ge(hgT_done, 1)
                    dve.tensor_scalar(hgT[:], tb[0][:, 0:2 * P], normw[:, 0:1], None, ALU.mult).then_inc(hgT_ready, 1)

                def global_mask(f):
                    dve.tensor_tensor(half(gm_all, f), place, half(cum, f), ALU.is_gt).then_inc(gm_ready, 1)
                    dve.wait_ge(gm_ready, f * 2 + 1)
                    dve.tensor_scalar(half(gm_all, f), half(gm_all, f), NEG, None, ALU.mult).then_inc(gm_ready, 1)

                beside = {(0, 0, 5): [take_scores], (0, 0, 6): [keep_scores],
                          (E // 2 - 1, 0, 1): [chosen], (E // 2 - 1, 0, 3): [counted],
                          (E // 2 - 1, 0, 5): [as_columns, lambda: one_hot(0)],
                          (E // 2 - 1, 0, 6): [lambda: one_hot(1)],
                          (E // 2 - 1, 0, 7): [lambda: one_hot_scaled(0)], (E // 2 - 1, 1, 0): [lambda: one_hot_scaled(1)],
                          (E // 2 - 1, 1, 3): [take_rows], (E // 2 - 1, 1, 5): [take_columns]}

                def body(r, last=False):
                    for i in range(2):
                        e = r * 2 + i
                        for s in range(STEPS):
                            n = e * STEPS + s
                            j, h = s // 2, s % 2
                            dve.wait_ge(esilu_done, n + 1)
                            if s == 0:
                                wait(dve, edn_done, e - 1)
                            dve.tensor_tensor(acte[i][:, j, h * HALF:(h + 1) * HALF], sile[:, h, :], up[h][:, 0:HALF],
                                              ALU.mult).then_inc(eact_ready, 1)
                            if s in (2, 3) and not (last and i == 1):
                                turned_low(e + 1, 1 - i, s - 2)
                            if isinstance(r, int):
                                for work in beside.get((r, i, s), []):
                                    work()
                            elif s == 4:
                                greatest(r, i)
                            elif s == 6:
                                strike(r, i)

                for k in range(2):
                    turned_low(0, 0, k)
                body(0)
                with dve.Fori(1, E // 2 - 1) as r:
                    body(r)
                body(E // 2 - 1, last=True)
                for f in range(2):
                    global_mask(f)
                dve.wait_ge(gm_ready, 2)
                dve.tensor_copy(maskb[:, :, P:KEYS], gm_all[:, 0, :, :])

            @block.tensor
            def _(pe):
                def turn_scores():
                    pe.wait_ge(xgT_ready, 4)
                    for w in range(W):
                        t = pe.transpose(tb[0][0:B, w * P:(w + 1) * P], score_all[:, :, w], ident[:])
                    t.then_inc(sc_done, 1)

                def turn_chosen():
                    pe.wait_ge(xgT_ready, 2 * E)
                    pe.wait_ge(sel_ready, 2)
                    for a in range(2):
                        for w in range(W):
                            o = (a * W + w) * B
                            t = pe.transpose(tb[0][:, o:o + B], sel8[:, a, w * P:(w + 1) * P], ident[0:B, 0:B])
                    t.then_inc(selc_done, 1)

                def pick_rows():
                    pe.wait_ge(seln_ready, 2)
                    for f in range(2):
                        for w in range(W):
                            for c in range(4):
                                t = pe.matmul(tb[1][32 * c:32 * c + 32, f * D:(f + 1) * D],
                                              seln[:, 4 * f + c, w, :], xn_all[:, 4 * f + c, w, :],
                                              start=(w == 0), stop=(w == W - 1), skip_group_check=True)
                    t.then_inc(hgr_done, 1)

                def turn_rows():
                    pe.wait_ge(hgr_ready, 1)
                    for f in range(2):
                        t = pe.transpose(tb[0][:, f * P:(f + 1) * P], hgr[:, f, :], ident[:])
                    t.then_inc(hgT_done, 1)

                def global_keys(m):
                    if m == 0:
                        pe.wait_ge(hgT_ready, 1)
                        pe.wait_ge(wattn_loaded, 3 * DMA)
                    wait(pe, kg_saved, m - 1)
                    for k in range(2):
                        blk = 2 * m + k
                        t = pe.matmul(tb[m % 2][:, k * B * NG:(k + 1) * B * NG], wk[:, blk * P:(blk + 1) * P], hgT[:],
                                      start=True, stop=True)
                    t.then_inc(kg_done, 1)

                beside = {(0, 0, 4): turn_scores, (E // 2 - 1, 0, 5): turn_chosen,
                          (E // 2 - 1, 1, 2): pick_rows, (E // 2 - 1, 1, 4): turn_rows,
                          (E // 2 - 1, 1, 6): lambda: global_keys(0), (E // 2 - 1, 1, 7): lambda: global_keys(1)}

                def turn(e, i, r):
                    if isinstance(e, int) and e == 2:
                        pe.wait_ge(sc_read, 1)
                    pe.wait_ge(xgr_loaded[i], r * DMA + DMA)
                    wait(pe, xgT_ready, e * 2)
                    for s in range(CT):
                        t = pe.transpose(tb[s // 4][:, (s % 4) * P:(s % 4 + 1) * P], xgr[i][:, s, :], ident[:])
                    t.then_inc(xt_done, 1)

                def up_gate(e, i, s):
                    n = e * STEPS + s
                    j, h = s // 2, s % 2
                    wait(pe, esilu_done, n - 1)
                    x2 = [xgT2[i][:, k, h * HALF:(h + 1) * HALF] for k in range(2)]
                    product(pe, gate[h][:, 0:HALF], [wge2[i][:, k, j * P:(j + 1) * P] for k in range(2)], x2)
                    wait(pe, eact_ready, n - 1)
                    product(pe, up[h][:, 0:HALF], [wue2[i][:, k, j * P:(j + 1) * P] for k in range(2)], x2)\
                        .then_inc(egu_done, 1)

                def down(e, i, r):
                    pe.wait_ge(wd_loaded[i], r * DMA + DMA)
                    pe.wait_ge(eact_ready, e * STEPS + STEPS)
                    wait(pe, eo_saved, e)
                    for s in range(CT):
                        for j in range(RB):
                            d = pe.matmul(dn[s // 4][:, (s % 4) * D:(s % 4 + 1) * D], acte[i][:, j, s * P:(s + 1) * P],
                                          wde[i][:, j, :], start=(j == 0), stop=(j == RB - 1))
                    d.then_inc(edn_done, 1)

                def body(r, first=False, last=False):
                    for i in range(2):
                        e = r * 2 + i
                        pe.wait_ge(xgT_ready, e * 2 + 1)
                        pe.wait_ge(we_low, e + 1)
                        for s in range(STEPS):
                            if s == 1:
                                pe.wait_ge(xgT_ready, e * 2 + 2)
                            up_gate(e, i, s)
                            if s == 1:
                                if not (first and i == 0):
                                    down(e - 1, 1 - i, r - 1 + i)
                                if not (last and i == 1):
                                    turn(e + 1, 1 - i, r + i)
                            if isinstance(r, int) and (r, i, s) in beside:
                                beside[r, i, s]()

                turn(0, 0, 0)
                body(0, first=True)
                with pe.Fori(1, E // 2 - 1) as r:
                    body(r)
                body(E // 2 - 1, last=True)
                global_keys(2)
                global_keys(3)
                down(E - 1, 1, E // 2 - 1)

        def stage3(s3):
            def sb(name, shape, dt=F32):
                return s3.enter_context(nc.sbuf_tensor(name, shape, dt))

            def sem(name):
                return s3.enter_context(nc.semaphore(name))

            vg_all = sb("vg_all", [P, B, G * HD])
            wts = sb("wts", [P, B, 2, W])
            e2 = sb("e2", [P, B, W])
            den = sb("den", [P, B, W])
            qT = [sb(f"qT{i}", [P, 2, S]) for i in range(2)]
            kT = [sb(f"kT{i}", [P, 2, W, KEYS]) for i in range(2)]
            vv = [sb(f"vv{i}", [P, W, HG * HD]) for i in range(2)]
            vgd = sb("vgd", [P, 2, HG, 32])
            vgbd = [sb(f"vgbd{i}", [P, 2, 2 * HG * 32], F32R) for i in range(2)]
            sm = [sb(f"sm{i}", [P, HG, KEYS]) for i in range(2)]
            nmx = [sb(f"nmx{i}", [P, HG]) for i in range(2)]
            ssum = [sb(f"ssum{i}", [P, HG]) for i in range(2)]
            rec = [sb(f"rec{i}", [P, HG]) for i in range(2)]
            ex = [sb(f"ex{i}", [P, HG, KEYS]) for i in range(2)]
            prob = sb("prob", [P, W, HG, P])
            probg = sb("probg", [P, W, HG, NG])
            pT = sb("pT", [P, W, HG, P])
            pTg = sb("pTg", [P, 2, S], F32R)
            oT = sb("oT", [P, G, 2, S])
            gd = sb("gd", [P, 2, W], U32)
            g_st = sb("g_st", [P, 2, W, D])
            ef = sb("ef", [P, W, D])
            ff, ss = (late[:, i, 0:W * D].rearrange("p (w d) -> p w d", w=W) for i in range(2))
            x_fin = sb("x_fin", [P, W, D])
            o_fin = sb("o_fin", [P, W, D])

            sx, sy, pa, tb, ob = bank[0], bank[1], bank[2:4], bank[4:6], bank[6:8]
            USES = 6
            TURNS = W + 1

            a_done, a_evac, kg_ready, vgbd_ready = (sem(n) for n in
                ("a_done", "a_evac", "kg_ready", "vgbd_ready"))
            sx_done, sy_done, sx_read, sy_read = (sem(n) for n in ("sx_done", "sy_done", "sx_read", "sy_read"))
            exp_done, rec_ready, prob_ready = (sem(n) for n in ("exp_done", "rec_ready", "prob_ready"))
            turn_done, turn_evac, pv_done, o_evac = (sem(n) for n in ("turn_done", "turn_evac", "pv_done", "o_evac"))
            out_done, out_read, mask_set = sem("out_done"), sem("out_read"), sem("mask_set")
            gd_ready, gathered, gw_ready = sem("gd_ready"), sem("gathered"), sem("gw_ready")
            vg_done, vg_saved, e2_ready, wc = sem("vg_done"), sem("vg_saved"), sem("e2_ready"), sem("wc")
            g_added, sf_ready, inv_ready, silu_ready = sem("g_added"), sem("sf_ready"), sem("inv_ready"), sem("silu_ready")
            prod_ready, pTg_low, vg_own, vg_high = sem("prod_ready"), sem("pTg_low"), sem("vg_own"), sem("vg_high")
            ff_ready, ef_ready, fin_ready, out_stored = sem("ff_ready"), sem("ef_ready"), sem("fin_ready"), sem("out_stored")
            xf_loaded = sem("xf_loaded")

            block = s3.enter_context(nc.Block())

            @block.sync
            def _(sp):
                def finish(b):
                    sp.wait_ge(fin_ready, b * 1 + 1)
                    sp.dma_start(out_rows[b], o_fin[:]).then_inc(out_stored, DMA)

                sp.dma_start(x_fin[:], x_rows[0]).then_inc(xf_loaded, DMA)
                with sp.Fori(0, B - 1) as b:
                    finish(b)
                    sp.wait_ge(out_stored, b * DMA + DMA)
                    sp.dma_start(x_fin[:], x_rows[b + 1]).then_inc(xf_loaded, DMA)
                for h in range(2):
                    sp.wait_ge(fin_ready, B + h)
                    sp.dma_start(out_rows[B - 1][:, 2 * h:2 * h + 2, :], o_fin[:, 2 * h:2 * h + 2, :]).then_inc(out_stored, DMA)
                sp.wait_ge(out_stored, (B + 1) * DMA)

            @block.tensor
            def _(pe):
                def project(b, g, some):
                    i = b * G + g
                    if g == 0 and some[0] == 0:
                        pe.wait_ge(hts_low, b * 1 + 1)
                    for m in some:
                        wait(pe, a_evac, i * USES + m - 1)
                        o = pa[m % 2]
                        if m < 4:
                            w2, blk = (wq2, wk2)[m // 2], 2 * g + m % 2
                            t = product(pe, o[:], [w2[:, k, blk * P:(blk + 1) * P] for k in range(2)],
                                        [hTs[:, k, :] for k in range(2)])
                        else:
                            for w in range(2):
                                u = 2 * (m - 4) + w
                                t = product(pe, o[:, w * HG * HD:(w + 1) * HG * HD],
                                            [hTs[:, k, u * P:(u + 1) * P] for k in range(2)],
                                            [wv2[:, k, g * HG * HD:(g + 1) * HG * HD] for k in range(2)])
                        t.then_inc(a_done, 1)

                def scores(b, g, w):
                    i, par = b * G + g, g % 2
                    if w == 0:
                        pe.wait_ge(a_evac, i * USES + 4)
                        pe.wait_ge(kg_ready, i + 1)
                    n = i * W + w
                    for blk in range(2):
                        for o, r0, s_done, s_read in ((sx, 0, sx_done, sx_read), (sy, 64, sy_done, sy_read)):
                            if blk == 0:
                                wait(pe, s_read, n)
                            t = pe.matmul(o[:, blk * KEYS:(blk + 1) * KEYS],
                                          qT[par][r0:r0 + 64, blk, w * P:(w + 1) * P],
                                          kT[par][r0:r0 + 64, blk, w, :], start=True, stop=True)
                            if blk == 1:
                                t.then_inc(s_done, 1)

                def values_local(b, g, f):
                    i, par = b * G + g, g % 2
                    if f == 0:
                        pe.wait_ge(turn_evac, i * TURNS + W)
                        pe.wait_ge(a_evac, i * USES + USES)
                        if g == 0:
                            wait(pe, out_read, b * 1)
                    wait(pe, o_evac, i * 2 + f - 1)
                    for w in range(W):
                        for c in range(HG):
                            v0 = HOME[c] * HD + f * 32
                            pe.matmul(ob[f][32 * c:32 * c + 32, w * P:(w + 1) * P], vv[par][:, w, v0:v0 + 32],
                                      pT[:, w, c, :], start=(w == 0), stop=False, skip_group_check=True)

                def values_global(b, g):
                    i, par = b * G + g, g % 2
                    pe.wait_ge(pTg_low, i + 1)
                    pe.wait_ge(vgbd_ready, i + 1)
                    for f in range(2):
                        cols = slice(f * P, (f + 1) * P)
                        product(pe, ob[f][:], [vgbd[par][:, k, cols] for k in range(2)], [pTg[:, k, :] for k in range(2)],
                                more=True).then_inc(pv_done, 1)

                def turn(b, g, some):
                    i = b * G + g
                    if isinstance(b, int) and b == 0 and g == 0:
                        pe.wait_ge(vg_saved, 4)
                    for u in some:
                        wait(pe, turn_evac, i * TURNS + u - 1)
                        if u == 1:
                            wait(pe, pTg_low, i)
                        o = tb[(g + u) % 2]
                        for c in range(4):
                            if u < W:
                                if c == 0:
                                    pe.wait_ge(prob_ready, i * W + u + 1)
                                src = prob[:, u, c, :]
                            else:
                                src = probg[:, c, :, :].rearrange("p c s -> p (c s)")
                            t = pe.transpose(o[:, c * P:(c + 1) * P], src, ident[:])
                        t.then_inc(turn_done, 1)

                def output(b, some):
                    pe.wait_ge(o_evac, b * (2 * G) + 2 * G)
                    for w in some:
                        for g in range(G):
                            for f in range(2):
                                t = pe.matmul(ob[0][:, w * D:(w + 1) * D], oT[:, g, f, w * P:(w + 1) * P],
                                              wo[:, g, f, :], start=(g + f == 0), stop=(g == G - 1 and f == 1))
                    if W - 1 in some:
                        t.then_inc(out_done, 1)

                def last_output(gs):
                    if gs[0] == 0:
                        pe.wait_ge(a_evac, B * G * USES)
                    for h in range(2):
                        for w in range(2 * h, 2 * h + 2):
                            for g in gs:
                                for f in range(2):
                                    pe.wait_ge(o_evac, ((B - 1) * G + g) * 2 + f + 1)
                                    t = pe.matmul(pa[h][:, (w % 2) * D:(w % 2 + 1) * D],
                                                  oT[:, g, f, w * P:(w + 1) * P], wo[:, g, f, :],
                                                  start=(w % 2 + g + f == 0), stop=(g == G - 1 and f == 1),
                                                  skip_group_check=True)
                        if gs[-1] == G - 1:
                            t.then_inc(out_done, 1)

                def step(b, g, first=False, last=False):
                    before_it = None if first and g == 0 else (b if g else b - 1, (g - 1) % G)
                    after_it = None if last and g == G - 1 else (b if g < G - 1 else b + 1, (g + 1) % G)
                    scores(b, g, 0)
                    if before_it:
                        values_local(*before_it, 0)
                    else:
                        project(*after_it, (0,))
                    scores(b, g, 1)
                    if before_it:
                        values_local(*before_it, 1)
                    else:
                        project(*after_it, (1,))
                    scores(b, g, 2)
                    if before_it:
                        values_global(*before_it)
                    else:
                        project(*after_it, (2,))
                    scores(b, g, 3)
                    if before_it and after_it:
                        project(*after_it, (0, 1))
                        turn(b, g, (0,))
                        project(*after_it, (2, 3))
                    else:
                        if after_it:
                            project(*after_it, (3,))
                        turn(b, g, (0,))
                    if last and g == G - 1:
                        last_output(range(G - 1))
                    if g == 0 and not first:
                        output(b - 1, (0, 1))
                    turn(b, g, (1,))
                    if after_it:
                        project(*after_it, (4,))
                    if g == 0 and not first:
                        output(b - 1, (2, 3))
                    turn(b, g, (2,))
                    if after_it:
                        project(*after_it, (5,))
                    turn(b, g, (3, 4))

                def all_global_values():
                    for k, o in enumerate((tb[0], tb[1], ob[0], ob[1])):
                        for f in range(2):
                            for c in range(HG):
                                cols = wv[:].rearrange("p (g j d) -> p j g d", g=G, j=HG)[:, HOME[c]]
                                t = pe.matmul(o[32 * c:32 * c + 32, f * G * HD:(f + 1) * G * HD],
                                              hgT[:, (2 * k + f) * NG:(2 * k + f + 1) * NG], cols, start=True, stop=True)
                        t.then_inc(vg_done, 1)

                project(0, 0, range(USES))
                all_global_values()
                for g in range(G):
                    step(0, g, first=True)
                pe.wait_ge(wout_loaded, 2 * HG * DMA)
                with pe.Fori(1, B - 1) as b:
                    for g in range(G):
                        step(b, g)
                for g in range(G):
                    step(B - 1, g, last=True)
                for f in range(2):
                    values_local(B - 1, G - 1, f)
                values_global(B - 1, G - 1)
                last_output((G - 1,))

            @block.vector
            def _(dve):
                def low_part(b):
                    dve.wait_ge(hts_high, b * 1 + 1)
                    dve.tensor_tensor(hTs[:, 1, :], hT_all[:, b, :], hTs[:, 0, :], ALU.subtract).then_inc(hts_low, 1)

                def mask_scores(b, g, w):
                    n = (b * G + g) * W + w
                    wait(dve, exp_done, n - 1)
                    for o, c0, s_done, s_read in ((sx, 0, sx_done, sx_read), (sy, 2, sy_done, sy_read)):
                        dve.wait_ge(s_done, n + 1)
                        settle(dve)
                        for c in range(2):
                            t = dve.tensor_tensor_reduce(out=sm[w % 2][:, c0 + c, :], in0=o[:, c * KEYS:(c + 1) * KEYS],
                                                         in1=maskb[:, w, :], scale=-1.0, scalar=BIG, op0=ALU.add,
                                                         op1=ALU.min, accum_out=nmx[w % 2][:, c0 + c:c0 + c + 1])
                        t.then_inc(s_read, 1)

                def invert(b, g, w):
                    n = (b * G + g) * W + w
                    dve.wait_ge(exp_done, n + 1)
                    wait(dve, prob_ready, n - 1)
                    dve.reciprocal(rec[w % 2][:], ssum[w % 2][:]).then_inc(rec_ready, 1)

                def take(b, g, some):
                    i, par = b * G + g, g % 2
                    for m in some:
                        dve.wait_ge(a_done, i * USES + m + 1)
                        o = pa[m % 2]
                        if m < 2:
                            t = dve.tensor_scalar(qT[par][:, m, :], o[:], float(HD) ** -0.5, None, ALU.mult)
                        elif m < 4:
                            t = dve.tensor_copy(kT[par][:, m - 2, :, 0:P], o[:].rearrange("p (w k) -> p w k", w=W))
                        else:
                            v = 2 * (m - 4)
                            t = dve.tensor_copy(vv[par][:, v:v + 2, :].rearrange("p w e -> p (w e)"), o[:])
                        t.then_inc(a_evac, 1)

                def global_low(b, g):
                    i = b * G + g
                    dve.wait_ge(turn_evac, i * TURNS + TURNS)
                    dve.tensor_tensor(pTg[:, 1, :], tb[g % 2][:], pTg[:, 0, :], ALU.subtract).then_inc(pTg_low, 1)

                def finish(b, part):
                    if part == "ff":
                        dve.wait_ge(gw_ready, b * 1 + 1)
                        dve.tensor_tensor(ff, g_st[:, 0, :, :], g_st[:, 1, :, :], ALU.add).then_inc(g_added, 1)
                    if part == "ff+":
                        dve.wait_ge(g_added, b * 1 + 1)
                        dve.tensor_tensor(ff, ff, ffn_all[:, b, :, :], ALU.add).then_inc(ff_ready, 1)
                    if part == "s":
                        dve.wait_ge(out_done, b * 1 + 1)
                        dve.tensor_tensor(ss, ob[0][:].rearrange("p (w d) -> p w d", w=W), xn_all[:, b, :, :],
                                          ALU.add).then_inc(out_read, 1)
                    if part == "1+e":
                        dve.wait_ge(ef_ready, b * 1 + 1)
                        dve.tensor_scalar(ef[:], ef[:], 1.0, None, ALU.add).then_inc(sf_ready, 1)
                    if part in range(W):
                        if part == 0:
                            dve.wait_ge(sf_ready, b * 1 + 1)
                        dve.reciprocal(ef[:, part, :], ef[:, part, :]).then_inc(inv_ready, 1)
                    if part == "silu":
                        dve.wait_ge(inv_ready, b * W + W)
                        dve.tensor_tensor(ff, ff, ef[:], ALU.mult).then_inc(silu_ready, 1)
                    if part == "s*silu":
                        dve.wait_ge(out_read, b * 1 + 1)
                        dve.wait_ge(silu_ready, b * 1 + 1)
                        dve.tensor_tensor(ss, ss, ff, ALU.mult).then_inc(prod_ready, 1)
                    if part == "x+":
                        dve.wait_ge(prod_ready, b * 1 + 1)
                        dve.wait_ge(xf_loaded, b * DMA + DMA)
                        dve.tensor_tensor(o_fin[:], ss, x_fin[:], ALU.add).then_inc(fin_ready, 1)

                def finish_half(b, h):
                    n = b + h
                    dve.wait_ge(out_done, n + 1)
                    v = slice(2 * h, 2 * h + 2)
                    dve.tensor_tensor(ss[:, v, :], pa[h][:, 0:2 * D].rearrange("p (w d) -> p w d", w=2),
                                      xn_all[:, b, v, :], ALU.add).then_inc(out_read, 1)
                    dve.wait_ge(out_read, n + 1)
                    dve.wait_ge(silu_ready, B)
                    dve.tensor_tensor(ss[:, v, :], ss[:, v, :], ff[:, v, :], ALU.mult).then_inc(prod_ready, 1)
                    dve.wait_ge(prod_ready, n + 1)
                    dve.wait_ge(xf_loaded, B * DMA)
                    dve.tensor_tensor(o_fin[:, v, :], ss[:, v, :], x_fin[:, v, :], ALU.add).then_inc(fin_ready, 1)

                def step(b, g, first=False, last=False):
                    after_it = None if last and g == G - 1 else (b if g < G - 1 else b + 1, (g + 1) % G)
                    parts = ((), (), ()) if first else ((("ff",), ("ff+",), ("s",)), (("1+e",), (0,), (1,)),
                                                        ((2,), (3,), ("silu",)), (("s*silu",), ("x+",), ()))[g]
                    if g == 0:
                        wait(dve, mask_set, b * 1)
                    fresh = first and g == 0
                    mask_scores(b, g, 0)
                    if not fresh:
                        global_low(b if g else b - 1, (g - 1) % G)
                    for part in parts[0]:
                        finish(b - 1, part)
                    mask_scores(b, g, 1)
                    if g == G - 1 and not last:
                        low_part(b + 1)
                    for part in parts[1]:
                        finish(b - 1, part)
                    invert(b, g, 0)
                    if fresh:
                        take(*after_it, (0,))
                    mask_scores(b, g, 2)
                    invert(b, g, 1)
                    if fresh:
                        take(*after_it, (1,))
                    mask_scores(b, g, 3)
                    if after_it and not fresh:
                        take(*after_it, (0,))
                    if g == G - 1 and not last:
                        dve.wait_ge(sy_read, (b * G + g) * W + W)
                        dve.tensor_copy(maskb[:, :, P:KEYS], gm_all[:, b + 1, :, :]).then_inc(mask_set, 1)
                    invert(b, g, 2)
                    if after_it:
                        take(*after_it, (2,) if fresh else (1, 2))
                    invert(b, g, 3)
                    if after_it:
                        take(*after_it, (3, 4))
                    for part in parts[2]:
                        finish(b - 1, part)
                    if after_it:
                        take(*after_it, (5,))

                def weights():
                    ch = Chain(dve, wc, 4)
                    ch.round(0)
                    dve.wait_ge(e2_ready, 1)
                    ch.link(dve.tensor_scalar(den[:], e2[:], 1.0, None, ALU.add))
                    ch.link(dve.reciprocal(den[:], den[:]))
                    ch.link(dve.tensor_tensor(e2[:], e2[:], den[:], ALU.mult))
                    dve.tensor_tensor(wts[:, :, 0, :], den[:], valid_all[:, :, 0, :], ALU.mult)
                    ch.link(dve.tensor_tensor(wts[:, :, 1, :], e2[:], valid_all[:, :, 1, :], ALU.mult))
                    ch.done()

                take(0, 0, range(USES))
                weights()
                for g in range(G):
                    step(0, g, first=True)
                with dve.Fori(1, B - 1) as b:
                    for g in range(G):
                        step(b, g)
                for g in range(G):
                    step(B - 1, g, last=True)
                for part in ("ff", "ff+", "1+e", 0):
                    finish(B - 1, part)
                global_low(B - 1, G - 1)
                for part in (1, 2, 3, "silu"):
                    finish(B - 1, part)
                for h in range(2):
                    finish_half(B - 1, h)

            @block.scalar
            def _(act):
                def exps(b, g, w):
                    i = b * G + g
                    n = i * W + w
                    act.wait_ge(sy_read, n + 1)
                    wait(act, rec_ready, n - 1)
                    wait(act, prob_ready, n - 1)
                    for c in range(HG):
                        t = act.activation(ex[w % 2][:, c, :], sm[w % 2][:, c, :], ACT.Exp, bias=nmx[w % 2][:, c:c + 1],
                                           scale=-1.0, accum_out=ssum[w % 2][:, c:c + 1])
                    t.then_inc(exp_done, 1)

                def high_part(b):
                    wait(act, a_done, b * (G * USES))
                    act.activation(hTs[:, 0, :], hT_all[:, b, :], ACT.Copy).then_inc(hts_high, 1)

                def save_values(b, g, f):
                    act.wait_ge(pv_done, (b * G + g) * 2 + f + 1)
                    act.activation(oT[:, g, f, :], ob[f][:], ACT.Copy).then_inc(o_evac, 1)

                def save_turned(b, g, some):
                    for u in some:
                        act.wait_ge(turn_done, (b * G + g) * TURNS + u + 1)
                        o = tb[(g + u) % 2]
                        dst = pT[:, u, :, :].rearrange("p c q -> p (c q)") if u < W else pTg[:, 0, :]
                        act.activation(dst, o[:], ACT.Copy).then_inc(turn_evac, 1)

                def sigmoid_part(b):
                    act.wait_ge(ff_ready, b * 1 + 1)
                    act.activation(ef[:], ff, ACT.Exp, scale=-1.0).then_inc(ef_ready, 1)

                def step(b, g, first=False, last=False):
                    if g == G - 1 and not last:
                        high_part(b + 1)
                    exps(b, g, 0)
                    exps(b, g, 1)
                    exps(b, g, 2)
                    if not (first and g == 0):
                        save_values(b if g else b - 1, (g - 1) % G, 0)
                    exps(b, g, 3)
                    if not (first and g == 0):
                        save_values(b if g else b - 1, (g - 1) % G, 1)
                    save_turned(b, g, (0, 1, 2))
                    if last and g == G - 1:
                        sigmoid_part(b)
                    save_turned(b, g, (3, 4))
                    if g == 0 and not first:
                        sigmoid_part(b - 1)

                act.activation(e2[:], dlog_all[:], ACT.Exp).then_inc(e2_ready, 1)
                for k, o in enumerate((tb[0], tb[1], ob[0], ob[1])):
                    act.wait_ge(vg_done, k + 1)
                    act.activation(vg_all[:, 2 * k:2 * k + 2, :].rearrange("p b e -> p (b e)"), o[:], ACT.Copy)\
                        .then_inc(vg_saved, 1)
                for g in range(G):
                    step(0, g, first=True)
                with act.Fori(1, B - 1) as b:
                    for g in range(G):
                        step(b, g)
                for g in range(G):
                    step(B - 1, g, last=True)
                for f in range(2):
                    save_values(B - 1, G - 1, f)

            @block.gpsimd
            def _(pool):
                def global_keys(b, g):
                    i, par = b * G + g, g % 2
                    wait(pool, sy_done, (i - 1) * W)
                    pool.tensor_copy(kT[par][:, :, :, P:KEYS],
                                     kg_all[:, 2 * g:2 * g + 2, b, :].unsqueeze(2).to_broadcast([P, 2, W, NG]))\
                        .then_inc(kg_ready, 1)

                def global_values(b, g):
                    i, par = b * G + g, g % 2
                    wait(pool, pv_done, (i - 1) * 2)
                    v = vg_all[:, b, g * HD:(g + 1) * HD].rearrange("p (f d) -> p f d", f=2)
                    wait(pool, vgbd_ready, i)
                    pool.tensor_tensor(vgd[:], v.unsqueeze(2).to_broadcast([P, 2, HG, 32]),
                                       own[:].unsqueeze(1).to_broadcast([P, 2, HG, 32]), ALU.mult).then_inc(vg_own, 1)
                    pool.wait_ge(vg_own, i + 1)
                    flat = vgd[:].rearrange("p f c d -> p (f c d)")
                    settle(pool)
                    pool.tensor_copy(vgbd[par][:, 0, :], flat).then_inc(vg_high, 1)
                    pool.wait_ge(vg_high, i + 1)
                    pool.tensor_tensor(vgbd[par][:, 1, :], flat, vgbd[par][:, 0, :], ALU.subtract).then_inc(vgbd_ready, 1)

                def divide(b, g, w):
                    n = (b * G + g) * W + w
                    pool.wait_ge(rec_ready, n + 1)
                    if w == 0:
                        wait(pool, turn_done, (b * G + g) * TURNS)
                    for dst, k0, k1 in ((prob, 0, P), (probg, P, KEYS)):
                        t = pool.tensor_tensor(dst[:, w, :, :], ex[w % 2][:, :, k0:k1],
                                               rec[w % 2][:].unsqueeze(2).to_broadcast([P, HG, k1 - k0]), ALU.mult)
                    t.then_inc(prob_ready, 1)

                picks = [(k, w) for w in range(W) for k in range(2)]

                def gather(b, some):
                    for k, w in some:
                        pool.indirect_dma_start(out=g_st[:, k, w, :], out_offset=None, in_=eo_dram,
                                                in_offset=bass.IndirectOffsetOnAxis(ap=gd[:, k, w:w + 1], axis=0))\
                            .then_inc(gathered, DMA)

                def step(b, g, last=False):
                    if not (last and g == G - 1):
                        ahead = (b if g < G - 1 else b + 1, (g + 1) % G)
                        global_keys(*ahead)
                    for w in range(W):
                        divide(b, g, w)
                    if not (last and g == G - 1):
                        global_values(*ahead)
                    if g == 0:
                        wait(pool, g_added, b * 1)
                        pool.tensor_copy(gd[:], dest_all[:, b, :, :]).then_inc(gd_ready, 1)
                        pool.wait_ge(gd_ready, b * 1 + 1)
                        if isinstance(b, int) and b == 0:
                            for i in range(2):
                                pool.wait_ge(eo_stored[i], (E // 2 + 1) * DMA)
                        settle(pool)
                    gather(b, picks[3 * g:3 * g + 3])
                    if g == G - 1:
                        pool.wait_ge(gathered, (b + 1) * (2 * W * DMA))
                        pool.wait_ge(wc, 4)
                        pool.tensor_tensor(g_st[:].rearrange("p k w d -> p (k w) d"),
                                           g_st[:].rearrange("p k w d -> p (k w) d"),
                                           wts[:, b, :, :].rearrange("p k w -> p (k w)").unsqueeze(2)
                                           .to_broadcast([P, 2 * W, D]), ALU.mult).then_inc(gw_ready, 1)

                global_keys(0, 0)
                pool.wait_ge(vg_saved, 4)
                global_values(0, 0)
                for g in range(G):
                    step(0, g)
                with pool.Fori(1, B - 1) as b:
                    for g in range(G):
                        step(b, g)
                for g in range(G):
                    step(B - 1, g, last=True)
        with early:
            for stage in (stage1, stage2):
                with ExitStack() as s:
                    stage(s)
        with ExitStack() as s:
            stage3(s)


def kernel(**inputs):
    import numpy as _np
    import concourse.bacc as _bacc
    from concourse import mybir as _mybir
    from concourse.bass_utils import run_bass_kernel_spmd as _run

    nc = _bacc.Bacc("TRN2", target_bir_lowering=False, num_devices=1)
    arrays, args = {}, []
    for name in ["L0_attn_x", "L0_attn_norm_w", "L0_attn_w_q", "L0_attn_w_k", "L0_attn_w_v", "L0_attn_w_out",
                 "L0_attn_scorer_w", "L0_attn_scorer_b", "L0_ffn_router_w", "L0_ffn_rg", "L0_ffn_ru", "L0_ffn_rd",
                 "L0_ffn_sg", "L0_ffn_su", "L0_ffn_sd"]:
        a = _np.asarray(inputs[name])
        a = _np.ascontiguousarray(a.T if name == "L0_ffn_router_w" else a)
        arrays["in_" + name] = a
        args.append(nc.dram_tensor("in_" + name, a.shape, _mybir.dt.from_np(a.dtype), kind="ExternalInput").ap())
    shape = inputs["L0_attn_x"].shape
    out = nc.dram_tensor("out_0", shape, _mybir.dt.float32, kind="ExternalOutput").ap()
    recurrent_layer(nc, *args, out)
    r = _run(nc, [arrays], core_ids=[0])
    return r.results[0]["out_0"]
```
